# Optimizing a Trainium2 kernel written in Bass

```python
import numpy as np
import jax
import jax.numpy as jnp

def _softmax(x, axis=-1):
    return jax.nn.softmax(x, axis=axis)

def _gelu(x):
    return jax.nn.gelu(x, approximate=True)

def _silu(x):
    return jax.nn.silu(x)

def _sigmoid(x):
    return jax.nn.sigmoid(x)

def _layernorm(x, axis=-1, eps=1e-05):
    m = jnp.mean(x, axis=axis, keepdims=True)
    v = jnp.var(x, axis=axis, keepdims=True)
    return (x - m) / jnp.sqrt(v + eps)

def _scatter_add(tgt, idx, src, axis=0):
    return tgt.at[idx].add(src)

def _segment_sum(src, seg, n):
    return jax.ops.segment_sum(src, seg, n)
kernel_name = 'mk_decoder_preln_d1_seqx_r4_ca1fda'

def setup_inputs(seed: int=0):
    np.random.seed(seed)
    _w = jnp.asarray

    def _rec_inputs():
        import jax
        import jax.numpy as jnp
        _rk = jax.random.key(seed)
        x = -0.0003929 + 0.9999 * jax.random.normal(jax.random.fold_in(_rk, 1), (1, 2048, 256), jnp.float32)
        _lenS = 2048 - jax.random.randint(jax.random.fold_in(_rk, 7), (1,), 0, max(1, 2048 // 4) + 1, jnp.int32)
        _lenS2 = 1601 - jax.random.randint(jax.random.fold_in(_rk, 8), (1,), 0, max(1, 1601 // 4) + 1, jnp.int32)
        _ctx_1024P = jax.random.normal(jax.random.fold_in(_rk, 11), (1, 16, 256), jnp.float32)
        _ctx_1024c = jax.random.dirichlet(jax.random.fold_in(_rk, 511), 0.3 * jnp.ones((16,), jnp.float32), (1, 1601))
        _ctx_1024t = jnp.einsum('bsk,bkd->bsd', _ctx_1024c, _ctx_1024P)
        _ctx_1024t = _ctx_1024t * jax.lax.rsqrt(jnp.mean(jnp.square(_ctx_1024t)) + 1e-12) * 0.953939
        ctx_1024 = -1.39393e-06 + 0.999914 * (_ctx_1024t + 0.3 * jax.random.normal(jax.random.fold_in(_rk, 611), (1, 1601, 256), jnp.float32))
        return (x, ctx_1024)
    x, ctx_1024 = _rec_inputs()

    def _L0_attn_setup():
        import jax, jax.numpy as jnp
        import numpy as np
        N_EMBD = 256
        N_HEAD = 16
        HEAD_DIM = N_EMBD // N_HEAD
        key = jax.random.key(seed)
        kx, kqkv, kw, kb = jax.random.split(key, 4)
        B, T = (4, 512)
        x = jax.random.normal(kx, (B, T, N_EMBD), dtype=jnp.float32)
        w_qkv = jax.random.normal(kqkv, (3 * N_EMBD, N_EMBD), dtype=jnp.float32) * N_EMBD ** (-0.5)
        w_out = jax.random.normal(kw, (N_EMBD, N_EMBD), dtype=jnp.float32) * N_EMBD ** (-0.5)
        b_out = jax.random.normal(kb, (N_EMBD,), dtype=jnp.float32) * 0.01
        return {'x': x, 'w_qkv': w_qkv, 'w_out': w_out, 'b_out': b_out}
    _L0_attn_all = _L0_attn_setup()
    _L0_attn_in = {k: v for k, v in _L0_attn_all.items() if k in ('w_qkv', 'w_out', 'b_out')}
    del _L0_attn_all

    def _L0_xattn_setup():
        import jax, jax.numpy as jnp
        import numpy as np
        B, C_LEN, Q_LEN, D = (8, 512, 128, 256)
        key = jax.random.key(seed)
        ks = jax.random.split(key, 10)
        scale = 1.0 / np.sqrt(D)
        return {'c': jax.random.normal(ks[0], (B, C_LEN, D), dtype=jnp.float32), 'q': jax.random.normal(ks[1], (B, Q_LEN, D), dtype=jnp.float32), 'w_cq': jax.random.normal(ks[2], (D,), dtype=jnp.float32) * scale, 'b_cq': jax.random.normal(ks[3], (), dtype=jnp.float32) * scale, 'w_c': jax.random.normal(ks[4], (D,), dtype=jnp.float32) * scale, 'b_c': jax.random.normal(ks[5], (), dtype=jnp.float32) * scale, 'w_q': jax.random.normal(ks[6], (D,), dtype=jnp.float32) * scale, 'b_q': jax.random.normal(ks[7], (), dtype=jnp.float32) * scale, 'W_l': jax.random.normal(ks[8], (D, 4 * D), dtype=jnp.float32) * (1.0 / np.sqrt(4 * D)), 'b_l': jax.random.normal(ks[9], (D,), dtype=jnp.float32) * (1.0 / np.sqrt(4 * D))}
    _L0_xattn_all = _L0_xattn_setup()
    _L0_xattn_in = {k: v for k, v in _L0_xattn_all.items() if k in ('w_cq', 'b_cq', 'w_c', 'b_c', 'w_q', 'b_q', 'W_l', 'b_l')}
    del _L0_xattn_all

    def _L0_ffn_setup():
        import jax, jax.numpy as jnp
        import numpy as np
        BS, L, D = (4, 512, 256)
        H, E, K = (8, 16, 2)
        HD = D // H
        I = 1024 // H
        key = jax.random.key(seed)
        ks = jax.random.split(key, 10)
        s = lambda k, shp, fan: jax.random.normal(k, shp, jnp.float32) / np.sqrt(fan)
        return {'x': jax.random.normal(ks[0], (BS, L, D), jnp.float32), 'Wm': s(ks[1], (D, D), D), 'bm': jnp.zeros((D,), jnp.float32), 'expert_emb': jax.random.normal(ks[2], (HD, E), jnp.float32), 'W1': s(ks[3], (E, HD, I), HD), 'b1': jnp.zeros((E, I), jnp.float32), 'W2': s(ks[4], (E, I, HD), I), 'b2': jnp.zeros((E, HD), jnp.float32), 'Wo': s(ks[5], (D, D), D), 'bo': jnp.zeros((D,), jnp.float32)}
    _L0_ffn_all = _L0_ffn_setup()
    _L0_ffn_in = {k: v for k, v in _L0_ffn_all.items() if k in ('Wm', 'bm', 'expert_emb', 'W1', 'b1', 'W2', 'b2', 'Wo', 'bo')}
    del _L0_ffn_all
    return {'x': x, 'ctx_1024': ctx_1024, 'L0_attn_w_qkv': _L0_attn_in['w_qkv'], 'L0_attn_w_out': _L0_attn_in['w_out'], 'L0_attn_b_out': _L0_attn_in['b_out'], 'L0_xattn_w_cq': _L0_xattn_in['w_cq'], 'L0_xattn_b_cq': _L0_xattn_in['b_cq'], 'L0_xattn_w_c': _L0_xattn_in['w_c'], 'L0_xattn_b_c': _L0_xattn_in['b_c'], 'L0_xattn_w_q': _L0_xattn_in['w_q'], 'L0_xattn_b_q': _L0_xattn_in['b_q'], 'L0_xattn_W_l': _L0_xattn_in['W_l'], 'L0_xattn_b_l': _L0_xattn_in['b_l'], 'L0_ffn_Wm': _L0_ffn_in['Wm'], 'L0_ffn_bm': _L0_ffn_in['bm'], 'L0_ffn_expert_emb': _L0_ffn_in['expert_emb'], 'L0_ffn_W1': _L0_ffn_in['W1'], 'L0_ffn_b1': _L0_ffn_in['b1'], 'L0_ffn_W2': _L0_ffn_in['W2'], 'L0_ffn_b2': _L0_ffn_in['b2'], 'L0_ffn_Wo': _L0_ffn_in['Wo'], 'L0_ffn_bo': _L0_ffn_in['bo']}

def reference(x, ctx_1024, L0_attn_w_qkv, L0_attn_w_out, L0_attn_b_out, L0_xattn_w_cq, L0_xattn_b_cq, L0_xattn_w_c, L0_xattn_b_c, L0_xattn_w_q, L0_xattn_b_q, L0_xattn_W_l, L0_xattn_b_l, L0_ffn_Wm, L0_ffn_bm, L0_ffn_expert_emb, L0_ffn_W1, L0_ffn_b1, L0_ffn_W2, L0_ffn_b2, L0_ffn_Wo, L0_ffn_bo):
    import jax
    import jax.numpy as jnp

    def _L0_attn_ref(x, w_qkv, w_out, b_out):
        import jax, jax.numpy as jnp
        import numpy as np
        N_EMBD = 256
        N_HEAD = 16
        HEAD_DIM = N_EMBD // N_HEAD
        B, T, C = x.shape
        H, D = (N_HEAD, HEAD_DIM)
        qkv = jnp.einsum('btc,fc->btf', x, w_qkv)
        q, k, v = jnp.split(qkv, 3, axis=-1)
        q = q.reshape(B, T, H, D).transpose(0, 2, 1, 3)
        k = k.reshape(B, T, H, D).transpose(0, 2, 1, 3)
        v = v.reshape(B, T, H, D).transpose(0, 2, 1, 3)
        att = jnp.einsum('bhqd,bhkd->bhqk', q, k) * D ** (-0.5)
        causal = jnp.tril(jnp.ones((T, T), dtype=bool))
        att = jnp.where(causal[None, None], att, jnp.float32(-jnp.inf))
        att = jax.nn.softmax(att, axis=-1)
        out = jnp.einsum('bhqk,bhkd->bhqd', att, v)
        out = out.transpose(0, 2, 1, 3).reshape(B, T, C)
        return jnp.einsum('btc,oc->bto', out, w_out) + b_out

    def _L0_xattn_ref(c, q, w_cq, b_cq, w_c, b_c, w_q, b_q, W_l, b_l):
        import jax, jax.numpy as jnp
        import numpy as np
        B, C_LEN, Q_LEN, D = (8, 512, 128, 256)
        cq = jnp.einsum('bcd,bqd,d->bcq', c, q, w_cq) + b_cq
        s = (c @ w_c + b_c)[:, :, None] + (q @ w_q + b_q)[:, None, :] + cq
        a = jax.nn.softmax(s, axis=2)
        c2q_att = jnp.einsum('bcq,bqd->bcd', a, q)
        b_att = jax.nn.softmax(jnp.max(s, axis=2), axis=1)
        q2c_att = jnp.einsum('bc,bcd->bd', b_att, c)[:, None, :]
        x = jnp.concatenate([c, c2q_att, c * c2q_att, c * q2c_att], axis=-1)
        z = x @ W_l.T + b_l
        return z

    def _L0_ffn_ref(x, Wm, bm, expert_emb, W1, b1, W2, b2, Wo, bo):
        import jax, jax.numpy as jnp
        import numpy as np
        BS, L, D = (4, 512, 256)
        H, E, K = (8, 16, 2)
        HD = D // H
        I = 1024 // H
        bs, L_, d = x.shape
        h = x @ Wm + bm
        t = h.reshape(bs * L_ * H, HD)
        logits = t @ expert_emb
        w = jax.nn.softmax(logits, axis=-1)
        topw, topi = jax.lax.top_k(w, K)
        hmid = jax.nn.gelu(jnp.einsum('td,edi->tei', t, W1) + b1, approximate=False)
        eo = jnp.einsum('tei,eio->teo', hmid, W2) + b2
        sel = jnp.take_along_axis(eo, topi[:, :, None], axis=1)
        comb = (sel * topw[:, :, None]).sum(axis=1)
        out = comb.reshape(bs, L_, d)
        return out @ Wo + bo
    x = x + _L0_attn_ref(_layernorm(x, axis=-1), L0_attn_w_qkv, L0_attn_w_out, L0_attn_b_out)
    x = x + _L0_xattn_ref(_layernorm(x, axis=-1), ctx_1024, L0_xattn_w_cq, L0_xattn_b_cq, L0_xattn_w_c, L0_xattn_b_c, L0_xattn_w_q, L0_xattn_b_q, L0_xattn_W_l, L0_xattn_b_l)
    x = x + _L0_ffn_ref(_layernorm(x, axis=-1), L0_ffn_Wm, L0_ffn_bm, L0_ffn_expert_emb, L0_ffn_W1, L0_ffn_b1, L0_ffn_W2, L0_ffn_b2, L0_ffn_Wo, L0_ffn_bo)
    return x

_drawn_inputs = setup_inputs


def setup_inputs(seed=0):
    import zlib

    import numpy as np

    out = dict(_drawn_inputs(seed))
    spreads = {'L0_ffn_bm': (0.0, 0.1),
     'L0_ffn_b1': (0.0, 0.1),
     'L0_ffn_b2': (0.0, 0.1),
     'L0_ffn_bo': (0.0, 0.1)}
    factors = {'L0_attn_b_out': 4.167}
    for name, (base, spread) in spreads.items():
        noise = np.random.default_rng([zlib.crc32(name.encode()), seed]).standard_normal(out[name].shape)
        drawn = base * np.exp(spread * noise) if base else spread * noise
        out[name] = jnp.asarray(drawn.astype(out[name].dtype))
    for name, factor in factors.items():
        out[name] = (out[name] * factor).astype(out[name].dtype)
    return out
```

```python
from contextlib import ExitStack

import concourse.bass as bass
from concourse import mybir

F32 = mybir.dt.float32
F32R = mybir.dt.float32r
BF16 = mybir.dt.bfloat16
ALU = mybir.AluOpType
ACT = mybir.ActivationFunctionType
AX = mybir.AxisListType

P = 128
T = 2048
D = 256
KD = D // P
NB = T // P
CH = 512
NC = T // CH
BPC = CH // P
LN_EPS = 1e-5

NH, HD = 16, 16
HG = 4
NG = NH // HG
VW = HD + 1
SCALE = HD ** -0.5
Q_PART = [0, 1, 2, 0, 1, 0]
K_PART = [0, 0, 0, 1, 1, 2]
KROWS = HD * len(Q_PART)
MROWS = KROWS + 3

L = 1601
LB = (L + P - 1) // P
LLAST = L - (LB - 1) * P
LPAD = L + L % 2

FH, FD = 8, 32
NE, EI = 16, 128
EG = 4
NEG = NE // EG
NEGBIG = -1e30
FREE = 1


def tokens(c):
    return slice(c * CH, (c + 1) * CH)


def at(i, n=1):
    return bass.ds(i, n)


def fresh(eng, i, top, least=0):
    if isinstance(i, int):
        return i
    reg = eng.alloc_register()
    eng.reg_mov(reg, i)
    return eng.snap(reg, min_val=least, max_val=top)


class Chain:

    def __init__(self, eng, sem, base=0):
        self.eng, self.sem, self.base, self.n = eng, sem, base, 0

    def then(self, instruction):
        instruction.then_inc(self.sem, 1)
        self.n += 1

    def wait(self):
        self.eng.wait_ge(self.sem, self.base + self.n)

    def link(self, instruction):
        self.then(instruction)
        self.wait()


class Phase:

    def __init__(self, nc, name):
        self.nc, self.name, self.stack = nc, name, ExitStack()

    def __enter__(self):
        self.stack.__enter__()
        return self

    def __exit__(self, *a):
        return self.stack.__exit__(*a)

    def sb(self, name, shape, dt=F32):
        return self.stack.enter_context(self.nc.sbuf_tensor(f"{self.name}_{name}", shape, dt))

    def ps(self, name, shape, dt=F32):
        return self.stack.enter_context(self.nc.psum_tensor(f"{self.name}_{name}", shape, dt))

    def sem(self, name):
        return self.stack.enter_context(self.nc.semaphore(f"{self.name}_{name}"))


class LayerNorm:

    def __init__(self, ph, name):
        self.stats, self.mv = ph.sb(name + "_stats", [P, NB, 6]), ph.sb(name + "_mv", [P, NB, 2])
        self.var, self.std, self.rstd = (ph.sb(f"{name}_{n}", [P, NB]) for n in ("var", "std", "rstd"))
        self.stats_done, self.mv_done, self.var_ready, self.std_ready, self.rstd_ready, self.done = (
            ph.sem(f"{name}_{n}") for n in ("stats_done", "mv_done", "var_ready", "std_ready", "rstd_ready", "done"))

    def collect(self, dve, x, c):
        blocks = range(c * BPC, (c + 1) * BPC)
        for b in blocks:
            dve.bn_stats(self.stats[:, b, :], x[:, b, :]).then_inc(self.stats_done, 1)
        for b in blocks:
            dve.wait_ge(self.stats_done, b + 1)
            dve.bn_aggr(self.mv[:, b, :], self.stats[:, b, :]).then_inc(self.mv_done, 1)
        dve.wait_ge(self.mv_done, (c + 1) * BPC)
        at_c = slice(c * BPC, (c + 1) * BPC)
        dve.tensor_scalar(self.var[:, at_c], self.mv[:, at_c, 1], LN_EPS, None, ALU.add).then_inc(self.var_ready, 1)

    def root(self, act, c):
        at_c = slice(c * BPC, (c + 1) * BPC)
        act.wait_ge(self.var_ready, c + 1)
        act.activation(self.std[:, at_c], self.var[:, at_c], ACT.Sqrt).then_inc(self.std_ready, 1)

    def apply(self, dve, x, out, c):
        at_c = slice(c * BPC, (c + 1) * BPC)
        dve.wait_ge(self.std_ready, c + 1)
        dve.reciprocal(self.rstd[:, at_c], self.std[:, at_c]).then_inc(self.rstd_ready, 1)
        dve.wait_ge(self.rstd_ready, c + 1)
        for b in range(c * BPC, (c + 1) * BPC):
            dve.tensor_scalar(out[:, b, :], x[:, b, :], self.mv[:, b, 0:1], self.rstd[:, b:b + 1],
                              ALU.subtract, ALU.mult).then_inc(self.done, 1)


class Turn:

    def __init__(self, ph, name, banks, ident):
        self.banks, self.ident = banks, ident
        self.turned, self.high_done, self.low_done = (
            ph.sem(f"{name}_{n}") for n in ("turned", "high_done", "low_done"))

    def turn(self, pe, src, c, k, ready=None):
        n = c * KD + k
        if ready is not None:
            pe.wait_ge(ready, (c + 1) * BPC)
        if n >= 2:
            pe.wait_ge(self.low_done, n - 1)
        for j in range(BPC):
            last = pe.transpose(self.banks[n % 2][:, j * P:(j + 1) * P], src[:, c * BPC + j, k * P:(k + 1) * P],
                                self.ident[:, :])
        last.then_inc(self.turned, 1)

    def high(self, act, hi, c, k, plain=None):
        n = c * KD + k
        act.wait_ge(self.turned, n + 1)
        if plain is not None:
            act.activation(plain, self.banks[n % 2], ACT.Copy)
        act.activation(hi, self.banks[n % 2], ACT.Copy).then_inc(self.high_done, 1)

    def low(self, dve, hi, lo, c, k):
        n = c * KD + k
        dve.wait_ge(self.high_done, n + 1)
        dve.tensor_tensor(lo, self.banks[n % 2], hi, ALU.subtract).then_inc(self.low_done, 1)


def phase_qkv(nc, io, keep):
    with Phase(nc, "qkv") as ph:
        x = ph.sb("x", [P, NB, D])
        w = ph.sb("w", [P, KD, 3 * D])
        wh, wl = ph.sb("wh", [P, KD, 3 * D], F32R), ph.sb("wl", [P, KD, 3 * D], F32R)
        ident = ph.sb("ident", [P, P])
        xh, xl = ph.sb("xh", [P, KD, T], F32R), ph.sb("xl", [P, KD, T], F32R)
        parts = ph.sb("parts", [P, 3, 3, CH], BF16)
        rem = ph.sb("rem", [P, 3, CH])
        banks = ph.ps("banks", [P, 8, CH])
        ln = LayerNorm(ph, "ln")
        turn = Turn(ph, "turn", (banks[:, 0, :], banks[:, 1, :]), ident)
        w_in, wh_done, w_split, qk_ready, p1_ready, r1_ready, p2_ready, p3_ready, v_ready, v_out, v_out_act = map(ph.sem, (
            "w_in", "wh_done", "w_split", "qk_ready", "p1_ready", "r1_ready", "p2_ready", "p3_ready", "v_ready", "v_out", "v_out_act"))
        x_in = [ph.sem(f"x_in{c}") for c in range(NC)]
        stored = [ph.sem(f"stored{n}") for n in range(3)]
        FT = 2 * KD
        NQ = FT * NC
        QB, VB = 2, 5
        block = ph.stack.enter_context(nc.Block())

        @block.sync
        def _(sp):
            for c in range(NC):
                sp.dma_start(x[:, c * BPC:(c + 1) * BPC, :],
                             io["x"][tokens(c), :].rearrange("(b p) d -> p b d", p=P)).then_inc(x_in[c], 16)
            for n in range(NQ):
                ft, c = n % FT, n // FT
                sp.wait_ge(p3_ready, n + 1)
                sp.dma_start(io["qk_parts"][ft // KD, :, at((ft % KD) * P, P), tokens(c)].rearrange("a p t -> p a t"),
                             parts[:, n % 3, :, :]).then_inc(stored[n % 3], 16)
            for s in range(3):
                sp.wait_ge(stored[s], 16 * len(range(s, NQ, 3)))

        @block.gpsimd
        def _(pool):
            pool.dma_start(ident[:, :], io["ident"]).then_inc(w_in, 16)
            pool.dma_start(w[:, :, :], io["wqkvT"].rearrange("(k p) f -> p k f", p=P)).then_inc(w_in, 16)
            pool.wait_ge(w_in, 32)
            pool.tensor_copy(wh[:, :, :], w[:, :, :]).then_inc(wh_done, 1)
            pool.wait_ge(wh_done, 1)
            pool.tensor_tensor(wl[:, :, :], w[:, :, :], wh[:, :, :], ALU.subtract).then_inc(w_split, 1)

        @block.vector
        def _(dve):
            def normalise(c):
                dve.wait_ge(x_in[c], 16)
                ln.collect(dve, x, c)
                ln.apply(dve, x, x, c)

            def triple(n):
                dve.wait_ge(p1_ready, n + 1)
                dve.tensor_tensor(rem[:, n % 3, :], banks[:, QB + n % 3, :], parts[:, n % 3, 0, :], ALU.subtract)\
                    .then_inc(r1_ready, 1)

            def finish(n):
                dve.wait_ge(p2_ready, n + 1)
                dve.tensor_tensor(parts[:, n % 3, 2, :], rem[:, n % 3, :], parts[:, n % 3, 1, :], ALU.subtract)\
                    .then_inc(p3_ready, 1)

            def low(c):
                for k in range(KD):
                    turn.low(dve, xh[:, k, tokens(c)], xl[:, k, tokens(c)], c, k)

            normalise(0)
            normalise(1)
            low(0)
            for c in range(NC):
                for n in range(c * FT, (c + 1) * FT):
                    triple(n)
                    if n >= 1:
                        finish(n - 1)
                if c + 2 < NC:
                    normalise(c + 2)
                if c + 1 < NC:
                    low(c + 1)
            finish(NQ - 1)
            for b in range(1, NB, 2):
                dve.wait_ge(v_ready, b + 1)
                dve.tensor_copy(keep["v"][:, b, :], banks[:, VB + b % 3, 0:D]).then_inc(v_out, 1)

        @block.scalar
        def _(act):
            def first(n):
                act.wait_ge(qk_ready, n + 1)
                if n >= 3:
                    act.wait_ge(stored[n % 3], 16 * (n // 3))
                act.activation(parts[:, n % 3, 0, :], banks[:, QB + n % 3, :], ACT.Copy).then_inc(p1_ready, 1)

            def second(n):
                act.wait_ge(r1_ready, n + 1)
                act.activation(parts[:, n % 3, 1, :], rem[:, n % 3, :], ACT.Copy).then_inc(p2_ready, 1)

            def high(c):
                for k in range(KD):
                    turn.high(act, xh[:, k, tokens(c)], c, k)

            ln.root(act, 0)
            ln.root(act, 1)
            high(0)
            for c in range(NC):
                for n in range(c * FT, (c + 1) * FT):
                    first(n)
                    if n >= 1:
                        second(n - 1)
                if c + 2 < NC:
                    ln.root(act, c + 2)
                if c + 1 < NC:
                    high(c + 1)
            second(NQ - 1)
            for b in range(0, NB, 2):
                act.wait_ge(v_ready, b + 1)
                act.activation(keep["v"][:, b, :], banks[:, VB + b % 3, 0:D], ACT.Copy).then_inc(v_out_act, 1)

        @block.tensor
        def _(pe):
            def turn_chunk(c):
                for k in range(KD):
                    turn.turn(pe, x, c, k, ready=ln.done)

            pe.wait_ge(w_in, 32)
            turn_chunk(0)
            pe.wait_ge(w_split, 1)
            for c in range(NC):
                pe.wait_ge(turn.low_done, (c + 1) * KD)
                for n in range(c * FT, (c + 1) * FT):
                    if n >= 3:
                        pe.wait_ge(r1_ready, n - 2)
                    feat = slice((n % FT) * P, (n % FT + 1) * P)
                    split_product(pe, banks[:, QB + n % 3, :],
                                  [(wh[:, k, feat], wl[:, k, feat], xh[:, k, tokens(c)], xl[:, k, tokens(c)])
                                   for k in range(KD)]).then_inc(qk_ready, 1)
                if c + 1 < NC:
                    turn_chunk(c + 1)
            for b in range(NB):
                if b >= 3:
                    pe.wait_ge(v_out if (b - 3) % 2 else v_out_act, (b - 3) // 2 + 1)
                tok, feat = slice(b * P, (b + 1) * P), slice(2 * D, 3 * D)
                split_product(pe, banks[:, VB + b % 3, 0:D],
                              [(xh[:, k, tok], xl[:, k, tok], wh[:, k, feat], wl[:, k, feat]) for k in range(KD)]).then_inc(v_ready, 1)


def causal_steps():
    return [(qc, kb, max(kb - BPC * qc, 0) * P) for qc in range(NC) for kb in range(BPC * (qc + 1))]


def max_tiles():
    return [(qb, c, min(CH, (qb + 1) * P - c * CH), h)
            for qb in range(NB) for c in range(qb // BPC + 1) for h in range(HG)]


def phase_attention(nc, io, keep):
    with Phase(nc, "att") as ph:
        qst, kst = ph.sb("qst", [P, NH * T], BF16), ph.sb("kst", [P, NH * T], BF16)
        vg = ph.sb("vg", [P, NB, HG, 32])
        prob = ph.sb("prob", [P, 3, HG, CH])
        osb = ph.sb("osb", [P, 2, CH])
        rden = ph.sb("rden", [P, BPC, HG])
        pmax = ph.sb("pmax", [P, HG * NB, NC])
        nmax = ph.sb("nmax", [P, HG * NB])
        nrem = ph.sb("nrem", [P, HG * NB])
        npart = ph.sb("npart", [P, 3, HG * NB], BF16)
        NTURN = 3 * HG * NB // 2
        NROW = [[(0, 0, 64)], [(0, 64, 96), (1, 0, 32)], [(1, 32, 96)]]
        nrow = ph.sb("nrow", [NTURN, 2, P], BF16)
        ident, identb = ph.sb("ident", [P, P]), ph.sb("identb", [P, P], BF16)
        mask_qk, mask_kq = ph.sb("mask_qk", [P, P], BF16), ph.sb("mask_kq", [P, P], BF16)
        banks = ph.ps("banks", [P, 8, CH])
        S, M, O, R = 0, 4, 6, 7
        rowbank = banks[0:NTURN, R, :].bitcast(BF16)

        const_in, stack_in, ones_ready, pmax_ready, vg_zero, m_ready, m_done, chain_s, nm_split, nmT_ready, \
            nmT_copied, nm_in, vg_ready, s_ready, exp_done, pv_done, o_copied, o_turned, o_scaled, rden_ready, constb_in = map(ph.sem, (
                "const_in", "stack_in", "ones_ready", "pmax_ready", "vg_zero", "m_ready", "m_done",
                "dve_chain", "nm_split", "nmT_ready", "nmT_copied", "nm_in", "vg_ready", "s_ready",
                "exp_done", "pv_done", "o_copied", "o_turned", "o_scaled", "rden_ready", "constb_in"))
        steps, tiles = causal_steps(), max_tiles()
        NS, NM = len(steps), len(tiles)
        last_step = [max(i for i, s in enumerate(steps) if s[0] == qc) for qc in range(NC)]
        LAG = 2
        SPREAD = NS - 3
        CHAIN = 4
        block = ph.stack.enter_context(nc.Block())

        @block.sync
        def _(sp):
            sp.dma_start(ident[:, :], io["ident"]).then_inc(const_in, 16)
            for g in range(NG):
                if g >= 1:
                    sp.wait_ge(stack_in, g * (2 * len(Q_PART) * 16))
                for side, (dst, which) in enumerate(((qst, Q_PART), (kst, K_PART))):
                    for j, part in enumerate(which):
                        src = io["qk_parts"][side, part, g * (HG * HD):(g + 1) * (HG * HD), :]
                        out = dst[j * HD:(j + 1) * HD, g * (HG * T):(g + 1) * (HG * T)]
                        sp.dma_start(out.rearrange("d (h t) -> d h t", h=HG),
                                     src.rearrange("(h d) t -> d h t", h=HG)).then_inc(stack_in, 16)
            for g in range(NG):
                sp.wait_ge(nmT_copied, g + 1)
                for part in range(3):
                    for turn, a, b in NROW[part]:
                        first = (turn * NTURN + a - part * HG * NB) * P
                        out = qst[KROWS + part:KROWS + part + 1, at(g * (HG * T) + first, (b - a) * P)]
                        sp.dma_start(out.rearrange("a (n t) -> a n t", t=P), nrow[a:b, turn, :]).then_inc(nm_in, 16)

        @block.gpsimd
        def _(pool):
            for dst, name in ((identb, "ident"), (mask_qk, "mask_qk"), (mask_kq, "mask_kq")):
                pool.dma_start(dst[:, :], io[name]).then_inc(constb_in, 16)
            pool.memset(kst[KROWS:MROWS, :], 1.0).then_inc(ones_ready, 1)

        @block.tensor
        def _(pe):
            def max_tile(r, u):
                qb, c, width, h = tiles[u]
                if u >= 2:
                    pe.wait_ge(m_done, r * NM + u - 1)
                elif not isinstance(r, int):
                    pe.wait_ge(m_done, r * NM)
                out = banks[:, M + u % 2, 0:width]
                diagonal = c == qb // BPC
                last = pe.matmul(out, qst[0:KROWS, at(r * (HG * T) + h * T + qb * P, P)],
                                 kst[0:KROWS, at(r * (HG * T) + h * T + c * CH, width)], start=True, stop=not diagonal)
                if diagonal:
                    last = pe.matmul(out[:, width - P:width], identb[:, :], mask_qk[:, :], start=False, stop=True)
                last.then_inc(m_ready, 1)

            def turn_maxima(r):
                pe.wait_ge(nm_split, r + 1)
                columns = npart[:, :, :].rearrange("p a n -> p (a n)")
                for half in range(2):
                    last = pe.transpose(rowbank[:, half * P:(half + 1) * P], columns[:, half * NTURN:(half + 1) * NTURN],
                                        identb[:, :])
                last.then_inc(nmT_ready, 1)

            def scores(g, s, pair):
                qc, kb, off = steps[s]
                if s >= 1:
                    pe.wait_ge(exp_done, g * (2 * NS) + 2 * (s - 1) + pair + 1)
                for h in (2 * pair, 2 * pair + 1):
                    out = banks[:, S + h, off:CH]
                    diagonal = kb >= BPC * qc
                    last = pe.matmul(out, kst[0:MROWS, at(g * (HG * T) + h * T + kb * P, P)],
                                     qst[0:MROWS, at(g * (HG * T) + h * T + qc * CH + off, CH - off)],
                                     start=True, stop=not diagonal)
                    if diagonal:
                        last = pe.matmul(out[:, 0:P], identb[:, :], mask_kq[:, :], start=False, stop=True)
                last.then_inc(s_ready, 1)

            def values(g, s):
                qc, kb, off = steps[s]
                if s == 0:
                    pe.wait_ge(vg_ready, g + 1)
                if kb == 0:
                    pe.wait_ge(o_copied, FREE + g * NC + qc)
                pe.wait_ge(exp_done, g * (2 * NS) + 2 * (s + 1))
                for h in range(HG):
                    last = pe.matmul(banks[32 * h:32 * h + 32, O, off:CH], vg[:, kb, h, :], prob[:, s % 3, h, off:CH],
                                     start=kb == 0, stop=kb == BPC * qc + BPC - 1)
                last.then_inc(pv_done, 1)

            def turn_output(g, qc, both):
                pe.wait_ge(o_copied, FREE + g * NC + qc + 1)
                pe.wait_ge(o_scaled, FREE + g * NC + qc)
                if both and qc == NC - 1:
                    pe.wait_ge(nmT_copied, g + 2)
                for j in range(BPC):
                    last = pe.transpose(banks[:, R, j * P:(j + 1) * P], osb[:, qc % 2, j * P:(j + 1) * P], ident[:, :])
                last.then_inc(o_turned, 1)

            def round_(g, both):
                pe.wait_ge(nm_in, (g + 1) * 64)
                if both:
                    pe.wait_ge(stack_in, (g + 2) * (2 * len(Q_PART) * 16))
                todo, loop = 0, g
                for s in range(NS + LAG):
                    g = fresh(pe, loop, NG - 2)
                    upto = min(NM, NM * (s + 1) // SPREAD) if both else 0
                    half = (todo + upto) // 2
                    if s < NS:
                        scores(g, s, 0)
                    for u in range(todo, half):
                        max_tile(g + 1, u)
                    if s < NS:
                        scores(g, s, 1)
                    for u in range(half, upto):
                        max_tile(g + 1, u)
                    todo = upto
                    if s >= LAG:
                        values(g, s - LAG)
                    if s - 4 in last_step:
                        turn_output(g, last_step.index(s - 4), both)
                    if both and s == NS - 1:
                        pe.wait_ge(o_scaled, FREE + g * NC + NC - 1)
                        turn_maxima(g + 1)
                turn_output(g, NC - 1, both)

            pe.sem_inc(pv_done, FREE)
            pe.wait_ge(const_in, 16)
            pe.wait_ge(constb_in, 48)
            pe.wait_ge(stack_in, 2 * len(Q_PART) * 16)
            for u in range(NM):
                max_tile(0, u)
            turn_maxima(0)
            pe.wait_ge(ones_ready, 1)
            with pe.Fori(0, NG - 1) as g:
                round_(g, True)
            round_(NG - 1, False)

        @block.scalar
        def _(act):
            def round_(loop):
                for s in range(NS):
                    g = fresh(act, loop, NG - 1)
                    qc, kb, off = steps[s]
                    act.wait_ge(pv_done, FREE + g * NS + max(s - 2, 0))
                    for pair in range(2):
                        act.wait_ge(s_ready, g * (2 * NS) + 2 * s + pair + 1)
                        heads = slice(2 * pair, 2 * pair + 2)
                        act.activation(prob[:, s % 3, heads, off:CH], banks[:, 2 * pair:2 * pair + 2, off:CH], ACT.Exp,
                                       scale=SCALE).then_inc(exp_done, 1)
                        if pair == 0 and s - 3 in last_step:
                            copy_output(g, last_step.index(s - 3))
                copy_output(g, NC - 1)

            def copy_output(g, qc):
                act.wait_ge(pv_done, FREE + g * NS + last_step[qc] + 1)
                if qc >= 2:
                    act.wait_ge(o_turned, g * NC + qc - 1)
                act.activation(osb[:, qc % 2, :], banks[:, O, :], ACT.Copy).then_inc(o_copied, 1)

            act.sem_inc(o_copied, FREE)
            with act.Fori(0, NG) as g:
                round_(g)

        @block.vector
        def _(dve):
            def max_tile(r, u):
                qb, c, width, h = tiles[u]
                dve.wait_ge(m_ready, r * NM + u + 1)
                n = h * NB + qb
                dve.tensor_reduce(pmax[:, n, c:c + 1], banks[:, M + u % 2, 0:width], AX.X, ALU.max).then_inc(m_done, 1)

            def split_maxima(r):
                chain = Chain(dve, chain_s, r * CHAIN)
                dve.wait_ge(m_done, (r + 1) * NM)
                chain.link(dve.tensor_reduce(nmax[:, :], pmax[:, :, :], AX.X, ALU.max, negate=True))
                chain.link(dve.tensor_copy(npart[:, 0, :], nmax[:, :]))
                chain.link(dve.tensor_tensor(nrem[:, :], nmax[:, :], npart[:, 0, :], ALU.subtract))
                chain.link(dve.tensor_copy(npart[:, 1, :], nrem[:, :]))
                assert chain.n == CHAIN
                dve.tensor_tensor(npart[:, 2, :], nrem[:, :], npart[:, 1, :], ALU.subtract).then_inc(nm_split, 1)

            def copy_maxima(r):
                dve.wait_ge(nmT_ready, r + 1)
                dve.tensor_copy(nrow[:, :, :], rowbank[:, 0:2 * P].rearrange("n (a q) -> n a q", a=2)).then_inc(nmT_copied, 1)

            def group_values(g):
                dve.wait_ge(pv_done, FREE + g * NS)
                dve.tensor_copy(vg[:, :, :, 0:HD], keep["v"][:, :, at(g * (HG * HD), HG * HD)]
                                .rearrange("p b (h d) -> p b h d", h=HG)).then_inc(vg_ready, 1)

            def scale_output(g, qc):
                dve.wait_ge(o_turned, g * NC + qc + 1)
                turned = banks[:, R, :].rearrange("p (b h d) -> p b h d", b=BPC, h=HG)
                dve.reciprocal(rden[:, :, :], turned[:, :, :, HD]).then_inc(rden_ready, 1)
                dve.wait_ge(rden_ready, g * NC + qc + 1)
                dve.tensor_tensor(keep["attn"][:, qc * BPC:(qc + 1) * BPC, at(g * (HG * HD), HG * HD)]
                                  .rearrange("p b (h d) -> p b h d", h=HG), turned[:, :, :, 0:HD],
                                  rden[:, :, :].unsqueeze(3).broadcast_to([P, BPC, HG, HD]), ALU.mult).then_inc(o_scaled, 1)

            def round_(g, both):
                group_values(g)
                todo, loop = 0, g
                for s in range(NS + LAG):
                    g = fresh(dve, loop, NG - 2)
                    upto = min(NM, NM * (s + 1) // SPREAD) if both else 0
                    for u in range(todo, upto):
                        max_tile(g + 1, u)
                    if both and upto == NM and todo < NM:
                        split_maxima(g + 1)
                    todo = upto
                    if s - 4 in last_step:
                        scale_output(g, last_step.index(s - 4))
                if both:
                    copy_maxima(g + 1)
                scale_output(g, NC - 1)

            dve.sem_inc(o_scaled, FREE)
            dve.memset(pmax[:, :, :], NEGBIG).then_inc(pmax_ready, 1)
            dve.memset(vg[:, :, :, :], 0.0).then_inc(vg_zero, 1)
            dve.wait_ge(vg_zero, 1)
            dve.memset(vg[:, :, :, HD:VW], 1.0).then_inc(vg_zero, 1)
            dve.wait_ge(vg_zero, 2)
            dve.wait_ge(pmax_ready, 1)
            for u in range(NM):
                max_tile(0, u)
            split_maxima(0)
            copy_maxima(0)
            with dve.Fori(0, NG - 1) as g:
                round_(g, True)
            round_(NG - 1, False)


def phase_projection(nc, io, keep):
    x1, cn, cT, ch, cl = (keep[n] for n in ("x1", "cn", "cT", "ch", "cl"))
    with Phase(nc, "proj") as ph:
        w, bias, ident = ph.sb("w", [P, KD, D]), ph.sb("bias", [P, D]), ph.sb("ident", [P, P])
        wh, wl = ph.sb("wh", [P, KD, D], F32R), ph.sb("wl", [P, KD, D], F32R)
        ah, al = ph.sb("ah", [P, KD, T], F32R), ph.sb("al", [P, KD, T], F32R)
        banks = ph.ps("banks", [P, 8, CH])
        ln = LayerNorm(ph, "ln")
        turn_a = Turn(ph, "a", (banks[:, 0, :], banks[:, 1, :]), ident)
        turn_c = Turn(ph, "c", (banks[:, 2, :], banks[:, 3, :]), ident)
        w_in, x_in, wh_done, w_split, xb_done, o_ready, o_added = map(ph.sem, (
            "w_in", "x_in", "wh_done", "w_split", "xb_done", "o_ready", "o_added"))
        block = ph.stack.enter_context(nc.Block())

        @block.sync
        def _(sp):
            sp.dma_start(ident[:, :], io["ident"]).then_inc(w_in, 16)
            sp.dma_start(w[:, :, :], io["woutT"].rearrange("(k p) f -> p k f", p=P)).then_inc(w_in, 16)
            sp.dma_start(bias[:, :], io["b_out"].partition_broadcast(P)).then_inc(x_in, 16)
            sp.dma_start(x1[:, :, :], io["x"].rearrange("(b p) d -> p b d", p=P)).then_inc(x_in, 16)

        @block.gpsimd
        def _(pool):
            pool.wait_ge(x_in, 32)
            for b in range(NB):
                pool.tensor_tensor(x1[:, b, :], x1[:, b, :], bias[:, :], ALU.add).then_inc(xb_done, 1)

        @block.vector
        def _(dve):
            dve.wait_ge(w_in, 32)
            dve.tensor_copy(wh[:, :, :], w[:, :, :]).then_inc(wh_done, 1)
            dve.wait_ge(wh_done, 1)
            dve.tensor_tensor(wl[:, :, :], w[:, :, :], wh[:, :, :], ALU.subtract).then_inc(w_split, 1)

            def low_a(c):
                for k in range(KD):
                    turn_a.low(dve, ah[:, k, tokens(c)], al[:, k, tokens(c)], c, k)

            def low_c(c):
                for k in range(KD):
                    turn_c.low(dve, ch[:, k, tokens(c)], cl[:, k, tokens(c)], c, k)

            low_a(0)
            low_a(1)
            for c in range(NC):
                for b in range(c * BPC, (c + 1) * BPC):
                    dve.wait_ge(o_ready, b + 1)
                    dve.wait_ge(xb_done, b + 1)
                    dve.tensor_tensor(x1[:, b, :], banks[:, 4 + b % 2, 0:D], x1[:, b, :], ALU.add).then_inc(o_added, 1)
                dve.wait_ge(o_added, (c + 1) * BPC)
                ln.collect(dve, x1, c)
                if c + 2 < NC:
                    low_a(c + 2)
                ln.apply(dve, x1, cn, c)
                if c >= 1:
                    low_c(c - 1)
            low_c(NC - 1)

        @block.scalar
        def _(act):
            def high_a(c):
                for k in range(KD):
                    turn_a.high(act, ah[:, k, tokens(c)], c, k)

            def high_c(c):
                for k in range(KD):
                    turn_c.high(act, ch[:, k, tokens(c)], c, k, plain=cT[:, k, tokens(c)])

            high_a(0)
            high_a(1)
            for c in range(NC):
                if c + 2 < NC:
                    high_a(c + 2)
                ln.root(act, c)
                if c >= 1:
                    high_c(c - 1)
            high_c(NC - 1)

        @block.tensor
        def _(pe):
            def turn_attention(c):
                for k in range(KD):
                    turn_a.turn(pe, keep["attn"], c, k)

            def turn_norm(c):
                for k in range(KD):
                    turn_c.turn(pe, cn, c, k, ready=ln.done)

            def project(c):
                pe.wait_ge(turn_a.low_done, (c + 1) * KD)
                for b in range(c * BPC, (c + 1) * BPC):
                    if b >= 2:
                        pe.wait_ge(o_added, b - 1)
                    tok = slice(b * P, (b + 1) * P)
                    split_product(pe, banks[:, 4 + b % 2, 0:D], [(ah[:, k, tok], al[:, k, tok], wh[:, k, :], wl[:, k, :])
                                                                 for k in range(KD)]).then_inc(o_ready, 1)

            pe.wait_ge(w_in, 32)
            turn_attention(0)
            turn_attention(1)
            pe.wait_ge(w_split, 1)
            for c in range(NC):
                project(c)
                if c + 2 < NC:
                    turn_attention(c + 2)
                if c >= 1:
                    turn_norm(c - 1)
            turn_norm(NC - 1)


def phase_cross(nc, io, keep):
    cT = keep["cT"]
    with Phase(nc, "cross") as ph:
        qT, q = ph.sb("qT", [P, KD, LPAD]), ph.sb("q", [P, LB, D])
        qTh, qTl = ph.sb("qTh", [P, KD, LPAD], F32R), ph.sb("qTl", [P, KD, LPAD], F32R)
        qh, ql = ph.sb("qh", [P, LB, D], F32R), ph.sb("ql", [P, LB, D], F32R)
        wcol, ident = ph.sb("wcol", [P, 2, KD]), ph.sb("ident", [P, P])
        cw, cwh, cwl = ph.sb("cw", [P, KD, P]), ph.sb("cwh", [P, KD, P], F32R), ph.sb("cwl", [P, KD, P], F32R)
        prob, total, rtotal = ph.sb("prob", [P, L]), ph.sb("total", [P, NB]), ph.sb("rtotal", [P, NB])
        pTh, pTl = ph.sb("pTh", [P, LB, P], F32R), ph.sb("pTl", [P, LB, P], F32R)
        banks = ph.ps("banks", [P, 8, CH])
        S, R, O = 0, 4, 6
        GROUPS = [list(range(t, min(t + 4, LB))) for t in range(0, LB, 4)]
        NGR = len(GROUPS)
        rows = lambda t: P if t < LB - 1 else LLAST
        in_, q_in, split_s, split_done, cw_s, cw_ready, s_ready, nm_ready, exp_done, turned, high_done, low_done, \
            o_ready, r_ready, o_done, qT_split = map(ph.sem, (
                "in", "q_in", "split_s", "split_done", "cw_s", "cw_ready", "s_ready", "nm_ready", "exp_done", "turned",
                "high_done", "low_done", "o_ready", "r_ready", "o_done", "qT_split"))
        block = ph.stack.enter_context(nc.Block())

        @block.sync
        def _(sp):
            sp.dma_start(wcol[:, 0, :], io["w_cq"]).then_inc(in_, 16)
            sp.dma_start(wcol[:, 1, :], io["w_q"]).then_inc(in_, 16)
            sp.dma_start(ident[:, :], io["ident"]).then_inc(in_, 16)
            sp.dma_start(qT[:, :, :], io["ctxT"].rearrange("(k p) l -> p k l", p=P)).then_inc(in_, 16)
            sp.dma_start(q[:, 0:LB - 1, :], io["ctx"][0:(LB - 1) * P, :].rearrange("(b p) d -> p b d", p=P)).then_inc(q_in, 16)
            sp.dma_start(q[0:LLAST, LB - 1, :], io["ctx"][(LB - 1) * P:L, :]).then_inc(q_in, 16)

        @block.gpsimd
        def _(pool):
            pool.wait_ge(q_in, 32)
            pool.tensor_copy(qh[:, 0:LB - 1, :], q[:, 0:LB - 1, :]).then_inc(split_s, 1)
            pool.tensor_copy(qh[0:LLAST, LB - 1, :], q[0:LLAST, LB - 1, :]).then_inc(split_s, 1)
            pool.wait_ge(split_s, 2)
            pool.tensor_tensor(ql[:, 0:LB - 1, :], q[:, 0:LB - 1, :], qh[:, 0:LB - 1, :], ALU.subtract).then_inc(split_done, 1)
            pool.tensor_tensor(ql[0:LLAST, LB - 1, :], q[0:LLAST, LB - 1, :], qh[0:LLAST, LB - 1, :],
                               ALU.subtract).then_inc(split_done, 1)

        @block.vector
        def _(dve):
            def weigh(i, first=False):
                for k in range(KD):
                    dve.tensor_scalar(cw[:, k, :], cT[:, k, at(i * P, P)], wcol[:, 0, k:k + 1], wcol[:, 1, k:k + 1],
                                      ALU.mult, ALU.add).then_inc(cw_s, 1)
                dve.wait_ge(cw_s, i * 3 + 2)
                dve.tensor_copy(cwh[:, :, :], cw[:, :, :]).then_inc(cw_s, 1)
                dve.wait_ge(cw_s, i * 3 + 3)
                dve.tensor_tensor(cwl[:, :, :], cw[:, :, :], cwh[:, :, :], ALU.subtract).then_inc(cw_ready, 1)

            def maximum(i):
                dve.wait_ge(s_ready, i + 1)
                dve.tensor_reduce(keep["nmax"][:, at(i)], banks[:, S:S + 4, :].rearrange("p b c -> p (b c)")[:, 0:L],
                                  AX.X, ALU.max, negate=True).then_inc(nm_ready, 1)

            def low(i):
                for g, ts in enumerate(GROUPS):
                    dve.wait_ge(high_done, i * NGR + g + 1)
                    r = rows(ts[-1])
                    dve.tensor_tensor(pTl[0:r, ts[0]:ts[-1] + 1, :], banks[0:r, R + g % 2, 0:len(ts) * P]
                                      .rearrange("p (t c) -> p t c", c=P), pTh[0:r, ts[0]:ts[-1] + 1, :],
                                      ALU.subtract).then_inc(low_done, 1)

            def normalise(i):
                dve.reciprocal(rtotal[:, at(i)], total[:, at(i)]).then_inc(r_ready, 1)
                dve.wait_ge(r_ready, i + 1)
                dve.wait_ge(o_ready, i + 1)
                dve.tensor_scalar(keep["c2q"][:, at(i), :].rearrange("p a d -> p (a d)"), banks[:, O, 0:D],
                                  rtotal[:, at(i)], None, ALU.mult).then_inc(o_done, 1)

            dve.sem_inc(o_done, FREE)
            dve.wait_ge(in_, 64)
            weigh(0)
            dve.tensor_copy(qTh[:, :, :], qT[:, :, :]).then_inc(qT_split, 1)
            dve.wait_ge(qT_split, 1)
            dve.tensor_tensor(qTl[:, :, :], qT[:, :, :], qTh[:, :, :], ALU.subtract).then_inc(qT_split, 1)
            maximum(0)
            weigh(1)
            with dve.Fori(1, NB - 1) as i:
                low(i - 1)
                maximum(i)
                weigh(i + 1)
                normalise(i - 1)
            low(NB - 2)
            maximum(NB - 1)
            normalise(NB - 2)
            low(NB - 1)
            normalise(NB - 1)

        @block.scalar
        def _(act):
            def exponent(i):
                act.wait_ge(nm_ready, i + 1)
                act.activation(prob[:, :], banks[:, S:S + 4, :].rearrange("p b c -> p (b c)")[:, 0:L], ACT.Exp,
                               bias=keep["nmax"][:, at(i)], accum_out=total[:, at(i)]).then_inc(exp_done, 1)

            def high(i):
                for g, ts in enumerate(GROUPS):
                    act.wait_ge(turned, i * NGR + g + 1)
                    r = rows(ts[-1])
                    act.activation(pTh[0:r, ts[0]:ts[-1] + 1, :], banks[0:r, R + g % 2, 0:len(ts) * P]
                                   .rearrange("p (t c) -> p t c", c=P), ACT.Copy).then_inc(high_done, 1)

            exponent(0)
            with act.Fori(1, NB) as i:
                high(i - 1)
                exponent(i)
            high(NB - 1)

        @block.tensor
        def _(pe):
            CHUNKS = [(a, min(a + CH, LPAD)) for a in range(0, LPAD, CH)]

            def score(i, chunk, first=False):
                a, b = CHUNKS[chunk]
                if chunk == 0:
                    pe.wait_ge(cw_ready, i + 1)
                    if not first:
                        pe.wait_ge(exp_done, i)
                last = split_product(pe, banks[:, S + chunk, 0:b - a],
                                     [(cwh[:, k, :], cwl[:, k, :], qTh[:, k, a:b], qTl[:, k, a:b]) for k in range(KD)])
                if chunk == len(CHUNKS) - 1:
                    last.then_inc(s_ready, 1)

            def turn(i, g, first=False):
                if g == 0:
                    pe.wait_ge(exp_done, i + 1)
                if g >= 2:
                    pe.wait_ge(low_done, i * NGR + g - 1)
                for n, t in enumerate(GROUPS[g]):
                    last = pe.transpose(banks[0:rows(t), R + g % 2, n * P:(n + 1) * P], prob[:, t * P:t * P + rows(t)],
                                        ident[:, :])
                last.then_inc(turned, 1)

            def attend(i):
                pe.wait_ge(low_done, (i + 1) * NGR)
                pe.wait_ge(o_done, FREE + i)
                split_product(pe, banks[:, O, 0:D], [(pTh[0:rows(t), t, :], pTl[0:rows(t), t, :], qh[0:rows(t), t, :],
                                                      ql[0:rows(t), t, :]) for t in range(LB)]).then_inc(o_ready, 1)

            pe.wait_ge(in_, 64)
            pe.wait_ge(qT_split, 2)
            for chunk in range(4):
                score(0, chunk, first=True)
            pe.wait_ge(split_done, 2)
            with pe.Fori(1, NB) as i:
                turn(i - 1, 0)
                turn(i - 1, 1)
                score(i, 0)
                turn(i - 1, 2)
                score(i, 1)
                turn(i - 1, 3)
                score(i, 2)
                score(i, 3)
                attend(i - 1)
            for g in range(NGR):
                turn(NB - 1, g)
            attend(NB - 1)


def phase_fuse(nc, io, keep):
    x1, cn, cT, ch, cl, c2q = (keep[n] for n in ("x1", "cn", "cT", "ch", "cl", "c2q"))
    with Phase(nc, "fuse") as ph:
        ident, ones = ph.sb("ident", [P, P]), ph.sb("ones", [P, P])
        w = ph.sb("w", [P, 4 * KD, D])
        wh, wl = ph.sb("wh", [P, 3 * KD, D], F32R), ph.sb("wl", [P, 3 * KD, D], F32R)
        bias, wc, bs = ph.sb("bias", [P, D]), ph.sb("wc", [P, D]), ph.sb("bs", [P, 3])
        junk, rowc = ph.sb("junk", [P, D]), ph.sb("rowc", [P, NB])
        smax, e = ph.sb("smax", [P, NB]), ph.sb("e", [P, NB])
        one = ph.sb("one", [P, 8])
        q2c, q2col = ph.sb("q2c", [1, D]), ph.sb("q2col", [P, KD])
        qTh, qTl = ph.sb("qTh", [P, 2, KD, CH], F32R), ph.sb("qTl", [P, 2, KD, CH], F32R)
        mul = ph.sb("mul", [P, 2, CH])
        mh, ml = ph.sb("mh", [P, 2, KD, CH], F32R), ph.sb("ml", [P, 2, KD, CH], F32R)
        banks = ph.ps("banks", [P, 8, CH])
        ln = LayerNorm(ph, "ln")
        turn_q = Turn(ph, "q", (banks[:, 0, :], banks[:, 1, :]), ident)
        turn_n = Turn(ph, "n", (banks[:, 2, :], banks[:, 3, :]), ident)
        in_, chain_s, w_split, xb_done, mul_done, mh_done, ml_done, z_ready, z_added, sm, sm_e, sm_pe, w_fused = map(ph.sem, (
            "in", "dve_chain", "w_split", "xb_done", "mul_done", "mh_done", "ml_done", "z_ready", "z_added", "sm",
            "sm_e", "sm_pe", "w_fused"))
        SM = 6
        block = ph.stack.enter_context(nc.Block())

        @block.sync
        def _(sp):
            sp.dma_start(wc[:, :], io["w_c"].partition_broadcast(P)).then_inc(in_, 16)
            for n, name in enumerate(("b_c", "b_q", "b_cq")):
                sp.dma_start(bs[:, n:n + 1], io[name].partition_broadcast(P)).then_inc(in_, 16)
            sp.dma_start(ident[:, :], io["ident"]).then_inc(in_, 16)
            sp.dma_start(ones[:, :], io["ones"]).then_inc(in_, 16)
            sp.dma_start(w[:, :, :], io["wlT"].rearrange("(k p) f -> p k f", p=P)).then_inc(in_, 16)
            sp.dma_start(bias[:, :], io["b_l"].partition_broadcast(P)).then_inc(in_, 16)

        @block.gpsimd
        def _(pool):
            pool.wait_ge(in_, 128)
            for b in range(NB):
                pool.tensor_tensor(x1[:, b, :], x1[:, b, :], bias[:, :], ALU.add).then_inc(xb_done, 1)

        @block.vector
        def _(dve):
            chain = Chain(dve, chain_s)
            dve.wait_ge(in_, 128)
            for b in range(NB):
                if b:
                    chain.wait()
                chain.then(dve.tensor_tensor_reduce(junk[:, :], cn[:, b, :], wc[:, :], 1.0, 0.0, ALU.mult, ALU.add,
                                                    rowc[:, b:b + 1]))
            chain.wait()
            chain.link(dve.tensor_tensor(smax[:, :], rowc[:, :], keep["nmax"][:, :], ALU.subtract))
            for n in range(3):
                chain.link(dve.tensor_scalar(smax[:, :], smax[:, :], bs[:, n:n + 1], None, ALU.add))
            dve.tensor_reduce(one[:, 0:1], smax[:, :], AX.X, ALU.max).then_inc(sm, 1)
            low_parts = slice(KD, 3 * KD)
            chain.link(dve.tensor_copy(wh[:, low_parts, :], w[:, low_parts, :]))
            dve.tensor_tensor(wl[:, low_parts, :], w[:, low_parts, :], wh[:, low_parts, :], ALU.subtract).then_inc(w_split, 1)
            dve.wait_ge(sm_pe, 1)
            dve.tensor_reduce(one[0:1, 1:2], banks[0:1, SM, 0:P], AX.X, ALU.max, negate=True).then_inc(sm, 1)
            dve.wait_ge(sm_pe, 2)
            dve.tensor_copy(one[:, 2:3], banks[:, SM, P:P + 1]).then_inc(sm, 1)
            dve.wait_ge(sm_pe, 3)
            chain.link(dve.reciprocal(one[:, 4:5], banks[:, SM, P + 2:P + 3]))
            dve.wait_ge(sm_pe, 4)
            dve.tensor_scalar(q2c[0:1, :], banks[0:1, SM + 1, 0:D], one[0:1, 4:5], None, ALU.mult).then_inc(sm, 1)
            dve.wait_ge(sm_pe, 5)
            chain.link(dve.tensor_copy(q2col[:, :], banks[:, SM, 256:256 + KD]))
            for k in range(KD):
                chain.then(dve.scalar_tensor_tensor(out=w[:, k, :], in0=w[:, 3 * KD + k, :], scalar=q2col[:, k:k + 1],
                                                    in1=w[:, k, :], op0=ALU.mult, op1=ALU.add))
            chain.wait()
            chain.link(dve.tensor_copy(wh[:, 0:KD, :], w[:, 0:KD, :]))
            dve.tensor_tensor(wl[:, 0:KD, :], w[:, 0:KD, :], wh[:, 0:KD, :], ALU.subtract).then_inc(w_fused, 1)

            def low_q(c):
                for k in range(KD):
                    n = c * KD + k
                    dve.wait_ge(turn_q.high_done, n + 1)
                    if n >= 2:
                        dve.wait_ge(ml_done, n - 1)
                    dve.tensor_tensor(mul[:, k, :], turn_q.banks[n % 2], cT[:, k, tokens(c)], ALU.mult).then_inc(mul_done, 1)
                    turn_q.low(dve, qTh[:, c % 2, k, :], qTl[:, c % 2, k, :], c, k)
                for k in range(KD):
                    dve.wait_ge(mh_done, c * KD + k + 1)
                    dve.tensor_tensor(ml[:, c % 2, k, :], mul[:, k, :], mh[:, c % 2, k, :], ALU.subtract).then_inc(ml_done, 1)

            def low_n(c):
                for k in range(KD):
                    turn_n.low(dve, keep["nh"][:, k, tokens(c)], keep["nl"][:, k, tokens(c)], c, k)

            low_q(0)
            for c in range(NC):
                if c + 1 < NC:
                    low_q(c + 1)
                for b in range(c * BPC, (c + 1) * BPC):
                    dve.wait_ge(z_ready, b + 1)
                    dve.wait_ge(xb_done, b + 1)
                    dve.tensor_tensor(x1[:, b, :], banks[:, 4 + b % 2, 0:D], x1[:, b, :], ALU.add).then_inc(z_added, 1)
                dve.wait_ge(z_added, (c + 1) * BPC)
                ln.collect(dve, x1, c)
                ln.apply(dve, x1, cn, c)
                if c >= 1:
                    low_n(c - 1)
            low_n(NC - 1)

        @block.scalar
        def _(act):
            act.wait_ge(sm, 3)
            act.activation(e[:, :], smax[:, :], ACT.Exp, bias=one[:, 2:3], accum_out=one[:, 3:4]).then_inc(sm_e, 1)

            def high_q(c):
                for k in range(KD):
                    if c >= 2:
                        act.wait_ge(z_ready, (c - 1) * BPC)
                    turn_q.high(act, qTh[:, c % 2, k, :], c, k)
                for k in range(KD):
                    act.wait_ge(mul_done, c * KD + k + 1)
                    act.activation(mh[:, c % 2, k, :], mul[:, k, :], ACT.Copy).then_inc(mh_done, 1)

            def high_n(c):
                for k in range(KD):
                    turn_n.high(act, keep["nh"][:, k, tokens(c)], c, k)

            high_q(0)
            for c in range(NC):
                if c + 1 < NC:
                    high_q(c + 1)
                ln.root(act, c)
                if c >= 1:
                    high_n(c - 1)
            high_n(NC - 1)

        @block.tensor
        def _(pe):
            pe.wait_ge(in_, 128)
            pe.wait_ge(sm, 1)
            pe.transpose(banks[0:1, SM, 0:P], one[:, 0:1], ident[:, :]).then_inc(sm_pe, 1)
            pe.wait_ge(sm, 2)
            pe.matmul(banks[:, SM, P:P + 1], ones[0:1, :], one[0:1, 1:2], start=True, stop=True).then_inc(sm_pe, 1)
            pe.wait_ge(sm_e, 1)
            pe.matmul(banks[:, SM, P + 2:P + 3], ones[:, :], one[:, 3:4], start=True, stop=True).then_inc(sm_pe, 1)
            for b in range(NB):
                last = pe.matmul(banks[0:1, SM + 1, 0:D], e[:, b:b + 1], cn[:, b, :], start=b == 0, stop=b == NB - 1)
            last.then_inc(sm_pe, 1)
            pe.wait_ge(sm, 4)
            for k in range(KD):
                last = pe.matmul(banks[:, SM, 256 + k:257 + k], q2c[0:1, k * P:(k + 1) * P], ones[0:1, 0:1],
                                 start=True, stop=True)
            last.then_inc(sm_pe, 1)

            def turn_attended(c):
                for k in range(KD):
                    turn_q.turn(pe, c2q, c, k)

            def turn_norm(c):
                for k in range(KD):
                    turn_n.turn(pe, cn, c, k, ready=ln.done)

            def fuse(c):
                pe.wait_ge(ml_done, (c + 1) * KD)
                pe.wait_ge(turn_q.low_done, (c + 1) * KD)
                if c == 0:
                    pe.wait_ge(w_split, 1)
                    pe.wait_ge(w_fused, 1)
                for b in range(c * BPC, (c + 1) * BPC):
                    if b >= 2:
                        pe.wait_ge(z_added, b - 1)
                    tok, own = slice(b * P, (b + 1) * P), slice((b % BPC) * P, (b % BPC + 1) * P)
                    terms = [(ch[:, k, tok], cl[:, k, tok], wh[:, k, :], wl[:, k, :]) for k in range(KD)]
                    terms += [(qTh[:, c % 2, k, own], qTl[:, c % 2, k, own], wh[:, KD + k, :], wl[:, KD + k, :])
                              for k in range(KD)]
                    terms += [(mh[:, c % 2, k, own], ml[:, c % 2, k, own], wh[:, 2 * KD + k, :], wl[:, 2 * KD + k, :])
                              for k in range(KD)]
                    split_product(pe, banks[:, 4 + b % 2, 0:D], terms).then_inc(z_ready, 1)

            turn_attended(0)
            for c in range(NC):
                if c + 1 < NC:
                    turn_attended(c + 1)
                fuse(c)
                if c >= 1:
                    turn_norm(c - 1)
            turn_norm(NC - 1)


def phase_route(nc, io, keep):
    nh, nl, stack, wT = (keep[n] for n in ("nh", "nl", "stack", "wT"))
    with Phase(nc, "route") as ph:
        ident, identb = ph.sb("ident", [P, P]), ph.sb("identb", [P, P], BF16)
        w, wh, wl = ph.sb("w", [P, KD, D]), ph.sb("wh", [P, KD, D], F32R), ph.sb("wl", [P, KD, D], F32R)
        HE = FH * NE
        gw, gh, gl = ph.sb("gw", [P, HE // 2]), ph.sb("gh", [P, HE // 2], F32R), ph.sb("gl", [P, HE // 2], F32R)
        bcol, iota = ph.sb("bcol", [P, KD]), ph.sb("iota", [P, NE])
        th, tl = ph.sb("th", [P, 2, CH], F32R), ph.sb("tl", [P, 2, CH], F32R)
        G = BPC * FH
        row = {n: ph.sb(n, [P, G, NE]) for n in ("shifted", "expd", "prob", "eq", "cand", "first", "rest", "second", "wgt", "rem")}
        col = {n: ph.sb(n, [P, G]) for n in ("max", "sum", "rsum", "top", "pick")}
        parts = ph.sb("parts", [P, BPC, FH // 2, 3, 2 * NE], BF16)
        banks = ph.ps("banks", [P, 8, CH])
        X, GB, TB = 0, 2, 4
        in_, chain_s, w_split, h_ready, th_done, tl_done, stacked0, stacked1, g_ready, shifted, expd, w1_done, rem_done, \
            w2_done, w3_done, turned, copied, identb_in = map(ph.sem, (
                "in", "dve_chain", "w_split", "h_ready", "th_done", "tl_done", "stacked0", "stacked1", "g_ready", "shifted",
                "expd", "w1_done", "rem_done", "w2_done", "w3_done", "turned", "copied", "identb_in"))
        stacked = (stacked0, stacked1)
        block = ph.stack.enter_context(nc.Block())

        @block.sync
        def _(sp):
            for dst, name in ((ident, "ident"), (gw, "gate"), (bcol, "bm"), (iota, "iota")):
                sp.dma_start(dst[:, :], io[name]).then_inc(in_, 16)
            sp.dma_start(w[:, :, :], io["wm"].rearrange("(k p) f -> p k f", p=P)).then_inc(in_, 16)
            for n in range(KD * NC):
                c, k = n // KD, n % KD
                sp.wait_ge(th_done, n + 1)
                sp.wait_ge(tl_done, n + 1)
                for rows, src in enumerate((th, tl, th)):
                    for h in range(4):
                        sp.dma_start(stack[rows * FD:(rows + 1) * FD, n, h, :].bitcast(F32),
                                     src[h * FD:(h + 1) * FD, n % 2, :].bitcast(F32))\
                            .then_inc(stacked[n % 2], 16)
            for s in stacked:
                sp.wait_ge(s, 12 * 16 * KD * NC // 2)

        @block.gpsimd
        def _(pool):
            pool.dma_start(identb[:, :], io["ident"]).then_inc(identb_in, 16)

        @block.vector
        def _(dve):
            chain = Chain(dve, chain_s)
            dve.wait_ge(in_, 80)
            chain.then(dve.tensor_copy(wh[:, :, :], w[:, :, :]))
            chain.link(dve.tensor_copy(gh[:, :], gw[:, :]))
            dve.tensor_tensor(wl[:, :, :], w[:, :, :], wh[:, :, :], ALU.subtract).then_inc(w_split, 1)
            dve.tensor_tensor(gl[:, :], gw[:, :], gh[:, :], ALU.subtract).then_inc(w_split, 1)

            def spread(a):
                return a[:, :].unsqueeze(2).broadcast_to([P, G, NE])

            def pick(probs, out):
                chain.link(dve.tensor_reduce(col["top"][:, :], probs[:, :, :], AX.X, ALU.max))
                chain.link(dve.tensor_tensor(row["eq"][:, :, :], probs[:, :, :], spread(col["top"]), ALU.is_equal))
                chain.link(dve.tensor_tensor(row["cand"][:, :, :], row["eq"][:, :, :],
                                             iota[:, :].unsqueeze(1).broadcast_to([P, G, NE]), ALU.mult))
                chain.link(dve.tensor_reduce(col["pick"][:, :], row["cand"][:, :, :], AX.X, ALU.max))
                chain.link(dve.tensor_tensor(out[:, :, :], row["cand"][:, :, :], spread(col["pick"]), ALU.is_equal))

            def pair(n):
                dve.wait_ge(th_done, n + 1)
                dve.scalar_tensor_tensor(out=tl[:, n % 2, :], in0=banks[:, X + n % 2, :], scalar=bcol[:, n % KD:n % KD + 1],
                                         in1=th[:, n % 2, :], op0=ALU.add, op1=ALU.subtract).then_inc(tl_done, 1)

            for c in range(NC):
                for k in range(KD):
                    pair(c * KD + k)
                gates = banks[:, GB + c % 2, :].rearrange("p (g e) -> p g e", e=NE)
                dve.wait_ge(g_ready, c + 1)
                chain.link(dve.tensor_reduce(col["max"][:, :], gates, AX.X, ALU.max))
                dve.tensor_tensor(row["shifted"][:, :, :], gates, spread(col["max"]), ALU.subtract).then_inc(shifted, 1)
                dve.wait_ge(expd, c + 1)
                chain.link(dve.tensor_reduce(col["sum"][:, :], row["expd"][:, :, :], AX.X, ALU.add))
                chain.link(dve.reciprocal(col["rsum"][:, :], col["sum"][:, :]))
                chain.link(dve.tensor_tensor(row["prob"][:, :, :], row["expd"][:, :, :], spread(col["rsum"]), ALU.mult))
                pick(row["prob"], row["first"])
                chain.link(dve.scalar_tensor_tensor(out=row["rest"][:, :, :], in0=row["first"][:, :, :], scalar=-2.0,
                                                    in1=row["prob"][:, :, :], op0=ALU.mult, op1=ALU.add))
                pick(row["rest"], row["second"])
                chain.link(dve.tensor_tensor(row["first"][:, :, :], row["first"][:, :, :], row["second"][:, :, :], ALU.add))
                if c >= 1:
                    dve.wait_ge(rem_done, c)
                dve.tensor_tensor(row["wgt"][:, :, :], row["first"][:, :, :], row["prob"][:, :, :], ALU.mult).then_inc(w1_done, 1)
                dve.wait_ge(w2_done, 2 * c + 1)
                wide = lambda n: row[n][:, :, :].rearrange("p (b q h) e -> p b q (h e)", b=BPC, q=FH // 2)
                dve.tensor_tensor(wide("rem"), wide("wgt"), parts[:, :, :, 0, :], ALU.subtract).then_inc(rem_done, 1)
                dve.wait_ge(w2_done, 2 * c + 2)
                dve.tensor_tensor(parts[:, :, :, 2, :], wide("rem"), parts[:, :, :, 1, :], ALU.subtract).then_inc(w3_done, 1)

        @block.scalar
        def _(act):
            act.wait_ge(in_, 80)
            for c in range(NC):
                for k in range(KD):
                    n = c * KD + k
                    act.wait_ge(h_ready, n + 1)
                    if n >= 2:
                        act.wait_ge(stacked[n % 2], 12 * 16 * (n // 2))
                        act.wait_ge(g_ready, (n - 2) // KD + 1)
                    act.activation(th[:, n % 2, :], banks[:, X + n % 2, :], ACT.Identity, bias=bcol[:, k:k + 1]).then_inc(th_done, 1)
                act.wait_ge(shifted, c + 1)
                act.activation(row["expd"][:, :, :], row["shifted"][:, :, :], ACT.Exp).then_inc(expd, 1)
                wide = lambda n: row[n][:, :, :].rearrange("p (b q h) e -> p b q (h e)", b=BPC, q=FH // 2)
                act.wait_ge(w1_done, c + 1)
                if c >= 1:
                    act.wait_ge(turned, c)
                act.activation(parts[:, :, :, 0, :], wide("wgt"), ACT.Copy).then_inc(w2_done, 1)
                act.wait_ge(rem_done, c + 1)
                act.activation(parts[:, :, :, 1, :], wide("rem"), ACT.Copy).then_inc(w2_done, 1)
                act.wait_ge(turned, c + 1)
                for q in range(FH // 2):
                    src = banks[0:96, TB + q // 2, :].bitcast(BF16)[:, (q % 2) * CH:(q % 2 + 1) * CH]
                    act.activation(wT[:, c * 2 + q // 2, q % 2, :], src, ACT.Copy).then_inc(copied, 1)

        @block.tensor
        def _(pe):
            pe.wait_ge(in_, 80)
            pe.wait_ge(identb_in, 16)
            pe.wait_ge(w_split, 2)

            def product(c):
                for k in range(KD):
                    n = c * KD + k
                    if n >= 2:
                        pe.wait_ge(tl_done, n - 1)
                    feat = slice(k * P, (k + 1) * P)
                    split_product(pe, banks[:, X + n % 2, :], [(wh[:, j, feat], wl[:, j, feat], nh[:, j, tokens(c)],
                                                                nl[:, j, tokens(c)]) for j in range(KD)]).then_inc(h_ready, 1)

            def gate(c):
                pe.wait_ge(tl_done, (c + 1) * KD)
                for b in range(BPC):
                    for k in range(KD):
                        tok, at_ = slice(b * P, (b + 1) * P), b * P + k * (HE // 2)
                        last = split_product(pe, banks[:, GB + c % 2, at_:at_ + HE // 2],
                                             [(th[:, k, tok], tl[:, k, tok], gh[:, :], gl[:, :])])
                last.then_inc(g_ready, 1)

            def turn(c):
                pe.wait_ge(w3_done, c + 1)
                if c >= 1:
                    pe.wait_ge(copied, c * (FH // 2))
                for q in range(FH // 2):
                    dst = banks[0:96, TB + q // 2, :].bitcast(BF16)
                    for b in range(BPC):
                        last = pe.transpose(dst[:, (q % 2) * CH + b * P:(q % 2) * CH + (b + 1) * P],
                                            parts[:, b, q, :, :].rearrange("p a e -> p (a e)"), identb[:, :])
                last.then_inc(turned, 1)

            product(0)
            for c in range(NC):
                gate(c)
                if c + 1 < NC:
                    product(c + 1)
                turn(c)


def phase_experts(nc, io, keep):
    nh, nl, stack, wT, x2 = (keep[n] for n in ("nh", "nl", "stack", "wT", "x1"))
    acc = keep["v"][:, 0:8, :].rearrange("p (q h c) d -> p q h (c d)", q=2, h=2)
    prod = keep["v"][:, 8:16, :].rearrange("p (q h c) d -> p q h (c d)", q=2, h=2)
    hid0 = keep["attn"][:, :, :].rearrange("p (e h c) d -> p e h (c d)", e=EG, h=2)
    high, low = (a[:, :, :].rearrange("p k t -> p (k t)") for a in (nh, nl))
    R = KD * NC
    NST = 2 * NEG
    NX = NST * EG
    with Phase(nc, "ffn") as ph:
        w1 = ph.sb("w1", [96, NE, EI], F32R)
        w2 = ph.sb("w2", [P, NE, FD])
        b1, b2 = ph.sb("b1", [P, NE]), ph.sb("b2", [P, NEG])
        spread_w = ph.sb("spread_w", [96, 2 * NEG, P], BF16)
        sum_w = ph.sb("sum_w", [P, FD])
        wo, woh, wol = ph.sb("wo", [P, KD, D]), ph.sb("woh", [P, KD, D], F32R), ph.sb("wol", [P, KD, D], F32R)
        bias = ph.sb("bias", [P, D])
        hid1 = ph.sb("hid1", [P, EG, 2, CH])
        hid = (hid0, hid1)
        wide = ph.sb("wide", [P, 2, 2, CH])
        w1f = wide[0:96, :, :, :].rearrange("p a h c -> p (a h c)")
        banks = ph.ps("banks", [P, 8, CH])
        combined = ph.sb("combined", [P, CH])
        A, B, W = 0, 6, 7
        in_, wo_in, w1_split, w1_ready, wo_split, a_ready, gelu_done, b_ready, wide_ready, wide_copied, prod_ready, \
            added, sum_ready, comb_out, comb_high, comb_low, x_ready, out_ready, out_added, stored, spread_in = map(ph.sem, (
                "in", "wo_in", "w1_split", "w1_ready", "wo_split", "a_ready", "gelu_done", "b_ready", "wide_ready",
                "wide_copied", "prod_ready", "added", "sum_ready", "comb_out", "comb_high", "comb_low", "x_ready", "out_ready",
                "out_added", "stored", "spread_in"))
        block = ph.stack.enter_context(nc.Block())

        NHALF = 2 * NST
        COMBINE = (13, 5)

        def back(r, j, by):
            return (r, j - by) if j >= by else (r - 1, j - by + NHALF)

        def pair_of(x):
            return x % 3

        def earlier_tiles(x):
            last = x - 3 if x >= 3 else max(y for y in range(NX) if pair_of(y) == x) - NX
            return last + 1

        def wait_from(eng, sem, value, r):
            if not isinstance(r, int) or value > 0:
                eng.wait_ge(sem, value)

        @block.sync
        def _(sp):
            for dst, name in ((w1f, "w1"), (b1[:, :], "b1"), (b2[:, :], "b2"), (sum_w[:, :], "sum_w")):
                sp.dma_start(dst, io[name]).then_inc(in_, 16)
            sp.dma_start(w2[:, :, :], io["w2"]).then_inc(in_, 16)
            sp.dma_start(bias[:, :], io["bo"].partition_broadcast(P)).then_inc(wo_in, 16)
            sp.dma_start(wo[:, :, :], io["wo"].rearrange("(k p) f -> p k f", p=P)).then_inc(wo_in, 16)
            for c in range(NC):
                sp.wait_ge(out_added, (c + 1) * BPC)
                sp.dma_start(io["out"][c * CH:(c + 1) * CH, :].rearrange("(b p) d -> p b d", p=P),
                             x2[:, c * BPC:(c + 1) * BPC, :]).then_inc(stored, 16)
            sp.wait_ge(stored, 16 * NC)

        @block.gpsimd
        def _(pool):
            pool.dma_start(spread_w[:, :, :], io["spread_w"]).then_inc(spread_in, 16)
            pool.wait_ge(wo_in, 32)
            for b in range(NB):
                pool.tensor_tensor(x2[:, b, :], x2[:, b, :], bias[:, :], ALU.add).then_inc(x_ready, 1)

            def add(r, n):
                q = n // NEG
                pool.wait_ge(prod_ready, r * NHALF + 2 * n + 2)
                if n % NEG >= 2:
                    pool.wait_ge(added, r * 6 + 3 * q + n % NEG - 1)
                pool.tensor_tensor(acc[:, q, :, :], acc[:, q, :, :], prod[:, n % 2, :, :], ALU.add).then_inc(added, 1)

            with pool.Fori(0, R) as r:
                for n in range(NST):
                    if n % NEG:
                        add(r, n)

        @block.tensor
        def _(pe):
            def first(r, n, e):
                x = n * EG + e
                wait_from(pe, gelu_done, r * NX + earlier_tiles(x), r)
                g = n % NEG
                for h in range(2):
                    last = pe.matmul(banks[:, A + 2 * pair_of(x) + h, :], w1[:, g * EG + e, :],
                                     stack[0:96, at(r), 2 * (n // NEG) + h, :].rearrange("p a t -> p (a t)"), start=True, stop=True)
                last.then_inc(a_ready, 1)

            def widen(r, i, combined_before=None):
                n, h = i // 2, i % 2
                wait_from(pe, wide_copied, r * NHALF + i, r)
                if combined_before is not None:
                    pe.wait_ge(comb_out, combined_before)
                pe.matmul(banks[:, W, :], spread_w[:, h * NEG + n % NEG, :],
                          wT[:, at(r), n // NEG, :].rearrange("p a t -> p (a t)"), start=True, stop=True).then_inc(wide_ready, 1)

            def second(r, i):
                n, h = i // 2, i % 2
                if h == 0:
                    pe.wait_ge(gelu_done, r * NX + (n + 1) * EG)
                wait_from(pe, prod_ready, r * NHALF + i, r)
                for e in range(EG):
                    last = pe.matmul(banks[32 * e:32 * e + 32, B, :], w2[:, (n % NEG) * EG + e, :],
                                     hid[n % 2][:, e, h, :], start=True, stop=True)
                last.then_inc(b_ready, 1)

            def combine(r, q, copied):
                pe.wait_ge(added, r * 6 + 3 * q + 3)
                pe.wait_ge(wide_copied, copied)
                for h in range(2):
                    hh = 2 * q + h
                    last = pe.matmul(banks[32 * hh:32 * hh + 32, W, :], sum_w[:, :], acc[:, q, h, :], start=True, stop=True)
                last.then_inc(sum_ready, 1)

            def round_(loop, lone=False):
                for j in range(NHALF):
                    r = fresh(pe, loop, R - 1, 1)
                    for e in range(2):
                        first(r, j // 2, 2 * (j % 2) + e)
                    combined_before = None
                    if j == COMBINE[0]:
                        combine(r, 0, r * NHALF + j - 1)
                        combined_before = 2 * r + 1
                    if j == COMBINE[1] and not lone:
                        combine(r - 1, 1, r * NHALF + j - 1)
                        combined_before = 2 * r
                    if j >= 2 or not lone:
                        second(*back(r, j, 2))
                    if j >= 1 or not lone:
                        widen(*back(r, j, 1), combined_before)

            pe.wait_ge(in_, 80)
            pe.wait_ge(spread_in, 16)
            pe.wait_ge(w1_ready, 1)
            round_(0, lone=True)
            with pe.Fori(1, R) as r:
                round_(r)
            second(R - 1, NHALF - 2)
            widen(R - 1, NHALF - 1)
            second(R - 1, NHALF - 1)
            combine(R - 1, 1, R * NHALF)
            pe.wait_ge(comb_low, 2 * R)
            pe.wait_ge(wo_split, 2)
            for b in range(NB):
                if b >= 2:
                    pe.wait_ge(out_added, b - 1)
                terms = []
                for k in range(KD):
                    own = at(((b // BPC) * KD + k) * CH + (b % BPC) * P, P)
                    terms.append((high[:, own], low[:, own], woh[:, k, :], wol[:, k, :]))
                split_product(pe, banks[:, A + b % 2, 0:D], terms).then_inc(out_ready, 1)

        @block.scalar
        def _(act):
            def gelu(r, n, e):
                x = n * EG + e
                act.wait_ge(a_ready, r * NX + x + 1)
                if e == 0:
                    wait_from(act, b_ready, r * NHALF + 2 * n - 2, r)
                pair = A + 2 * pair_of(x)
                ex = (n % NEG) * EG + e
                act.activation(hid[n % 2][:, e, :, :], banks[:, pair:pair + 2, :], ACT.Gelu,
                               bias=b1[:, ex:ex + 1]).then_inc(gelu_done, 1)

            act.wait_ge(in_, 80)
            for n in range(NST):
                for e in range(EG):
                    gelu(0, n, e)
            with act.Fori(1, R) as r:
                for n in range(NST):
                    for e in range(EG):
                        gelu(r, n, e)

        @block.vector
        def _(dve):
            def copy_wide(r, i):
                dve.wait_ge(wide_ready, r * NHALF + i + 1)
                wait_from(dve, prod_ready, r * NHALF + i - 3, r)
                dve.tensor_copy(wide[:, (i // 2) % 2, i % 2, :], banks[:, W, :]).then_inc(wide_copied, 1)

            def weigh(r, i):
                n, h = i // 2, i % 2
                q, g = n // NEG, n % NEG
                dve.wait_ge(wide_copied, r * NHALF + i + 1)
                if h == 0:
                    if g == 0:
                        wait_from(dve, sum_ready, 2 * r + q - 1, r)
                    elif g < 3:
                        wait_from(dve, added, r * 6 + 3 * q, r)
                    else:
                        dve.wait_ge(added, r * 6 + 3 * q + 1)
                dst = acc[:, q] if g == 0 else prod[:, n % 2]
                dve.wait_ge(b_ready, r * NHALF + i + 1)
                dve.scalar_tensor_tensor(out=dst[:, h, :], in0=banks[:, B, :], scalar=b2[:, g:g + 1],
                                         in1=wide[:, n % 2, h, :], op0=ALU.add, op1=ALU.mult).then_inc(prod_ready, 1)

            def copy_combined(r, q):
                dve.wait_ge(sum_ready, 2 * r + q + 1)
                wait_from(dve, comb_low, 2 * r + q, r)
                rows = slice(64 * q, 64 * q + 64)
                dve.tensor_copy(combined[rows, :], banks[rows, W, :]).then_inc(comb_out, 1)

            def split_combined(r, q):
                rows, own = slice(64 * q, 64 * q + 64), at(r * CH, CH)
                dve.wait_ge(comb_out, 2 * r + q + 1)
                dve.tensor_copy(high[rows, own], combined[rows, :]).then_inc(comb_high, 1)
                dve.wait_ge(comb_high, 2 * r + q + 1)
                dve.tensor_tensor(low[rows, own], combined[rows, :], high[rows, own], ALU.subtract).then_inc(comb_low, 1)

            def round_(loop, lone=False):
                for j in range(NHALF):
                    r = fresh(dve, loop, R - 1, 1)
                    now = None
                    if j == COMBINE[0]:
                        now = (r, 0)
                    if j == COMBINE[1] and not lone:
                        now = (r - 1, 1)
                    if now:
                        copy_combined(*now)
                    if j >= 2 or not lone:
                        weigh(*back(r, j, 2))
                    if j >= 1 or not lone:
                        copy_wide(*back(r, j, 1))
                    if now:
                        split_combined(*now)

            dve.wait_ge(in_, 80)
            dve.tensor_copy(w1[:, :, :].rearrange("p e i -> p (e i)"), w1f).then_inc(w1_split, 1)
            dve.wait_ge(w1_split, 1)
            dve.tensor_tensor(w1[64:96, :, :].rearrange("p e i -> p (e i)"), w1f[64:96, :],
                              w1[64:96, :, :].rearrange("p e i -> p (e i)"), ALU.subtract).then_inc(w1_ready, 1)
            dve.wait_ge(w1_ready, 1)
            dve.wait_ge(wo_in, 32)
            dve.tensor_copy(woh[:, :, :], wo[:, :, :]).then_inc(wo_split, 1)
            dve.wait_ge(wo_split, 1)
            dve.tensor_tensor(wol[:, :, :], wo[:, :, :], woh[:, :, :], ALU.subtract).then_inc(wo_split, 1)
            round_(0, lone=True)
            with dve.Fori(1, R) as r:
                round_(r)
            weigh(R - 1, NHALF - 2)
            copy_wide(R - 1, NHALF - 1)
            weigh(R - 1, NHALF - 1)
            copy_combined(R - 1, 1)
            split_combined(R - 1, 1)
            for b in range(NB):
                dve.wait_ge(out_ready, b + 1)
                dve.wait_ge(x_ready, b + 1)
                dve.tensor_tensor(x2[:, b, :], banks[:, A + b % 2, 0:D], x2[:, b, :], ALU.add).then_inc(out_added, 1)


def split_product(pe, out, terms, start=True, stop=True):
    n = 0
    for ah, al, bh, bl in terms:
        for a, b in ((ah, bh), (ah, bl), (al, bh)):
            last = pe.matmul(out, a, b, start=start and n == 0, stop=stop and n == 3 * len(terms) - 1)
            n += 1
    return last


def program(nc, io, stop_after=99):
    keep = {}
    with ExitStack() as stack:
        def sb(name, shape, dt=F32):
            keep[name] = stack.enter_context(nc.sbuf_tensor("keep_" + name, shape, dt))

        for name in ("v", "attn"):
            sb(name, [P, NB, D])
        phase_qkv(nc, io, keep)
        phase_attention(nc, io, keep)
        keep["cn"], keep["c2q"] = keep["v"], keep["attn"]
        sb("x1", [P, NB, D])
        sb("ch", [P, KD, T], F32R)
        sb("cl", [P, KD, T], F32R)
        keep["nh"], keep["nl"] = keep["ch"], keep["cl"]
        with ExitStack() as inner:
            keep["cT"] = inner.enter_context(nc.sbuf_tensor("keep_cT", [P, KD, T], F32))
            keep["nmax"] = inner.enter_context(nc.sbuf_tensor("keep_nmax", [P, NB], F32))
            phase_projection(nc, io, keep)
            phase_cross(nc, io, keep)
            phase_fuse(nc, io, keep)
        sb("stack", [96, KD * NC, 4, CH], F32R)
        sb("wT", [96, KD * NC, 2, CH], BF16)
        phase_route(nc, io, keep)
        phase_experts(nc, io, keep)


def host_inputs(inputs):
    import numpy as np
    g = {k: np.asarray(v) for k, v in inputs.items()}
    c = np.ascontiguousarray
    a = {"x": g["x"][0], "ctx": g["ctx_1024"][0], "ctxT": g["ctx_1024"][0].T,
         "wqkvT": g["L0_attn_w_qkv"].T, "ident": np.eye(P, dtype=np.float32)}
    a["ones"] = np.ones((P, P), np.float32)
    a["ctxT"] = np.pad(a["ctxT"], ((0, 0), (0, LPAD - L)))
    a["woutT"], a["b_out"] = g["L0_attn_w_out"].T, g["L0_attn_b_out"]
    a["wlT"], a["b_l"] = g["L0_xattn_W_l"].T, g["L0_xattn_b_l"]
    a["w_c"] = g["L0_xattn_w_c"]
    for n in ("w_cq", "w_q"):
        a[n] = g["L0_xattn_" + n].reshape(KD, P).T
    for n in ("b_cq", "b_c", "b_q"):
        a[n] = g["L0_xattn_" + n].reshape(1)
    f = lambda n: g["L0_ffn_" + n]
    eye = np.eye(4, dtype=np.float32)
    a["wm"], a["bm"], a["wo"], a["bo"] = f("Wm"), f("bm").reshape(KD, P).T, f("Wo"), f("bo")
    gate = np.zeros((4, FD, 4, NE), np.float32)
    for h in range(4):
        gate[h, :, h, :] = f("expert_emb")
    a["gate"] = gate.reshape(P, 4 * NE)
    a["iota"] = np.tile(np.arange(NE, 0, -1, dtype=np.float32), (P, 1))
    a["w1"] = np.tile(f("W1").transpose(1, 0, 2).reshape(FD, NE * EI), (3, 1))
    a["b1"], a["w2"] = f("b1").T, f("W2").transpose(1, 0, 2)
    a["b2"] = f("b2").reshape(NEG, EG * FD).T
    a["sum_w"] = np.tile(np.eye(FD, dtype=np.float32), (EG, 1))
    spread = np.zeros((3, 2, NE, 2, NEG, EG, FD), np.float32)
    for h in range(2):
        for e in range(NE):
            spread[:, h, e, h, e // EG, e % EG, :] = 1.0
    a["spread_w"] = spread.reshape(96, 2 * NEG, P)
    future = np.triu(np.full((P, P), NEGBIG, np.float32), 1)
    a["mask_qk"], a["mask_kq"] = future, future.T
    return {k: c(v) for k, v in a.items()}


SCRATCH = {"qk_parts": ((2, 3, D, T), BF16)}


def declare(nc, arrays):
    from concourse import mybir as _mybir
    io = {}
    for name, a in arrays.items():
        io[name] = nc.dram_tensor(f"in_{name}", a.shape, _mybir.dt.from_np(a.dtype), kind="ExternalInput").ap()
    for name, (shape, dt) in SCRATCH.items():
        io[name] = nc.dram_tensor(f"scratch_{name}", shape, dt, kind="Internal").ap()
    io["out"] = nc.dram_tensor("out", (T, D), F32, kind="ExternalOutput").ap()
    return io


def kernel(**inputs):
    import concourse.bacc as _bacc
    from concourse.bass_utils import run_bass_kernel_spmd as _run

    nc = _bacc.Bacc("TRN2", target_bir_lowering=False, num_devices=1)
    arrays = host_inputs(inputs)
    io = declare(nc, arrays)
    program(nc, io)
    r = _run(nc, [{f"in_{k}": v for k, v in arrays.items()}], core_ids=[0])
    return r.results[0]["out"].reshape(1, T, D)
```

```python
from contextlib import ExitStack

import concourse.bass as bass
from concourse import mybir

F32 = mybir.dt.float32
F32R = mybir.dt.float32r
BF16 = mybir.dt.bfloat16
ALU = mybir.AluOpType
ACT = mybir.ActivationFunctionType
AX = mybir.AxisListType

P = 128
T = 2048
D = 256
KD = D // P
NB = T // P
CH = 512
NC = T // CH
BPC = CH // P
LN_EPS = 1e-5

NH, HD = 16, 16
HG = 4
NG = NH // HG
VW = HD + 1
SCALE = HD ** -0.5
Q_PART = [0, 1, 2, 0, 1, 0]
K_PART = [0, 0, 0, 1, 1, 2]
KROWS = HD * len(Q_PART)
MROWS = KROWS + 3

L = 1601
LB = (L + P - 1) // P
LLAST = L - (LB - 1) * P
LPAD = L + L % 2

FH, FD = 8, 32
NE, EI = 16, 128
EG = 4
NEG = NE // EG
NEGBIG = -1e30
FREE = 1


def tokens(c):
    return slice(c * CH, (c + 1) * CH)


def at(i, n=1):
    return bass.ds(i, n)


def fresh(eng, i, top, least=0):
    if isinstance(i, int):
        return i
    reg = eng.alloc_register()
    eng.reg_mov(reg, i)
    return eng.snap(reg, min_val=least, max_val=top)


class Chain:

    def __init__(self, eng, sem, base=0):
        self.eng, self.sem, self.base, self.n = eng, sem, base, 0

    def then(self, instruction):
        instruction.then_inc(self.sem, 1)
        self.n += 1

    def wait(self):
        self.eng.wait_ge(self.sem, self.base + self.n)

    def link(self, instruction):
        self.then(instruction)
        self.wait()


class Phase:

    def __init__(self, nc, name):
        self.nc, self.name, self.stack = nc, name, ExitStack()

    def __enter__(self):
        self.stack.__enter__()
        return self

    def __exit__(self, *a):
        return self.stack.__exit__(*a)

    def sb(self, name, shape, dt=F32):
        return self.stack.enter_context(self.nc.sbuf_tensor(f"{self.name}_{name}", shape, dt))

    def ps(self, name, shape, dt=F32):
        return self.stack.enter_context(self.nc.psum_tensor(f"{self.name}_{name}", shape, dt))

    def sem(self, name):
        return self.stack.enter_context(self.nc.semaphore(f"{self.name}_{name}"))


class LayerNorm:

    def __init__(self, ph, name):
        self.stats, self.mv = ph.sb(name + "_stats", [P, NB, 6]), ph.sb(name + "_mv", [P, NB, 2])
        self.var, self.std, self.rstd = (ph.sb(f"{name}_{n}", [P, NB]) for n in ("var", "std", "rstd"))
        self.stats_done, self.mv_done, self.var_ready, self.std_ready, self.rstd_ready, self.done = (
            ph.sem(f"{name}_{n}") for n in ("stats_done", "mv_done", "var_ready", "std_ready", "rstd_ready", "done"))

    def collect(self, dve, x, c):
        blocks = range(c * BPC, (c + 1) * BPC)
        for b in blocks:
            dve.bn_stats(self.stats[:, b, :], x[:, b, :]).then_inc(self.stats_done, 1)
        for b in blocks:
            dve.wait_ge(self.stats_done, b + 1)
            dve.bn_aggr(self.mv[:, b, :], self.stats[:, b, :]).then_inc(self.mv_done, 1)
        dve.wait_ge(self.mv_done, (c + 1) * BPC)
        at_c = slice(c * BPC, (c + 1) * BPC)
        dve.tensor_scalar(self.var[:, at_c], self.mv[:, at_c, 1], LN_EPS, None, ALU.add).then_inc(self.var_ready, 1)

    def root(self, act, c):
        at_c = slice(c * BPC, (c + 1) * BPC)
        act.wait_ge(self.var_ready, c + 1)
        act.activation(self.std[:, at_c], self.var[:, at_c], ACT.Sqrt).then_inc(self.std_ready, 1)

    def apply(self, dve, x, out, c):
        at_c = slice(c * BPC, (c + 1) * BPC)
        dve.wait_ge(self.std_ready, c + 1)
        dve.reciprocal(self.rstd[:, at_c], self.std[:, at_c]).then_inc(self.rstd_ready, 1)
        dve.wait_ge(self.rstd_ready, c + 1)
        for b in range(c * BPC, (c + 1) * BPC):
            dve.tensor_scalar(out[:, b, :], x[:, b, :], self.mv[:, b, 0:1], self.rstd[:, b:b + 1],
                              ALU.subtract, ALU.mult).then_inc(self.done, 1)


class Turn:

    def __init__(self, ph, name, banks, ident):
        self.banks, self.ident = banks, ident
        self.turned, self.high_done, self.low_done = (
            ph.sem(f"{name}_{n}") for n in ("turned", "high_done", "low_done"))

    def turn(self, pe, src, c, k, ready=None):
        n = c * KD + k
        if ready is not None:
            pe.wait_ge(ready, (c + 1) * BPC)
        if n >= 2:
            pe.wait_ge(self.low_done, n - 1)
        for j in range(BPC):
            last = pe.transpose(self.banks[n % 2][:, j * P:(j + 1) * P], src[:, c * BPC + j, k * P:(k + 1) * P],
                                self.ident[:, :])
        last.then_inc(self.turned, 1)

    def high(self, act, hi, c, k, plain=None):
        n = c * KD + k
        act.wait_ge(self.turned, n + 1)
        if plain is not None:
            act.activation(plain, self.banks[n % 2], ACT.Copy)
        act.activation(hi, self.banks[n % 2], ACT.Copy).then_inc(self.high_done, 1)

    def low(self, dve, hi, lo, c, k):
        n = c * KD + k
        dve.wait_ge(self.high_done, n + 1)
        dve.tensor_tensor(lo, self.banks[n % 2], hi, ALU.subtract).then_inc(self.low_done, 1)


def phase_qkv(nc, io, keep):
    with Phase(nc, "qkv") as ph:
        x = ph.sb("x", [P, NB, D])
        w = ph.sb("w", [P, KD, 3 * D])
        wh, wl = ph.sb("wh", [P, KD, 3 * D], F32R), ph.sb("wl", [P, KD, 3 * D], F32R)
        ident = ph.sb("ident", [P, P])
        xh, xl = ph.sb("xh", [P, KD, T], F32R), ph.sb("xl", [P, KD, T], F32R)
        parts = ph.sb("parts", [P, 3, 3, CH], BF16)
        rem = ph.sb("rem", [P, 3, CH])
        banks = ph.ps("banks", [P, 8, CH])
        ln = LayerNorm(ph, "ln")
        turn = Turn(ph, "turn", (banks[:, 0, :], banks[:, 1, :]), ident)
        ident_in, w_in, wh_done, w_split, qk_ready, p1_ready, r1_ready, p2_ready, p3_ready, v_ready, v_out, v_out_act = map(ph.sem, (
            "ident_in", "w_in", "wh_done", "w_split", "qk_ready", "p1_ready", "r1_ready", "p2_ready", "p3_ready", "v_ready", "v_out", "v_out_act"))
        x_in = [ph.sem(f"x_in{c}") for c in range(NC)]
        stored = [ph.sem(f"stored{n}") for n in range(3)]
        FT = 2 * KD
        NQ = FT * NC
        QB, VB = 2, 5
        block = ph.stack.enter_context(nc.Block())

        @block.sync
        def _(sp):
            for c in range(NC):
                sp.dma_start(x[:, c * BPC:(c + 1) * BPC, :],
                             io["x"][tokens(c), :].rearrange("(b p) d -> p b d", p=P)).then_inc(x_in[c], 16)
                if c == 0:
                    sp.dma_start(ident[:, :], io["ident"]).then_inc(ident_in, 16)
                    sp.dma_start(w[:, :, :], io["wqkvT"].rearrange("(k p) f -> p k f", p=P)).then_inc(w_in, 16)
            for n in range(NQ):
                ft, c = n % FT, n // FT
                sp.wait_ge(p3_ready, n + 1)
                sp.dma_start(io["qk_parts"][ft // KD, :, at((ft % KD) * P, P), tokens(c)].rearrange("a p t -> p a t"),
                             parts[:, n % 3, :, :]).then_inc(stored[n % 3], 16)
            for s in range(3):
                sp.wait_ge(stored[s], 16 * len(range(s, NQ, 3)))

        @block.vector
        def _(dve):
            def normalise(c):
                dve.wait_ge(x_in[c], 16)
                ln.collect(dve, x, c)
                ln.apply(dve, x, x, c)

            def triple(n):
                dve.wait_ge(p1_ready, n + 1)
                dve.tensor_tensor(rem[:, n % 3, :], banks[:, QB + n % 3, :], parts[:, n % 3, 0, :], ALU.subtract)\
                    .then_inc(r1_ready, 1)

            def finish(n):
                dve.wait_ge(p2_ready, n + 1)
                dve.tensor_tensor(parts[:, n % 3, 2, :], rem[:, n % 3, :], parts[:, n % 3, 1, :], ALU.subtract)\
                    .then_inc(p3_ready, 1)

            def low(c):
                for k in range(KD):
                    turn.low(dve, xh[:, k, tokens(c)], xl[:, k, tokens(c)], c, k)

            normalise(0)
            normalise(1)
            low(0)
            dve.wait_ge(wh_done, 1)
            dve.tensor_tensor(wl[:, :, :], w[:, :, :], wh[:, :, :], ALU.subtract).then_inc(w_split, 1)
            low(1)
            for c in range(2, NC):
                normalise(c)
            for c in range(NC):
                for n in range(c * FT, (c + 1) * FT):
                    triple(n)
                    if n >= 1:
                        finish(n - 1)
                if c + 2 < NC:
                    low(c + 2)
            finish(NQ - 1)
            for b in range(1, NB, 2):
                dve.wait_ge(v_ready, b + 1)
                dve.tensor_copy(keep["v"][:, b, :], banks[:, VB + b % 3, 0:D]).then_inc(v_out, 1)

        @block.scalar
        def _(act):
            def first(n):
                act.wait_ge(qk_ready, n + 1)
                if n >= 3:
                    act.wait_ge(stored[n % 3], 16 * (n // 3))
                act.activation(parts[:, n % 3, 0, :], banks[:, QB + n % 3, :], ACT.Copy).then_inc(p1_ready, 1)

            def second(n):
                act.wait_ge(r1_ready, n + 1)
                act.activation(parts[:, n % 3, 1, :], rem[:, n % 3, :], ACT.Copy).then_inc(p2_ready, 1)

            def high(c):
                for k in range(KD):
                    turn.high(act, xh[:, k, tokens(c)], c, k)

            for c in range(2):
                ln.root(act, c)
            high(0)
            act.wait_ge(w_in, 16)
            act.activation(wh[:, :, :], w[:, :, :], ACT.Copy).then_inc(wh_done, 1)
            high(1)
            for c in range(2, NC):
                ln.root(act, c)
            for c in range(NC):
                for n in range(c * FT, (c + 1) * FT):
                    first(n)
                    if n >= 1:
                        second(n - 1)
                if c + 2 < NC:
                    high(c + 2)
            second(NQ - 1)
            for b in range(0, NB, 2):
                act.wait_ge(v_ready, b + 1)
                act.activation(keep["v"][:, b, :], banks[:, VB + b % 3, 0:D], ACT.Copy).then_inc(v_out_act, 1)

        @block.tensor
        def _(pe):
            def turn_chunk(c):
                for k in range(KD):
                    turn.turn(pe, x, c, k, ready=ln.done)

            pe.wait_ge(ident_in, 16)
            turn_chunk(0)
            turn_chunk(1)
            pe.wait_ge(w_split, 1)
            for c in range(NC):
                pe.wait_ge(turn.low_done, (c + 1) * KD)
                for n in range(c * FT, (c + 1) * FT):
                    if n >= 3:
                        pe.wait_ge(r1_ready, n - 2)
                    feat = slice((n % FT) * P, (n % FT + 1) * P)
                    split_product(pe, banks[:, QB + n % 3, :],
                                  [(wh[:, k, feat], wl[:, k, feat], xh[:, k, tokens(c)], xl[:, k, tokens(c)])
                                   for k in range(KD)]).then_inc(qk_ready, 1)
                    if n == c * FT and c + 2 < NC:
                        turn_chunk(c + 2)
            for b in range(NB):
                if b >= 3:
                    pe.wait_ge(v_out if (b - 3) % 2 else v_out_act, (b - 3) // 2 + 1)
                tok, feat = slice(b * P, (b + 1) * P), slice(2 * D, 3 * D)
                split_product(pe, banks[:, VB + b % 3, 0:D],
                              [(xh[:, k, tok], xl[:, k, tok], wh[:, k, feat], wl[:, k, feat]) for k in range(KD)]).then_inc(v_ready, 1)


def causal_steps():
    return [(qc, kb, max(kb - BPC * qc, 0) * P) for qc in range(NC) for kb in range(BPC * (qc + 1))]


def max_tiles():
    return [(qb, c, min(CH, (qb + 1) * P - c * CH), h)
            for qb in range(NB) for c in range(qb // BPC + 1) for h in range(HG)]


def ring_items(steps, tiles, ahead, lag):
    ns, wait = len(steps), 6
    chunk_end = {max(u for u, tile in enumerate(tiles) if tile[0] // BPC == qc): qc for qc in range(NC)}

    def with_rows(run):
        items, pending = [], []
        for n, (a, u) in enumerate(run):
            items.append(("max", a, u))
            if u in chunk_end:
                pending.append((n + wait, ("rows", a, chunk_end[u])))
            if pending and pending[0][0] <= n:
                items.append(pending.pop(0)[1])
        assert not pending
        return items

    before = with_rows([(0, u) for u in range(ahead)])
    items = with_rows([(0, u) for u in range(ahead, len(tiles))] + [(1, u) for u in range(ahead)])
    cost = lambda item: 64 + tiles[item[2]][2] if item[0] == "max" else 300
    weights = [(CH - off + 64) * w for _, _, off in steps for w in (2, 1, 1)]
    plan, given, due, total = [[[], [], [], []] for _ in range(ns + lag)], 0.0, 0.0, sum(map(cost, items))
    for slot, weight in enumerate(weights):
        due += total * weight / sum(weights)
        while items and (given + cost(items[0]) / 2 <= due or slot == len(weights) - 1):
            given += cost(items[0])
            plan[slot // 3][slot % 3].append(items.pop(0))
    for qc in range(NC):
        last = max(i for i, step in enumerate(steps) if step[0] == qc)
        plan[min(last + 4, ns + lag - 1)][3].append(("out", 0, qc))
    return before, plan


def phase_attention(nc, io, keep):
    with Phase(nc, "att") as ph:
        qst, kst = ph.sb("qst", [P, NH * T], BF16), ph.sb("kst", [P, NH * T], BF16)
        vg = ph.sb("vg", [P, NB, HG, 32])
        prob = ph.sb("prob", [P, 3, HG, CH])
        osb = ph.sb("osb", [P, 2, CH])
        rden = ph.sb("rden", [P, BPC, HG])
        pmax = ph.sb("pmax", [P, HG * NB, NC])
        NU = HG * BPC
        NTURN = 96
        nmax, nrem = ph.sb("nmax", [P, HG, BPC]), ph.sb("nrem", [P, HG, BPC])
        nparts = ph.sb("nparts", [P, NTURN], BF16)
        npart = nparts[:, 0:3 * NU].rearrange("p (a h b) -> p a h b", a=3, h=HG)
        nrow = ph.sb("nrow", [NTURN, 2, P], BF16)
        ident, identb = ph.sb("ident", [P, P]), ph.sb("identb", [P, P], BF16)
        mask_qk, mask_kq = ph.sb("mask_qk", [P, P], BF16), ph.sb("mask_kq", [P, P], BF16)
        banks = ph.ps("banks", [P, 8, CH])
        S, O, RING = 0, 4, (5, 6, 7)

        const_in, stack_in, ones_ready, pmax_ready, vg_zero, ring_ready, ring_read, chain_s, nm_split, \
            vg_ready, s_ready, exp_done, pv_done, o_copied, rden_ready, constb_in = map(ph.sem, (
                "const_in", "stack_in", "ones_ready", "pmax_ready", "vg_zero", "ring_ready",
                "ring_read", "dve_chain", "nm_split", "vg_ready", "s_ready",
                "exp_done", "pv_done", "o_copied", "rden_ready", "constb_in"))
        nm_in = [ph.sem(f"nm_in{p}") for p in range(2)]
        first_in = [ph.sem(f"first_in{c}") for c in range(NC)]
        steps, tiles = causal_steps(), max_tiles()
        NS, NM = len(steps), len(tiles)
        last_step = [max(i for i, s in enumerate(steps) if s[0] == qc) for qc in range(NC)]
        LAG = 2
        AHEAD = next(u for u, tile in enumerate(tiles) if tile[0] == NB - 5)
        before, plan = ring_items(steps, tiles, AHEAD, LAG)
        last_plan = [[[item for item in slot if not item[1]] for slot in step] for step in plan]
        flat = lambda p: [item for step in p for slot in step for item in slot]
        FIRST, ITEMS = len(before), len(flat(plan))
        assert ITEMS % len(RING) == 0
        PARTS_IN = 2 * len(Q_PART) * 16
        ROWS_IN = 3 * HG * 16

        need_next = next(s for s, step in enumerate(plan) for slot in step for item in slot if item[1])

        def rows_at(g, qc):
            if ("rows", 0, qc) in before:
                return before.index(("rows", 0, qc)) if g == 0 else FIRST + (g - 1) * ITEMS + flat(plan).index(("rows", 1, qc))
            return FIRST + g * ITEMS + flat(plan if g < NG - 1 else last_plan).index(("rows", 0, qc))

        CHAIN = 4
        block = ph.stack.enter_context(nc.Block())

        @block.sync
        def _(sp):
            sp.dma_start(ident[:, :], io["ident"]).then_inc(const_in, 16)

            def load(g, own, sem):
                for side, (dst, which) in enumerate(((qst, Q_PART), (kst, K_PART))):
                    for j, part in enumerate(which):
                        src = io["qk_parts"][side, part, g * (HG * HD):(g + 1) * (HG * HD), own]
                        out = dst[j * HD:(j + 1) * HD, g * (HG * T):(g + 1) * (HG * T)]
                        sp.dma_start(out.rearrange("d (h t) -> d h t", h=HG)[:, :, own],
                                     src.rearrange("(h d) t -> d h t", h=HG)).then_inc(sem, 16)

            for c in range(NC):
                load(0, tokens(c), first_in[c])
            for g in range(NG):
                for qc in range(NC):
                    sp.wait_ge(ring_read, rows_at(g, qc) + 1)
                    for part in range(3):
                        for h in range(HG):
                            own = (g * HG + h) * T + qc * CH
                            sp.dma_start(qst[KROWS + part:KROWS + part + 1, own:own + CH].rearrange("a (b t) -> a b t", t=P),
                                         nrow[part * NU + h * BPC:part * NU + (h + 1) * BPC, qc % 2, :])\
                                .then_inc(nm_in[qc % 2], 16)
                    if qc == 1 and g + 1 < NG:
                        if g >= 1:
                            sp.wait_ge(stack_in, g * PARTS_IN)
                        load(g + 1, slice(0, T), stack_in)

        @block.gpsimd
        def _(pool):
            for dst, name in ((identb, "ident"), (mask_qk, "mask_qk"), (mask_kq, "mask_kq")):
                pool.dma_start(dst[:, :], io[name]).then_inc(constb_in, 16)
            pool.memset(kst[KROWS:MROWS, :], 1.0).then_inc(ones_ready, 1)

        @block.tensor
        def _(pe):
            def max_tile(r, u, bank):
                qb, c, width, h = tiles[u]
                out = banks[:, bank, 0:width]
                diagonal = c == qb // BPC
                last = pe.matmul(out, qst[0:KROWS, at(r * (HG * T) + h * T + qb * P, P)],
                                 kst[0:KROWS, at(r * (HG * T) + h * T + c * CH, width)], start=True, stop=not diagonal)
                if diagonal:
                    last = pe.matmul(out[:, width - P:width], identb[:, :], mask_qk[:, :], start=False, stop=True)
                return last

            def turn_maxima(r, qc, bank):
                pe.wait_ge(nm_split, r * NC + qc + 1)
                rowbank = banks[0:NTURN, bank, :].bitcast(BF16)
                return pe.transpose(rowbank[:, 0:P], nparts[:, :], identb[:, :])

            def turn_output(g, qc, bank):
                pe.wait_ge(o_copied, FREE + g * NC + qc + 1)
                for j in range(BPC):
                    last = pe.transpose(banks[:, bank, j * P:(j + 1) * P], osb[:, qc % 2, j * P:(j + 1) * P], ident[:, :])
                return last

            def items(g, slot, n):
                for kind, ahead, what in slot:
                    pe.wait_ge(ring_read, FIRST + g * ITEMS + n - len(RING) + 1)
                    bank = RING[(FIRST + n) % len(RING)]
                    last = (max_tile(g + ahead, what, bank) if kind == "max" else
                            turn_maxima(g + ahead, what, bank) if kind == "rows" else turn_output(g, what, bank))
                    last.then_inc(ring_ready, 1)
                    n += 1
                return n

            def scores(g, s, pair):
                qc, kb, off = steps[s]
                if kb == 0 and pair == 0:
                    pe.wait_ge(nm_in[qc % 2], g * (NC // 2 * ROWS_IN) + (qc // 2 + 1) * ROWS_IN)
                if s >= 1:
                    pe.wait_ge(exp_done, g * (2 * NS) + 2 * (s - 1) + pair + 1)
                for h in (2 * pair, 2 * pair + 1):
                    out = banks[:, S + h, off:CH]
                    diagonal = kb >= BPC * qc
                    last = pe.matmul(out, kst[0:MROWS, at(g * (HG * T) + h * T + kb * P, P)],
                                     qst[0:MROWS, at(g * (HG * T) + h * T + qc * CH + off, CH - off)],
                                     start=True, stop=not diagonal)
                    if diagonal:
                        last = pe.matmul(out[:, 0:P], identb[:, :], mask_kq[:, :], start=False, stop=True)
                last.then_inc(s_ready, 1)

            def values(g, s):
                qc, kb, off = steps[s]
                if s == 0:
                    pe.wait_ge(vg_ready, g + 1)
                if kb == 0:
                    pe.wait_ge(o_copied, FREE + g * NC + qc)
                pe.wait_ge(exp_done, g * (2 * NS) + 2 * (s + 1))
                for h in range(HG):
                    last = pe.matmul(banks[32 * h:32 * h + 32, O, off:CH], vg[:, kb, h, :], prob[:, s % 3, h, off:CH],
                                     start=kb == 0, stop=kb == BPC * qc + BPC - 1)
                last.then_inc(pv_done, 1)

            def round_(g, plan):
                n, loop = 0, g
                for s, slots in enumerate(plan):
                    g = fresh(pe, loop, NG - 2)
                    if s == need_next and plan is not last_plan:
                        pe.wait_ge(stack_in, (g + 1) * PARTS_IN)
                    n = items(g, slots[0], n)
                    if s < NS:
                        scores(g, s, 0)
                    n = items(g, slots[1], n)
                    if s < NS:
                        scores(g, s, 1)
                    n = items(g, slots[2], n)
                    if s >= LAG:
                        values(g, s - LAG)
                    n = items(g, slots[3], n)

            pe.sem_inc(pv_done, FREE)
            pe.wait_ge(const_in, 16)
            pe.wait_ge(constb_in, 48)
            for n, (kind, _, what) in enumerate(before):
                if n >= len(RING):
                    pe.wait_ge(ring_read, n - len(RING) + 1)
                bank = RING[n % len(RING)]
                if kind == "max":
                    pe.wait_ge(first_in[tiles[what][0] // BPC], PARTS_IN)
                (max_tile(0, what, bank) if kind == "max" else turn_maxima(0, what, bank)).then_inc(ring_ready, 1)
            pe.wait_ge(first_in[NC - 1], PARTS_IN)
            pe.wait_ge(ones_ready, 1)
            with pe.Fori(0, NG - 1) as g:
                round_(g, plan)
            round_(NG - 1, last_plan)

        @block.scalar
        def _(act):
            def round_(loop):
                for s in range(NS):
                    g = fresh(act, loop, NG - 1)
                    qc, kb, off = steps[s]
                    act.wait_ge(pv_done, FREE + g * NS + max(s - 2, 0))
                    for pair in range(2):
                        act.wait_ge(s_ready, g * (2 * NS) + 2 * s + pair + 1)
                        heads = slice(2 * pair, 2 * pair + 2)
                        act.activation(prob[:, s % 3, heads, off:CH], banks[:, 2 * pair:2 * pair + 2, off:CH], ACT.Exp,
                                       scale=SCALE).then_inc(exp_done, 1)
                        if pair == 0 and s - 3 in last_step:
                            copy_output(g, last_step.index(s - 3))
                copy_output(g, NC - 1)

            def copy_output(g, qc):
                act.wait_ge(pv_done, FREE + g * NS + last_step[qc] + 1)
                act.activation(osb[:, qc % 2, :], banks[:, O, :], ACT.Copy).then_inc(o_copied, 1)

            act.sem_inc(o_copied, FREE)
            with act.Fori(0, NG) as g:
                round_(g)

        @block.vector
        def _(dve):
            def max_tile(r, u, bank):
                qb, c, width, h = tiles[u]
                n = h * NB + qb
                return dve.tensor_reduce(pmax[:, n, c:c + 1], banks[:, bank, 0:width], AX.X, ALU.max)

            def ends_chunk(u):
                return u == NM - 1 or tiles[u + 1][0] // BPC > tiles[u][0] // BPC

            def split_maxima(r, qc, reduced):
                chain = Chain(dve, chain_s, (r * NC + qc) * CHAIN)
                dve.wait_ge(ring_read, reduced)
                own = pmax[:, :, :].rearrange("p (h n) c -> p h n c", h=HG)[:, :, qc * BPC:(qc + 1) * BPC, :]
                chain.link(dve.tensor_reduce(nmax[:, :, :], own, AX.X, ALU.max, negate=True))
                chain.link(dve.tensor_copy(npart[:, 0, :, :], nmax[:, :, :]))
                chain.link(dve.tensor_tensor(nrem[:, :, :], nmax[:, :, :], npart[:, 0, :, :], ALU.subtract))
                chain.link(dve.tensor_copy(npart[:, 1, :, :], nrem[:, :, :]))
                assert chain.n == CHAIN
                dve.tensor_tensor(npart[:, 2, :, :], nrem[:, :, :], npart[:, 1, :, :], ALU.subtract).then_inc(nm_split, 1)

            def copy_maxima(r, qc, bank):
                if not isinstance(r, int) or r * NC + qc >= 2:
                    dve.wait_ge(nm_in[qc % 2], r * (NC // 2 * ROWS_IN) + qc // 2 * ROWS_IN)
                rowbank = banks[0:NTURN, bank, :].bitcast(BF16)
                return dve.tensor_copy(nrow[:, qc % 2, :], rowbank[:, 0:P])

            def group_values(g):
                dve.wait_ge(pv_done, FREE + g * NS)
                dve.tensor_copy(vg[:, :, :, 0:HD], keep["v"][:, :, at(g * (HG * HD), HG * HD)]
                                .rearrange("p b (h d) -> p b h d", h=HG)).then_inc(vg_ready, 1)

            def scale_output(g, qc, bank, n):
                dve.wait_ge(ring_read, FIRST + g * ITEMS + n)
                turned = banks[:, bank, :].rearrange("p (b h d) -> p b h d", b=BPC, h=HG)
                dve.reciprocal(rden[:, :, :], turned[:, :, :, HD]).then_inc(rden_ready, 1)
                dve.wait_ge(rden_ready, g * NC + qc + 1)
                return dve.tensor_tensor(keep["attn"][:, qc * BPC:(qc + 1) * BPC, at(g * (HG * HD), HG * HD)]
                                         .rearrange("p b (h d) -> p b h d", h=HG), turned[:, :, :, 0:HD],
                                         rden[:, :, :].unsqueeze(3).broadcast_to([P, BPC, HG, HD]), ALU.mult)

            def items(g, slot, n):
                for kind, ahead, what in slot:
                    dve.wait_ge(ring_ready, FIRST + g * ITEMS + n + 1)
                    bank = RING[(FIRST + n) % len(RING)]
                    last = (max_tile(g + ahead, what, bank) if kind == "max" else
                            copy_maxima(g + ahead, what, bank) if kind == "rows" else scale_output(g, what, bank, n))
                    last.then_inc(ring_read, 1)
                    n += 1
                    if kind == "max" and ends_chunk(what):
                        split_maxima(g + ahead, tiles[what][0] // BPC, FIRST + g * ITEMS + n)
                return n

            def round_(g, plan):
                n, loop = 0, g
                for s, slots in enumerate(plan):
                    g = fresh(dve, loop, NG - 2)
                    if s == 1:
                        group_values(g)
                    for slot in slots:
                        n = items(g, slot, n)

            dve.memset(pmax[:, :, :], NEGBIG).then_inc(pmax_ready, 1)
            dve.memset(nparts[:, :], 0.0).then_inc(pmax_ready, 1)
            dve.memset(vg[:, :, :, :], 0.0).then_inc(vg_zero, 1)
            dve.wait_ge(vg_zero, 1)
            dve.memset(vg[:, :, :, HD:VW], 1.0).then_inc(vg_zero, 1)
            dve.wait_ge(vg_zero, 2)
            dve.wait_ge(pmax_ready, 2)
            for n, (kind, _, what) in enumerate(before):
                dve.wait_ge(ring_ready, n + 1)
                bank = RING[n % len(RING)]
                (max_tile(0, what, bank) if kind == "max" else copy_maxima(0, what, bank)).then_inc(ring_read, 1)
                if kind == "max" and ends_chunk(what):
                    split_maxima(0, tiles[what][0] // BPC, n + 1)
            with dve.Fori(0, NG - 1) as g:
                round_(g, plan)
            round_(NG - 1, last_plan)


def phase_projection(nc, io, keep):
    x1, cn, cT, ch, cl = (keep[n] for n in ("x1", "cn", "cT", "ch", "cl"))
    with Phase(nc, "proj") as ph:
        w, bias, ident = ph.sb("w", [P, KD, D]), ph.sb("bias", [P, D]), ph.sb("ident", [P, P])
        wh, wl = ph.sb("wh", [P, KD, D], F32R), ph.sb("wl", [P, KD, D], F32R)
        ah, al = ph.sb("ah", [P, KD, T], F32R), ph.sb("al", [P, KD, T], F32R)
        banks = ph.ps("banks", [P, 8, CH])
        ln = LayerNorm(ph, "ln")
        turn_a = Turn(ph, "a", (banks[:, 0, :], banks[:, 1, :]), ident)
        turn_c = Turn(ph, "c", (banks[:, 2, :], banks[:, 3, :]), ident)
        w_in, x_in, wh_done, w_split, xb_done, o_ready, o_added = map(ph.sem, (
            "w_in", "x_in", "wh_done", "w_split", "xb_done", "o_ready", "o_added"))
        block = ph.stack.enter_context(nc.Block())

        @block.sync
        def _(sp):
            sp.dma_start(ident[:, :], io["ident"]).then_inc(w_in, 16)
            sp.dma_start(w[:, :, :], io["woutT"].rearrange("(k p) f -> p k f", p=P)).then_inc(w_in, 16)
            sp.dma_start(bias[:, :], io["b_out"].partition_broadcast(P)).then_inc(x_in, 16)
            sp.dma_start(x1[:, :, :], io["x"].rearrange("(b p) d -> p b d", p=P)).then_inc(x_in, 16)

        @block.gpsimd
        def _(pool):
            pool.wait_ge(x_in, 32)
            for b in range(NB):
                pool.tensor_tensor(x1[:, b, :], x1[:, b, :], bias[:, :], ALU.add).then_inc(xb_done, 1)

        @block.vector
        def _(dve):
            dve.wait_ge(w_in, 32)
            dve.tensor_copy(wh[:, :, :], w[:, :, :]).then_inc(wh_done, 1)
            dve.wait_ge(wh_done, 1)
            dve.tensor_tensor(wl[:, :, :], w[:, :, :], wh[:, :, :], ALU.subtract).then_inc(w_split, 1)

            def low_a(c):
                for k in range(KD):
                    turn_a.low(dve, ah[:, k, tokens(c)], al[:, k, tokens(c)], c, k)

            def low_c(c):
                for k in range(KD):
                    turn_c.low(dve, ch[:, k, tokens(c)], cl[:, k, tokens(c)], c, k)

            low_a(0)
            low_a(1)
            for c in range(NC):
                for b in range(c * BPC, (c + 1) * BPC):
                    dve.wait_ge(o_ready, b + 1)
                    dve.wait_ge(xb_done, b + 1)
                    dve.tensor_tensor(x1[:, b, :], banks[:, 4 + b % 2, 0:D], x1[:, b, :], ALU.add).then_inc(o_added, 1)
                dve.wait_ge(o_added, (c + 1) * BPC)
                ln.collect(dve, x1, c)
                if c + 2 < NC:
                    low_a(c + 2)
                ln.apply(dve, x1, cn, c)
                if c >= 1:
                    low_c(c - 1)
            low_c(NC - 1)

        @block.scalar
        def _(act):
            def high_a(c):
                for k in range(KD):
                    turn_a.high(act, ah[:, k, tokens(c)], c, k)

            def high_c(c):
                for k in range(KD):
                    turn_c.high(act, ch[:, k, tokens(c)], c, k, plain=cT[:, k, tokens(c)])

            high_a(0)
            high_a(1)
            for c in range(NC):
                if c + 2 < NC:
                    high_a(c + 2)
                ln.root(act, c)
                if c >= 1:
                    high_c(c - 1)
            high_c(NC - 1)

        @block.tensor
        def _(pe):
            def turn_attention(c):
                for k in range(KD):
                    turn_a.turn(pe, keep["attn"], c, k)

            def turn_norm(c):
                for k in range(KD):
                    turn_c.turn(pe, cn, c, k, ready=ln.done)

            def project(c):
                pe.wait_ge(turn_a.low_done, (c + 1) * KD)
                for b in range(c * BPC, (c + 1) * BPC):
                    if b >= 2:
                        pe.wait_ge(o_added, b - 1)
                    tok = slice(b * P, (b + 1) * P)
                    split_product(pe, banks[:, 4 + b % 2, 0:D], [(ah[:, k, tok], al[:, k, tok], wh[:, k, :], wl[:, k, :])
                                                                 for k in range(KD)]).then_inc(o_ready, 1)

            pe.wait_ge(w_in, 32)
            turn_attention(0)
            turn_attention(1)
            pe.wait_ge(w_split, 1)
            for c in range(NC):
                project(c)
                if c + 2 < NC:
                    turn_attention(c + 2)
                if c >= 1:
                    turn_norm(c - 1)
            turn_norm(NC - 1)


def phase_cross(nc, io, keep):
    cT = keep["cT"]
    with Phase(nc, "cross") as ph:
        qT, q = ph.sb("qT", [P, KD, LPAD]), ph.sb("q", [P, LB, D])
        qTh, qTl = ph.sb("qTh", [P, KD, LPAD], F32R), ph.sb("qTl", [P, KD, LPAD], F32R)
        qh, ql = ph.sb("qh", [P, LB, D], F32R), ph.sb("ql", [P, LB, D], F32R)
        wcol, ident = ph.sb("wcol", [P, 2, KD]), ph.sb("ident", [P, P])
        cw, cwh, cwl = ph.sb("cw", [P, KD, P]), ph.sb("cwh", [P, KD, P], F32R), ph.sb("cwl", [P, KD, P], F32R)
        prob, total, rtotal = ph.sb("prob", [P, L]), ph.sb("total", [P, NB]), ph.sb("rtotal", [P, NB])
        pTh, pTl = ph.sb("pTh", [P, LB, P], F32R), ph.sb("pTl", [P, LB, P], F32R)
        banks = ph.ps("banks", [P, 8, CH])
        S, R, O = 0, 4, 6
        GROUPS = [list(range(t, min(t + 4, LB))) for t in range(0, LB, 4)]
        NGR = len(GROUPS)
        rows = lambda t: P if t < LB - 1 else LLAST
        in_, q_in, split_s, split_done, cw_s, cw_ready, s_ready, nm_ready, exp_done, turned, high_done, low_done, \
            o_ready, r_ready, o_done, qT_split = map(ph.sem, (
                "in", "q_in", "split_s", "split_done", "cw_s", "cw_ready", "s_ready", "nm_ready", "exp_done", "turned",
                "high_done", "low_done", "o_ready", "r_ready", "o_done", "qT_split"))
        block = ph.stack.enter_context(nc.Block())

        @block.sync
        def _(sp):
            sp.dma_start(wcol[:, 0, :], io["w_cq"]).then_inc(in_, 16)
            sp.dma_start(wcol[:, 1, :], io["w_q"]).then_inc(in_, 16)
            sp.dma_start(ident[:, :], io["ident"]).then_inc(in_, 16)
            sp.dma_start(qT[:, :, :], io["ctxT"].rearrange("(k p) l -> p k l", p=P)).then_inc(in_, 16)
            sp.dma_start(q[:, 0:LB - 1, :], io["ctx"][0:(LB - 1) * P, :].rearrange("(b p) d -> p b d", p=P)).then_inc(q_in, 16)
            sp.dma_start(q[0:LLAST, LB - 1, :], io["ctx"][(LB - 1) * P:L, :]).then_inc(q_in, 16)

        @block.gpsimd
        def _(pool):
            pool.wait_ge(q_in, 32)
            pool.tensor_copy(qh[:, 0:LB - 1, :], q[:, 0:LB - 1, :]).then_inc(split_s, 1)
            pool.tensor_copy(qh[0:LLAST, LB - 1, :], q[0:LLAST, LB - 1, :]).then_inc(split_s, 1)
            pool.wait_ge(split_s, 2)
            pool.tensor_tensor(ql[:, 0:LB - 1, :], q[:, 0:LB - 1, :], qh[:, 0:LB - 1, :], ALU.subtract).then_inc(split_done, 1)
            pool.tensor_tensor(ql[0:LLAST, LB - 1, :], q[0:LLAST, LB - 1, :], qh[0:LLAST, LB - 1, :],
                               ALU.subtract).then_inc(split_done, 1)

        @block.vector
        def _(dve):
            def weigh(i, first=False):
                for k in range(KD):
                    dve.tensor_scalar(cw[:, k, :], cT[:, k, at(i * P, P)], wcol[:, 0, k:k + 1], wcol[:, 1, k:k + 1],
                                      ALU.mult, ALU.add).then_inc(cw_s, 1)
                dve.wait_ge(cw_s, i * 3 + 2)
                dve.tensor_copy(cwh[:, :, :], cw[:, :, :]).then_inc(cw_s, 1)
                dve.wait_ge(cw_s, i * 3 + 3)
                dve.tensor_tensor(cwl[:, :, :], cw[:, :, :], cwh[:, :, :], ALU.subtract).then_inc(cw_ready, 1)

            def maximum(i):
                dve.wait_ge(s_ready, i + 1)
                dve.tensor_reduce(keep["nmax"][:, at(i)], banks[:, S:S + 4, :].rearrange("p b c -> p (b c)")[:, 0:L],
                                  AX.X, ALU.max, negate=True).then_inc(nm_ready, 1)

            def low(i):
                for g, ts in enumerate(GROUPS):
                    dve.wait_ge(high_done, i * NGR + g + 1)
                    r = rows(ts[-1])
                    dve.tensor_tensor(pTl[0:r, ts[0]:ts[-1] + 1, :], banks[0:r, R + g % 2, 0:len(ts) * P]
                                      .rearrange("p (t c) -> p t c", c=P), pTh[0:r, ts[0]:ts[-1] + 1, :],
                                      ALU.subtract).then_inc(low_done, 1)

            def normalise(i):
                dve.reciprocal(rtotal[:, at(i)], total[:, at(i)]).then_inc(r_ready, 1)
                dve.wait_ge(r_ready, i + 1)
                dve.wait_ge(o_ready, i + 1)
                dve.tensor_scalar(keep["c2q"][:, at(i), :].rearrange("p a d -> p (a d)"), banks[:, O, 0:D],
                                  rtotal[:, at(i)], None, ALU.mult).then_inc(o_done, 1)

            dve.sem_inc(o_done, FREE)
            dve.wait_ge(in_, 64)
            weigh(0)
            dve.tensor_copy(qTh[:, :, :], qT[:, :, :]).then_inc(qT_split, 1)
            dve.wait_ge(qT_split, 1)
            dve.tensor_tensor(qTl[:, :, :], qT[:, :, :], qTh[:, :, :], ALU.subtract).then_inc(qT_split, 1)
            maximum(0)
            weigh(1)
            with dve.Fori(1, NB - 1) as i:
                low(i - 1)
                maximum(i)
                weigh(i + 1)
                normalise(i - 1)
            low(NB - 2)
            maximum(NB - 1)
            normalise(NB - 2)
            low(NB - 1)
            normalise(NB - 1)

        @block.scalar
        def _(act):
            def exponent(i):
                act.wait_ge(nm_ready, i + 1)
                act.activation(prob[:, :], banks[:, S:S + 4, :].rearrange("p b c -> p (b c)")[:, 0:L], ACT.Exp,
                               bias=keep["nmax"][:, at(i)], accum_out=total[:, at(i)]).then_inc(exp_done, 1)

            def high(i):
                for g, ts in enumerate(GROUPS):
                    act.wait_ge(turned, i * NGR + g + 1)
                    r = rows(ts[-1])
                    act.activation(pTh[0:r, ts[0]:ts[-1] + 1, :], banks[0:r, R + g % 2, 0:len(ts) * P]
                                   .rearrange("p (t c) -> p t c", c=P), ACT.Copy).then_inc(high_done, 1)

            exponent(0)
            with act.Fori(1, NB) as i:
                high(i - 1)
                exponent(i)
            high(NB - 1)

        @block.tensor
        def _(pe):
            CHUNKS = [(a, min(a + CH, LPAD)) for a in range(0, LPAD, CH)]

            def score(i, chunk, first=False):
                a, b = CHUNKS[chunk]
                if chunk == 0:
                    pe.wait_ge(cw_ready, i + 1)
                    if not first:
                        pe.wait_ge(exp_done, i)
                last = split_product(pe, banks[:, S + chunk, 0:b - a],
                                     [(cwh[:, k, :], cwl[:, k, :], qTh[:, k, a:b], qTl[:, k, a:b]) for k in range(KD)])
                if chunk == len(CHUNKS) - 1:
                    last.then_inc(s_ready, 1)

            def turn(i, g, first=False):
                if g == 0:
                    pe.wait_ge(exp_done, i + 1)
                if g >= 2:
                    pe.wait_ge(low_done, i * NGR + g - 1)
                for n, t in enumerate(GROUPS[g]):
                    last = pe.transpose(banks[0:rows(t), R + g % 2, n * P:(n + 1) * P], prob[:, t * P:t * P + rows(t)],
                                        ident[:, :])
                last.then_inc(turned, 1)

            def attend(i):
                pe.wait_ge(low_done, (i + 1) * NGR)
                pe.wait_ge(o_done, FREE + i)
                split_product(pe, banks[:, O, 0:D], [(pTh[0:rows(t), t, :], pTl[0:rows(t), t, :], qh[0:rows(t), t, :],
                                                      ql[0:rows(t), t, :]) for t in range(LB)]).then_inc(o_ready, 1)

            pe.wait_ge(in_, 64)
            pe.wait_ge(qT_split, 2)
            for chunk in range(4):
                score(0, chunk, first=True)
            pe.wait_ge(split_done, 2)
            with pe.Fori(1, NB) as i:
                turn(i - 1, 0)
                turn(i - 1, 1)
                score(i, 0)
                turn(i - 1, 2)
                score(i, 1)
                turn(i - 1, 3)
                score(i, 2)
                score(i, 3)
                attend(i - 1)
            for g in range(NGR):
                turn(NB - 1, g)
            attend(NB - 1)


def phase_fuse(nc, io, keep):
    x1, cn, cT, ch, cl, c2q = (keep[n] for n in ("x1", "cn", "cT", "ch", "cl", "c2q"))
    with Phase(nc, "fuse") as ph:
        ident, ones = ph.sb("ident", [P, P]), ph.sb("ones", [P, P])
        w = ph.sb("w", [P, 4 * KD, D])
        wh, wl = ph.sb("wh", [P, 3 * KD, D], F32R), ph.sb("wl", [P, 3 * KD, D], F32R)
        bias, wc, bs = ph.sb("bias", [P, D]), ph.sb("wc", [P, D]), ph.sb("bs", [P, 3])
        junk, rowc = ph.sb("junk", [P, D]), ph.sb("rowc", [P, NB])
        smax, e = ph.sb("smax", [P, NB]), ph.sb("e", [P, NB])
        one = ph.sb("one", [P, 8])
        q2c, q2col = ph.sb("q2c", [1, D]), ph.sb("q2col", [P, KD])
        qTh, qTl = ph.sb("qTh", [P, 2, KD, CH], F32R), ph.sb("qTl", [P, 2, KD, CH], F32R)
        mul = ph.sb("mul", [P, 2, CH])
        mh, ml = ph.sb("mh", [P, 2, KD, CH], F32R), ph.sb("ml", [P, 2, KD, CH], F32R)
        banks = ph.ps("banks", [P, 8, CH])
        ln = LayerNorm(ph, "ln")
        turn_q = Turn(ph, "q", (banks[:, 0, :], banks[:, 1, :]), ident)
        turn_n = Turn(ph, "n", (banks[:, 2, :], banks[:, 3, :]), ident)
        in_, chain_s, w_split, xb_done, mul_done, mh_done, ml_done, z_ready, z_added, sm, sm_e, sm_pe, w_fused = map(ph.sem, (
            "in", "dve_chain", "w_split", "xb_done", "mul_done", "mh_done", "ml_done", "z_ready", "z_added", "sm",
            "sm_e", "sm_pe", "w_fused"))
        SM = 6
        block = ph.stack.enter_context(nc.Block())

        @block.sync
        def _(sp):
            sp.dma_start(wc[:, :], io["w_c"].partition_broadcast(P)).then_inc(in_, 16)
            for n, name in enumerate(("b_c", "b_q", "b_cq")):
                sp.dma_start(bs[:, n:n + 1], io[name].partition_broadcast(P)).then_inc(in_, 16)
            sp.dma_start(ident[:, :], io["ident"]).then_inc(in_, 16)
            sp.dma_start(ones[:, :], io["ones"]).then_inc(in_, 16)
            sp.dma_start(w[:, :, :], io["wlT"].rearrange("(k p) f -> p k f", p=P)).then_inc(in_, 16)
            sp.dma_start(bias[:, :], io["b_l"].partition_broadcast(P)).then_inc(in_, 16)

        @block.gpsimd
        def _(pool):
            pool.wait_ge(in_, 128)
            for b in range(NB):
                pool.tensor_tensor(x1[:, b, :], x1[:, b, :], bias[:, :], ALU.add).then_inc(xb_done, 1)

        @block.vector
        def _(dve):
            chain = Chain(dve, chain_s)
            dve.wait_ge(in_, 128)
            for b in range(NB):
                if b:
                    chain.wait()
                chain.then(dve.tensor_tensor_reduce(junk[:, :], cn[:, b, :], wc[:, :], 1.0, 0.0, ALU.mult, ALU.add,
                                                    rowc[:, b:b + 1]))
            chain.wait()
            chain.link(dve.tensor_tensor(smax[:, :], rowc[:, :], keep["nmax"][:, :], ALU.subtract))
            for n in range(3):
                chain.link(dve.tensor_scalar(smax[:, :], smax[:, :], bs[:, n:n + 1], None, ALU.add))
            dve.tensor_reduce(one[:, 0:1], smax[:, :], AX.X, ALU.max).then_inc(sm, 1)
            low_parts = slice(KD, 3 * KD)
            chain.link(dve.tensor_copy(wh[:, low_parts, :], w[:, low_parts, :]))
            dve.tensor_tensor(wl[:, low_parts, :], w[:, low_parts, :], wh[:, low_parts, :], ALU.subtract).then_inc(w_split, 1)
            dve.wait_ge(sm_pe, 1)
            dve.tensor_reduce(one[0:1, 1:2], banks[0:1, SM, 0:P], AX.X, ALU.max, negate=True).then_inc(sm, 1)
            dve.wait_ge(sm_pe, 2)
            dve.tensor_copy(one[:, 2:3], banks[:, SM, P:P + 1]).then_inc(sm, 1)
            dve.wait_ge(sm_pe, 3)
            chain.link(dve.reciprocal(one[:, 4:5], banks[:, SM, P + 2:P + 3]))
            dve.wait_ge(sm_pe, 4)
            dve.tensor_scalar(q2c[0:1, :], banks[0:1, SM + 1, 0:D], one[0:1, 4:5], None, ALU.mult).then_inc(sm, 1)
            dve.wait_ge(sm_pe, 5)
            chain.link(dve.tensor_copy(q2col[:, :], banks[:, SM, 256:256 + KD]))
            for k in range(KD):
                chain.then(dve.scalar_tensor_tensor(out=w[:, k, :], in0=w[:, 3 * KD + k, :], scalar=q2col[:, k:k + 1],
                                                    in1=w[:, k, :], op0=ALU.mult, op1=ALU.add))
            chain.wait()
            chain.link(dve.tensor_copy(wh[:, 0:KD, :], w[:, 0:KD, :]))
            dve.tensor_tensor(wl[:, 0:KD, :], w[:, 0:KD, :], wh[:, 0:KD, :], ALU.subtract).then_inc(w_fused, 1)

            def low_q(c):
                for k in range(KD):
                    n = c * KD + k
                    dve.wait_ge(turn_q.high_done, n + 1)
                    if n >= 2:
                        dve.wait_ge(ml_done, n - 1)
                    dve.tensor_tensor(mul[:, k, :], turn_q.banks[n % 2], cT[:, k, tokens(c)], ALU.mult).then_inc(mul_done, 1)
                    turn_q.low(dve, qTh[:, c % 2, k, :], qTl[:, c % 2, k, :], c, k)
                for k in range(KD):
                    dve.wait_ge(mh_done, c * KD + k + 1)
                    dve.tensor_tensor(ml[:, c % 2, k, :], mul[:, k, :], mh[:, c % 2, k, :], ALU.subtract).then_inc(ml_done, 1)

            def low_n(c):
                for k in range(KD):
                    turn_n.low(dve, keep["nh"][:, k, tokens(c)], keep["nl"][:, k, tokens(c)], c, k)

            low_q(0)
            for c in range(NC):
                if c + 1 < NC:
                    low_q(c + 1)
                for b in range(c * BPC, (c + 1) * BPC):
                    dve.wait_ge(z_ready, b + 1)
                    dve.wait_ge(xb_done, b + 1)
                    dve.tensor_tensor(x1[:, b, :], banks[:, 4 + b % 2, 0:D], x1[:, b, :], ALU.add).then_inc(z_added, 1)
                dve.wait_ge(z_added, (c + 1) * BPC)
                ln.collect(dve, x1, c)
                ln.apply(dve, x1, cn, c)
                if c >= 1:
                    low_n(c - 1)
            low_n(NC - 1)

        @block.scalar
        def _(act):
            act.wait_ge(sm, 3)
            act.activation(e[:, :], smax[:, :], ACT.Exp, bias=one[:, 2:3], accum_out=one[:, 3:4]).then_inc(sm_e, 1)

            def high_q(c):
                for k in range(KD):
                    if c >= 2:
                        act.wait_ge(z_ready, (c - 1) * BPC)
                    turn_q.high(act, qTh[:, c % 2, k, :], c, k)
                for k in range(KD):
                    act.wait_ge(mul_done, c * KD + k + 1)
                    act.activation(mh[:, c % 2, k, :], mul[:, k, :], ACT.Copy).then_inc(mh_done, 1)

            def high_n(c):
                for k in range(KD):
                    turn_n.high(act, keep["nh"][:, k, tokens(c)], c, k)

            high_q(0)
            for c in range(NC):
                if c + 1 < NC:
                    high_q(c + 1)
                ln.root(act, c)
                if c >= 1:
                    high_n(c - 1)
            high_n(NC - 1)

        @block.tensor
        def _(pe):
            pe.wait_ge(in_, 128)
            pe.wait_ge(sm, 1)
            pe.transpose(banks[0:1, SM, 0:P], one[:, 0:1], ident[:, :]).then_inc(sm_pe, 1)
            pe.wait_ge(sm, 2)
            pe.matmul(banks[:, SM, P:P + 1], ones[0:1, :], one[0:1, 1:2], start=True, stop=True).then_inc(sm_pe, 1)
            pe.wait_ge(sm_e, 1)
            pe.matmul(banks[:, SM, P + 2:P + 3], ones[:, :], one[:, 3:4], start=True, stop=True).then_inc(sm_pe, 1)
            for b in range(NB):
                last = pe.matmul(banks[0:1, SM + 1, 0:D], e[:, b:b + 1], cn[:, b, :], start=b == 0, stop=b == NB - 1)
            last.then_inc(sm_pe, 1)
            pe.wait_ge(sm, 4)
            for k in range(KD):
                last = pe.matmul(banks[:, SM, 256 + k:257 + k], q2c[0:1, k * P:(k + 1) * P], ones[0:1, 0:1],
                                 start=True, stop=True)
            last.then_inc(sm_pe, 1)

            def turn_attended(c):
                for k in range(KD):
                    turn_q.turn(pe, c2q, c, k)

            def turn_norm(c):
                for k in range(KD):
                    turn_n.turn(pe, cn, c, k, ready=ln.done)

            def fuse(c):
                pe.wait_ge(ml_done, (c + 1) * KD)
                pe.wait_ge(turn_q.low_done, (c + 1) * KD)
                if c == 0:
                    pe.wait_ge(w_split, 1)
                    pe.wait_ge(w_fused, 1)
                for b in range(c * BPC, (c + 1) * BPC):
                    if b >= 2:
                        pe.wait_ge(z_added, b - 1)
                    tok, own = slice(b * P, (b + 1) * P), slice((b % BPC) * P, (b % BPC + 1) * P)
                    terms = [(ch[:, k, tok], cl[:, k, tok], wh[:, k, :], wl[:, k, :]) for k in range(KD)]
                    terms += [(qTh[:, c % 2, k, own], qTl[:, c % 2, k, own], wh[:, KD + k, :], wl[:, KD + k, :])
                              for k in range(KD)]
                    terms += [(mh[:, c % 2, k, own], ml[:, c % 2, k, own], wh[:, 2 * KD + k, :], wl[:, 2 * KD + k, :])
                              for k in range(KD)]
                    split_product(pe, banks[:, 4 + b % 2, 0:D], terms).then_inc(z_ready, 1)

            turn_attended(0)
            for c in range(NC):
                if c + 1 < NC:
                    turn_attended(c + 1)
                fuse(c)
                if c >= 1:
                    turn_norm(c - 1)
            turn_norm(NC - 1)


def phase_route(nc, io, keep):
    nh, nl, stack, wT = (keep[n] for n in ("nh", "nl", "stack", "wT"))
    with Phase(nc, "route") as ph:
        ident, identb = ph.sb("ident", [P, P]), ph.sb("identb", [P, P], BF16)
        w, wh, wl = ph.sb("w", [P, KD, D]), ph.sb("wh", [P, KD, D], F32R), ph.sb("wl", [P, KD, D], F32R)
        HE = FH * NE
        gw, gh, gl = ph.sb("gw", [P, HE // 2]), ph.sb("gh", [P, HE // 2], F32R), ph.sb("gl", [P, HE // 2], F32R)
        bcol, iota = ph.sb("bcol", [P, KD]), ph.sb("iota", [P, NE])
        th, tl = ph.sb("th", [P, 2, CH], F32R), ph.sb("tl", [P, 2, CH], F32R)
        G = BPC * FH
        row = {n: ph.sb(n, [P, G, NE]) for n in ("shifted", "expd", "prob", "eq", "cand", "first", "rest", "second", "wgt", "rem")}
        col = {n: ph.sb(n, [P, G]) for n in ("max", "sum", "rsum", "top", "pick")}
        parts = ph.sb("parts", [P, BPC, FH // 2, 3, 2 * NE], BF16)
        banks = ph.ps("banks", [P, 8, CH])
        X, GB, TB = 0, 2, 4
        in_, chain_s, w_split, h_ready, th_done, tl_done, stacked0, stacked1, g_ready, shifted, expd, w1_done, rem_done, \
            w2_done, w3_done, turned, copied, identb_in = map(ph.sem, (
                "in", "dve_chain", "w_split", "h_ready", "th_done", "tl_done", "stacked0", "stacked1", "g_ready", "shifted",
                "expd", "w1_done", "rem_done", "w2_done", "w3_done", "turned", "copied", "identb_in"))
        stacked = (stacked0, stacked1)
        block = ph.stack.enter_context(nc.Block())

        @block.sync
        def _(sp):
            for dst, name in ((ident, "ident"), (gw, "gate"), (bcol, "bm"), (iota, "iota")):
                sp.dma_start(dst[:, :], io[name]).then_inc(in_, 16)
            sp.dma_start(w[:, :, :], io["wm"].rearrange("(k p) f -> p k f", p=P)).then_inc(in_, 16)
            for n in range(KD * NC):
                c, k = n // KD, n % KD
                sp.wait_ge(th_done, n + 1)
                sp.wait_ge(tl_done, n + 1)
                for rows, src in enumerate((th, tl, th)):
                    for h in range(4):
                        sp.dma_start(stack[rows * FD:(rows + 1) * FD, n, h, :].bitcast(F32),
                                     src[h * FD:(h + 1) * FD, n % 2, :].bitcast(F32))\
                            .then_inc(stacked[n % 2], 16)
            for s in stacked:
                sp.wait_ge(s, 12 * 16 * KD * NC // 2)

        @block.gpsimd
        def _(pool):
            pool.dma_start(identb[:, :], io["ident"]).then_inc(identb_in, 16)

        @block.vector
        def _(dve):
            chain = Chain(dve, chain_s)
            dve.wait_ge(in_, 80)
            chain.then(dve.tensor_copy(wh[:, :, :], w[:, :, :]))
            chain.link(dve.tensor_copy(gh[:, :], gw[:, :]))
            dve.tensor_tensor(wl[:, :, :], w[:, :, :], wh[:, :, :], ALU.subtract).then_inc(w_split, 1)
            dve.tensor_tensor(gl[:, :], gw[:, :], gh[:, :], ALU.subtract).then_inc(w_split, 1)

            def spread(a):
                return a[:, :].unsqueeze(2).broadcast_to([P, G, NE])

            def pick(probs, out):
                chain.link(dve.tensor_reduce(col["top"][:, :], probs[:, :, :], AX.X, ALU.max))
                chain.link(dve.tensor_tensor(row["eq"][:, :, :], probs[:, :, :], spread(col["top"]), ALU.is_equal))
                chain.link(dve.tensor_tensor(row["cand"][:, :, :], row["eq"][:, :, :],
                                             iota[:, :].unsqueeze(1).broadcast_to([P, G, NE]), ALU.mult))
                chain.link(dve.tensor_reduce(col["pick"][:, :], row["cand"][:, :, :], AX.X, ALU.max))
                chain.link(dve.tensor_tensor(out[:, :, :], row["cand"][:, :, :], spread(col["pick"]), ALU.is_equal))

            def pair(n):
                dve.wait_ge(th_done, n + 1)
                dve.scalar_tensor_tensor(out=tl[:, n % 2, :], in0=banks[:, X + n % 2, :], scalar=bcol[:, n % KD:n % KD + 1],
                                         in1=th[:, n % 2, :], op0=ALU.add, op1=ALU.subtract).then_inc(tl_done, 1)

            for c in range(NC):
                for k in range(KD):
                    pair(c * KD + k)
                gates = banks[:, GB + c % 2, :].rearrange("p (g e) -> p g e", e=NE)
                dve.wait_ge(g_ready, c + 1)
                chain.link(dve.tensor_reduce(col["max"][:, :], gates, AX.X, ALU.max))
                dve.tensor_tensor(row["shifted"][:, :, :], gates, spread(col["max"]), ALU.subtract).then_inc(shifted, 1)
                dve.wait_ge(expd, c + 1)
                chain.link(dve.tensor_reduce(col["sum"][:, :], row["expd"][:, :, :], AX.X, ALU.add))
                chain.link(dve.reciprocal(col["rsum"][:, :], col["sum"][:, :]))
                chain.link(dve.tensor_tensor(row["prob"][:, :, :], row["expd"][:, :, :], spread(col["rsum"]), ALU.mult))
                pick(row["prob"], row["first"])
                chain.link(dve.scalar_tensor_tensor(out=row["rest"][:, :, :], in0=row["first"][:, :, :], scalar=-2.0,
                                                    in1=row["prob"][:, :, :], op0=ALU.mult, op1=ALU.add))
                pick(row["rest"], row["second"])
                chain.link(dve.tensor_tensor(row["first"][:, :, :], row["first"][:, :, :], row["second"][:, :, :], ALU.add))
                if c >= 1:
                    dve.wait_ge(rem_done, c)
                dve.tensor_tensor(row["wgt"][:, :, :], row["first"][:, :, :], row["prob"][:, :, :], ALU.mult).then_inc(w1_done, 1)
                dve.wait_ge(w2_done, 2 * c + 1)
                wide = lambda n: row[n][:, :, :].rearrange("p (b q h) e -> p b q (h e)", b=BPC, q=FH // 2)
                dve.tensor_tensor(wide("rem"), wide("wgt"), parts[:, :, :, 0, :], ALU.subtract).then_inc(rem_done, 1)
                dve.wait_ge(w2_done, 2 * c + 2)
                dve.tensor_tensor(parts[:, :, :, 2, :], wide("rem"), parts[:, :, :, 1, :], ALU.subtract).then_inc(w3_done, 1)

        @block.scalar
        def _(act):
            act.wait_ge(in_, 80)
            for c in range(NC):
                for k in range(KD):
                    n = c * KD + k
                    act.wait_ge(h_ready, n + 1)
                    if n >= 2:
                        act.wait_ge(stacked[n % 2], 12 * 16 * (n // 2))
                        act.wait_ge(g_ready, (n - 2) // KD + 1)
                    act.activation(th[:, n % 2, :], banks[:, X + n % 2, :], ACT.Identity, bias=bcol[:, k:k + 1]).then_inc(th_done, 1)
                act.wait_ge(shifted, c + 1)
                act.activation(row["expd"][:, :, :], row["shifted"][:, :, :], ACT.Exp).then_inc(expd, 1)
                wide = lambda n: row[n][:, :, :].rearrange("p (b q h) e -> p b q (h e)", b=BPC, q=FH // 2)
                act.wait_ge(w1_done, c + 1)
                if c >= 1:
                    act.wait_ge(turned, c)
                act.activation(parts[:, :, :, 0, :], wide("wgt"), ACT.Copy).then_inc(w2_done, 1)
                act.wait_ge(rem_done, c + 1)
                act.activation(parts[:, :, :, 1, :], wide("rem"), ACT.Copy).then_inc(w2_done, 1)
                act.wait_ge(turned, c + 1)
                for q in range(FH // 2):
                    src = banks[0:96, TB + q // 2, :].bitcast(BF16)[:, (q % 2) * CH:(q % 2 + 1) * CH]
                    act.activation(wT[:, c * 2 + q // 2, q % 2, :], src, ACT.Copy).then_inc(copied, 1)

        @block.tensor
        def _(pe):
            pe.wait_ge(in_, 80)
            pe.wait_ge(identb_in, 16)
            pe.wait_ge(w_split, 2)

            def product(c):
                for k in range(KD):
                    n = c * KD + k
                    if n >= 2:
                        pe.wait_ge(tl_done, n - 1)
                    feat = slice(k * P, (k + 1) * P)
                    split_product(pe, banks[:, X + n % 2, :], [(wh[:, j, feat], wl[:, j, feat], nh[:, j, tokens(c)],
                                                                nl[:, j, tokens(c)]) for j in range(KD)]).then_inc(h_ready, 1)

            def gate(c):
                pe.wait_ge(tl_done, (c + 1) * KD)
                for b in range(BPC):
                    for k in range(KD):
                        tok, at_ = slice(b * P, (b + 1) * P), b * P + k * (HE // 2)
                        last = split_product(pe, banks[:, GB + c % 2, at_:at_ + HE // 2],
                                             [(th[:, k, tok], tl[:, k, tok], gh[:, :], gl[:, :])])
                last.then_inc(g_ready, 1)

            def turn(c):
                pe.wait_ge(w3_done, c + 1)
                if c >= 1:
                    pe.wait_ge(copied, c * (FH // 2))
                for q in range(FH // 2):
                    dst = banks[0:96, TB + q // 2, :].bitcast(BF16)
                    for b in range(BPC):
                        last = pe.transpose(dst[:, (q % 2) * CH + b * P:(q % 2) * CH + (b + 1) * P],
                                            parts[:, b, q, :, :].rearrange("p a e -> p (a e)"), identb[:, :])
                last.then_inc(turned, 1)

            product(0)
            for c in range(NC):
                gate(c)
                if c + 1 < NC:
                    product(c + 1)
                turn(c)


def phase_experts(nc, io, keep):
    nh, nl, stack, wT, x2 = (keep[n] for n in ("nh", "nl", "stack", "wT", "x1"))
    acc = keep["v"][:, 0:8, :].rearrange("p (q h c) d -> p q h (c d)", q=2, h=2)
    prod = keep["v"][:, 8:16, :].rearrange("p (q h c) d -> p q h (c d)", q=2, h=2)
    hid0 = keep["attn"][:, :, :].rearrange("p (e h c) d -> p e h (c d)", e=EG, h=2)
    high, low = (a[:, :, :].rearrange("p k t -> p (k t)") for a in (nh, nl))
    R = KD * NC
    NST = 2 * NEG
    NX = NST * EG
    with Phase(nc, "ffn") as ph:
        w1 = ph.sb("w1", [96, NE, EI], F32R)
        w2 = ph.sb("w2", [P, NE, FD])
        b1, b2 = ph.sb("b1", [P, NE]), ph.sb("b2", [P, NEG])
        spread_w = ph.sb("spread_w", [96, 2 * NEG, P], BF16)
        sum_w = ph.sb("sum_w", [P, FD])
        wo, woh, wol = ph.sb("wo", [P, KD, D]), ph.sb("woh", [P, KD, D], F32R), ph.sb("wol", [P, KD, D], F32R)
        bias = ph.sb("bias", [P, D])
        hid1 = ph.sb("hid1", [P, EG, 2, CH])
        hid = (hid0, hid1)
        wide = ph.sb("wide", [P, 2, 2, CH])
        w1f = wide[0:96, :, :, :].rearrange("p a h c -> p (a h c)")
        banks = ph.ps("banks", [P, 8, CH])
        combined = ph.sb("combined", [P, CH])
        A, B, W = 0, 6, 7
        in_, wo_in, w1_split, w1_ready, wo_split, a_ready, gelu_done, b_ready, wide_ready, wide_copied, prod_ready, \
            added, sum_ready, comb_out, comb_high, comb_low, x_ready, out_ready, out_added, stored, spread_in = map(ph.sem, (
                "in", "wo_in", "w1_split", "w1_ready", "wo_split", "a_ready", "gelu_done", "b_ready", "wide_ready",
                "wide_copied", "prod_ready", "added", "sum_ready", "comb_out", "comb_high", "comb_low", "x_ready", "out_ready",
                "out_added", "stored", "spread_in"))
        block = ph.stack.enter_context(nc.Block())

        NHALF = 2 * NST
        COMBINE = (13, 5)

        def back(r, j, by):
            return (r, j - by) if j >= by else (r - 1, j - by + NHALF)

        def pair_of(x):
            return x % 3

        def earlier_tiles(x):
            last = x - 3 if x >= 3 else max(y for y in range(NX) if pair_of(y) == x) - NX
            return last + 1

        def wait_from(eng, sem, value, r):
            if not isinstance(r, int) or value > 0:
                eng.wait_ge(sem, value)

        @block.sync
        def _(sp):
            for dst, name in ((w1f, "w1"), (b1[:, :], "b1"), (b2[:, :], "b2"), (sum_w[:, :], "sum_w")):
                sp.dma_start(dst, io[name]).then_inc(in_, 16)
            sp.dma_start(w2[:, :, :], io["w2"]).then_inc(in_, 16)
            sp.dma_start(bias[:, :], io["bo"].partition_broadcast(P)).then_inc(wo_in, 16)
            sp.dma_start(wo[:, :, :], io["wo"].rearrange("(k p) f -> p k f", p=P)).then_inc(wo_in, 16)
            for c in range(NC):
                sp.wait_ge(out_added, (c + 1) * BPC)
                sp.dma_start(io["out"][c * CH:(c + 1) * CH, :].rearrange("(b p) d -> p b d", p=P),
                             x2[:, c * BPC:(c + 1) * BPC, :]).then_inc(stored, 16)
            sp.wait_ge(stored, 16 * NC)

        @block.gpsimd
        def _(pool):
            pool.dma_start(spread_w[:, :, :], io["spread_w"]).then_inc(spread_in, 16)
            pool.wait_ge(wo_in, 32)
            for b in range(NB):
                pool.tensor_tensor(x2[:, b, :], x2[:, b, :], bias[:, :], ALU.add).then_inc(x_ready, 1)

            def add(r, n):
                q = n // NEG
                pool.wait_ge(prod_ready, r * NHALF + 2 * n + 2)
                if n % NEG >= 2:
                    pool.wait_ge(added, r * 6 + 3 * q + n % NEG - 1)
                pool.tensor_tensor(acc[:, q, :, :], acc[:, q, :, :], prod[:, n % 2, :, :], ALU.add).then_inc(added, 1)

            with pool.Fori(0, R) as r:
                for n in range(NST):
                    if n % NEG:
                        add(r, n)

        @block.tensor
        def _(pe):
            def first(r, n, e):
                x = n * EG + e
                wait_from(pe, gelu_done, r * NX + earlier_tiles(x), r)
                g = n % NEG
                for h in range(2):
                    last = pe.matmul(banks[:, A + 2 * pair_of(x) + h, :], w1[:, g * EG + e, :],
                                     stack[0:96, at(r), 2 * (n // NEG) + h, :].rearrange("p a t -> p (a t)"), start=True, stop=True)
                last.then_inc(a_ready, 1)

            def widen(r, i, combined_before=None):
                n, h = i // 2, i % 2
                wait_from(pe, wide_copied, r * NHALF + i, r)
                if combined_before is not None:
                    pe.wait_ge(comb_out, combined_before)
                pe.matmul(banks[:, W, :], spread_w[:, h * NEG + n % NEG, :],
                          wT[:, at(r), n // NEG, :].rearrange("p a t -> p (a t)"), start=True, stop=True).then_inc(wide_ready, 1)

            def second(r, i):
                n, h = i // 2, i % 2
                if h == 0:
                    pe.wait_ge(gelu_done, r * NX + (n + 1) * EG)
                wait_from(pe, prod_ready, r * NHALF + i, r)
                for e in range(EG):
                    last = pe.matmul(banks[32 * e:32 * e + 32, B, :], w2[:, (n % NEG) * EG + e, :],
                                     hid[n % 2][:, e, h, :], start=True, stop=True)
                last.then_inc(b_ready, 1)

            def combine(r, q, copied):
                pe.wait_ge(added, r * 6 + 3 * q + 3)
                pe.wait_ge(wide_copied, copied)
                for h in range(2):
                    hh = 2 * q + h
                    last = pe.matmul(banks[32 * hh:32 * hh + 32, W, :], sum_w[:, :], acc[:, q, h, :], start=True, stop=True)
                last.then_inc(sum_ready, 1)

            def round_(loop, lone=False):
                for j in range(NHALF):
                    r = fresh(pe, loop, R - 1, 1)
                    for e in range(2):
                        first(r, j // 2, 2 * (j % 2) + e)
                    combined_before = None
                    if j == COMBINE[0]:
                        combine(r, 0, r * NHALF + j - 1)
                        combined_before = 2 * r + 1
                    if j == COMBINE[1] and not lone:
                        combine(r - 1, 1, r * NHALF + j - 1)
                        combined_before = 2 * r
                    if j >= 2 or not lone:
                        second(*back(r, j, 2))
                    if j >= 1 or not lone:
                        widen(*back(r, j, 1), combined_before)

            pe.wait_ge(in_, 80)
            pe.wait_ge(spread_in, 16)
            pe.wait_ge(w1_ready, 1)
            round_(0, lone=True)
            with pe.Fori(1, R) as r:
                round_(r)
            second(R - 1, NHALF - 2)
            widen(R - 1, NHALF - 1)
            second(R - 1, NHALF - 1)
            combine(R - 1, 1, R * NHALF)
            pe.wait_ge(comb_low, 2 * R)
            pe.wait_ge(wo_split, 2)
            for b in range(NB):
                if b >= 2:
                    pe.wait_ge(out_added, b - 1)
                terms = []
                for k in range(KD):
                    own = at(((b // BPC) * KD + k) * CH + (b % BPC) * P, P)
                    terms.append((high[:, own], low[:, own], woh[:, k, :], wol[:, k, :]))
                split_product(pe, banks[:, A + b % 2, 0:D], terms).then_inc(out_ready, 1)

        @block.scalar
        def _(act):
            def gelu(r, n, e):
                x = n * EG + e
                act.wait_ge(a_ready, r * NX + x + 1)
                if e == 0:
                    wait_from(act, b_ready, r * NHALF + 2 * n - 2, r)
                pair = A + 2 * pair_of(x)
                ex = (n % NEG) * EG + e
                act.activation(hid[n % 2][:, e, :, :], banks[:, pair:pair + 2, :], ACT.Gelu,
                               bias=b1[:, ex:ex + 1]).then_inc(gelu_done, 1)

            act.wait_ge(in_, 80)
            for n in range(NST):
                for e in range(EG):
                    gelu(0, n, e)
            with act.Fori(1, R) as r:
                for n in range(NST):
                    for e in range(EG):
                        gelu(r, n, e)

        @block.vector
        def _(dve):
            def copy_wide(r, i):
                dve.wait_ge(wide_ready, r * NHALF + i + 1)
                wait_from(dve, prod_ready, r * NHALF + i - 3, r)
                dve.tensor_copy(wide[:, (i // 2) % 2, i % 2, :], banks[:, W, :]).then_inc(wide_copied, 1)

            def weigh(r, i):
                n, h = i // 2, i % 2
                q, g = n // NEG, n % NEG
                dve.wait_ge(wide_copied, r * NHALF + i + 1)
                if h == 0:
                    if g == 0:
                        wait_from(dve, sum_ready, 2 * r + q - 1, r)
                    elif g < 3:
                        wait_from(dve, added, r * 6 + 3 * q, r)
                    else:
                        dve.wait_ge(added, r * 6 + 3 * q + 1)
                dst = acc[:, q] if g == 0 else prod[:, n % 2]
                dve.wait_ge(b_ready, r * NHALF + i + 1)
                dve.scalar_tensor_tensor(out=dst[:, h, :], in0=banks[:, B, :], scalar=b2[:, g:g + 1],
                                         in1=wide[:, n % 2, h, :], op0=ALU.add, op1=ALU.mult).then_inc(prod_ready, 1)

            def copy_combined(r, q):
                dve.wait_ge(sum_ready, 2 * r + q + 1)
                wait_from(dve, comb_low, 2 * r + q, r)
                rows = slice(64 * q, 64 * q + 64)
                dve.tensor_copy(combined[rows, :], banks[rows, W, :]).then_inc(comb_out, 1)

            def split_combined(r, q):
                rows, own = slice(64 * q, 64 * q + 64), at(r * CH, CH)
                dve.wait_ge(comb_out, 2 * r + q + 1)
                dve.tensor_copy(high[rows, own], combined[rows, :]).then_inc(comb_high, 1)
                dve.wait_ge(comb_high, 2 * r + q + 1)
                dve.tensor_tensor(low[rows, own], combined[rows, :], high[rows, own], ALU.subtract).then_inc(comb_low, 1)

            def round_(loop, lone=False):
                for j in range(NHALF):
                    r = fresh(dve, loop, R - 1, 1)
                    now = None
                    if j == COMBINE[0]:
                        now = (r, 0)
                    if j == COMBINE[1] and not lone:
                        now = (r - 1, 1)
                    if now:
                        copy_combined(*now)
                    if j >= 2 or not lone:
                        weigh(*back(r, j, 2))
                    if j >= 1 or not lone:
                        copy_wide(*back(r, j, 1))
                    if now:
                        split_combined(*now)

            dve.wait_ge(in_, 80)
            dve.tensor_copy(w1[:, :, :].rearrange("p e i -> p (e i)"), w1f).then_inc(w1_split, 1)
            dve.wait_ge(w1_split, 1)
            dve.tensor_tensor(w1[64:96, :, :].rearrange("p e i -> p (e i)"), w1f[64:96, :],
                              w1[64:96, :, :].rearrange("p e i -> p (e i)"), ALU.subtract).then_inc(w1_ready, 1)
            dve.wait_ge(w1_ready, 1)
            dve.wait_ge(wo_in, 32)
            dve.tensor_copy(woh[:, :, :], wo[:, :, :]).then_inc(wo_split, 1)
            dve.wait_ge(wo_split, 1)
            dve.tensor_tensor(wol[:, :, :], wo[:, :, :], woh[:, :, :], ALU.subtract).then_inc(wo_split, 1)
            round_(0, lone=True)
            with dve.Fori(1, R) as r:
                round_(r)
            weigh(R - 1, NHALF - 2)
            copy_wide(R - 1, NHALF - 1)
            weigh(R - 1, NHALF - 1)
            copy_combined(R - 1, 1)
            split_combined(R - 1, 1)
            for b in range(NB):
                dve.wait_ge(out_ready, b + 1)
                dve.wait_ge(x_ready, b + 1)
                dve.tensor_tensor(x2[:, b, :], banks[:, A + b % 2, 0:D], x2[:, b, :], ALU.add).then_inc(out_added, 1)


def split_product(pe, out, terms, start=True, stop=True):
    n = 0
    for ah, al, bh, bl in terms:
        for a, b in ((ah, bh), (ah, bl), (al, bh)):
            last = pe.matmul(out, a, b, start=start and n == 0, stop=stop and n == 3 * len(terms) - 1)
            n += 1
    return last


def program(nc, io, stop_after=99):
    keep = {}
    with ExitStack() as stack:
        def sb(name, shape, dt=F32):
            keep[name] = stack.enter_context(nc.sbuf_tensor("keep_" + name, shape, dt))

        for name in ("v", "attn"):
            sb(name, [P, NB, D])
        phase_qkv(nc, io, keep)
        phase_attention(nc, io, keep)
        keep["cn"], keep["c2q"] = keep["v"], keep["attn"]
        sb("x1", [P, NB, D])
        sb("ch", [P, KD, T], F32R)
        sb("cl", [P, KD, T], F32R)
        keep["nh"], keep["nl"] = keep["ch"], keep["cl"]
        with ExitStack() as inner:
            keep["cT"] = inner.enter_context(nc.sbuf_tensor("keep_cT", [P, KD, T], F32))
            keep["nmax"] = inner.enter_context(nc.sbuf_tensor("keep_nmax", [P, NB], F32))
            phase_projection(nc, io, keep)
            phase_cross(nc, io, keep)
            phase_fuse(nc, io, keep)
        sb("stack", [96, KD * NC, 4, CH], F32R)
        sb("wT", [96, KD * NC, 2, CH], BF16)
        phase_route(nc, io, keep)
        phase_experts(nc, io, keep)


def host_inputs(inputs):
    import numpy as np
    g = {k: np.asarray(v) for k, v in inputs.items()}
    c = np.ascontiguousarray
    a = {"x": g["x"][0], "ctx": g["ctx_1024"][0], "ctxT": g["ctx_1024"][0].T,
         "wqkvT": g["L0_attn_w_qkv"].T, "ident": np.eye(P, dtype=np.float32)}
    a["ones"] = np.ones((P, P), np.float32)
    a["ctxT"] = np.pad(a["ctxT"], ((0, 0), (0, LPAD - L)))
    a["woutT"], a["b_out"] = g["L0_attn_w_out"].T, g["L0_attn_b_out"]
    a["wlT"], a["b_l"] = g["L0_xattn_W_l"].T, g["L0_xattn_b_l"]
    a["w_c"] = g["L0_xattn_w_c"]
    for n in ("w_cq", "w_q"):
        a[n] = g["L0_xattn_" + n].reshape(KD, P).T
    for n in ("b_cq", "b_c", "b_q"):
        a[n] = g["L0_xattn_" + n].reshape(1)
    f = lambda n: g["L0_ffn_" + n]
    eye = np.eye(4, dtype=np.float32)
    a["wm"], a["bm"], a["wo"], a["bo"] = f("Wm"), f("bm").reshape(KD, P).T, f("Wo"), f("bo")
    gate = np.zeros((4, FD, 4, NE), np.float32)
    for h in range(4):
        gate[h, :, h, :] = f("expert_emb")
    a["gate"] = gate.reshape(P, 4 * NE)
    a["iota"] = np.tile(np.arange(NE, 0, -1, dtype=np.float32), (P, 1))
    a["w1"] = np.tile(f("W1").transpose(1, 0, 2).reshape(FD, NE * EI), (3, 1))
    a["b1"], a["w2"] = f("b1").T, f("W2").transpose(1, 0, 2)
    a["b2"] = f("b2").reshape(NEG, EG * FD).T
    a["sum_w"] = np.tile(np.eye(FD, dtype=np.float32), (EG, 1))
    spread = np.zeros((3, 2, NE, 2, NEG, EG, FD), np.float32)
    for h in range(2):
        for e in range(NE):
            spread[:, h, e, h, e // EG, e % EG, :] = 1.0
    a["spread_w"] = spread.reshape(96, 2 * NEG, P)
    future = np.triu(np.full((P, P), NEGBIG, np.float32), 1)
    a["mask_qk"], a["mask_kq"] = future, future.T
    return {k: c(v) for k, v in a.items()}


SCRATCH = {"qk_parts": ((2, 3, D, T), BF16)}


def declare(nc, arrays):
    from concourse import mybir as _mybir
    io = {}
    for name, a in arrays.items():
        io[name] = nc.dram_tensor(f"in_{name}", a.shape, _mybir.dt.from_np(a.dtype), kind="ExternalInput").ap()
    for name, (shape, dt) in SCRATCH.items():
        io[name] = nc.dram_tensor(f"scratch_{name}", shape, dt, kind="Internal").ap()
    io["out"] = nc.dram_tensor("out", (T, D), F32, kind="ExternalOutput").ap()
    return io


def kernel(**inputs):
    import concourse.bacc as _bacc
    from concourse.bass_utils import run_bass_kernel_spmd as _run

    nc = _bacc.Bacc("TRN2", target_bir_lowering=False, num_devices=1)
    arrays = host_inputs(inputs)
    io = declare(nc, arrays)
    program(nc, io)
    r = _run(nc, [{f"in_{k}": v for k, v in arrays.items()}], core_ids=[0])
    return r.results[0]["out"].reshape(1, T, D)
```

```python
from contextlib import ExitStack

import concourse.bass as bass
from concourse import mybir

F32 = mybir.dt.float32
F32R = mybir.dt.float32r
BF16 = mybir.dt.bfloat16
ALU = mybir.AluOpType
ACT = mybir.ActivationFunctionType
AX = mybir.AxisListType

P = 128
T = 2048
D = 256
KD = D // P
NB = T // P
CH = 512
NC = T // CH
BPC = CH // P
LN_EPS = 1e-5

NH, HD = 16, 16
HG = 4
NG = NH // HG
VW = HD + 1
SCALE = HD ** -0.5
Q_PART = [0, 1, 2, 0, 1, 0]
K_PART = [0, 0, 0, 1, 1, 2]
KROWS = HD * len(Q_PART)
MROWS = KROWS + 3

L = 1601
LB = (L + P - 1) // P
LLAST = L - (LB - 1) * P
LPAD = L + L % 2

FH, FD = 8, 32
NE, EI = 16, 128
EG = 4
NEG = NE // EG
NEGBIG = -1e30
FREE = 1


def tokens(c):
    return slice(c * CH, (c + 1) * CH)


def at(i, n=1):
    return bass.ds(i, n)


def fresh(eng, i, top, least=0):
    if isinstance(i, int):
        return i
    reg = eng.alloc_register()
    eng.reg_mov(reg, i)
    return eng.snap(reg, min_val=least, max_val=top)


class Chain:

    def __init__(self, eng, sem, base=0):
        self.eng, self.sem, self.base, self.n = eng, sem, base, 0

    def then(self, instruction):
        instruction.then_inc(self.sem, 1)
        self.n += 1

    def wait(self):
        self.eng.wait_ge(self.sem, self.base + self.n)

    def link(self, instruction):
        self.then(instruction)
        self.wait()


class Phase:

    def __init__(self, nc, name):
        self.nc, self.name, self.stack = nc, name, ExitStack()

    def __enter__(self):
        self.stack.__enter__()
        return self

    def __exit__(self, *a):
        return self.stack.__exit__(*a)

    def sb(self, name, shape, dt=F32):
        return self.stack.enter_context(self.nc.sbuf_tensor(f"{self.name}_{name}", shape, dt))

    def ps(self, name, shape, dt=F32):
        return self.stack.enter_context(self.nc.psum_tensor(f"{self.name}_{name}", shape, dt))

    def sem(self, name):
        return self.stack.enter_context(self.nc.semaphore(f"{self.name}_{name}"))


class LayerNorm:

    def __init__(self, ph, name):
        self.stats, self.mv = ph.sb(name + "_stats", [P, NB, 6]), ph.sb(name + "_mv", [P, NB, 2])
        self.var, self.std, self.rstd = (ph.sb(f"{name}_{n}", [P, NB]) for n in ("var", "std", "rstd"))
        self.collected, self.var_ready, self.std_ready, self.rstd_ready, self.done = (
            ph.sem(f"{name}_{n}") for n in ("collected", "var_ready", "std_ready", "rstd_ready", "done"))

    def collect(self, dve, x, c):
        blocks = range(c * BPC, (c + 1) * BPC)
        for b in blocks:
            dve.bn_stats(self.stats[:, b, :], x[:, b, :]).then_inc(self.collected, 1)
        for n, b in enumerate(blocks):
            dve.wait_ge(self.collected, 2 * c * BPC + n + 1)
            dve.bn_aggr(self.mv[:, b, :], self.stats[:, b, :]).then_inc(self.collected, 1)
        dve.wait_ge(self.collected, 2 * (c + 1) * BPC)
        at_c = slice(c * BPC, (c + 1) * BPC)
        dve.tensor_scalar(self.var[:, at_c], self.mv[:, at_c, 1], LN_EPS, None, ALU.add).then_inc(self.var_ready, 1)

    def root(self, act, c):
        at_c = slice(c * BPC, (c + 1) * BPC)
        act.wait_ge(self.var_ready, c + 1)
        act.activation(self.std[:, at_c], self.var[:, at_c], ACT.Sqrt).then_inc(self.std_ready, 1)

    def apply(self, dve, x, out, c):
        at_c = slice(c * BPC, (c + 1) * BPC)
        dve.wait_ge(self.std_ready, c + 1)
        dve.reciprocal(self.rstd[:, at_c], self.std[:, at_c]).then_inc(self.rstd_ready, 1)
        dve.wait_ge(self.rstd_ready, c + 1)
        for b in range(c * BPC, (c + 1) * BPC):
            dve.tensor_scalar(out[:, b, :], x[:, b, :], self.mv[:, b, 0:1], self.rstd[:, b:b + 1],
                              ALU.subtract, ALU.mult).then_inc(self.done, 1)


class Turn:

    def __init__(self, ph, name, banks, ident):
        self.banks, self.ident = banks, ident
        self.turned, self.high_done, self.low_done = (
            ph.sem(f"{name}_{n}") for n in ("turned", "high_done", "low_done"))

    def turn(self, pe, src, c, k, ready=None):
        n = c * KD + k
        if ready is not None:
            pe.wait_ge(ready, (c + 1) * BPC)
        if n >= 2:
            pe.wait_ge(self.low_done, n - 1)
        for j in range(BPC):
            last = pe.transpose(self.banks[n % 2][:, j * P:(j + 1) * P], src[:, c * BPC + j, k * P:(k + 1) * P],
                                self.ident[:, :])
        last.then_inc(self.turned, 1)

    def high(self, act, hi, c, k, plain=None):
        n = c * KD + k
        act.wait_ge(self.turned, n + 1)
        if plain is not None:
            act.activation(plain, self.banks[n % 2], ACT.Copy)
        act.activation(hi, self.banks[n % 2], ACT.Copy).then_inc(self.high_done, 1)

    def low(self, dve, hi, lo, c, k):
        n = c * KD + k
        dve.wait_ge(self.high_done, n + 1)
        dve.tensor_tensor(lo, self.banks[n % 2], hi, ALU.subtract).then_inc(self.low_done, 1)


def phase_qkv(nc, io, keep):
    with Phase(nc, "qkv") as ph:
        x = ph.sb("x", [P, NB, D])
        w = ph.sb("w", [P, KD, 3 * D])
        wh, wl = ph.sb("wh", [P, KD, 3 * D], F32R), ph.sb("wl", [P, KD, 3 * D], F32R)
        ident = keep["ident"]
        xh, xl = ph.sb("xh", [P, KD, T], F32R), ph.sb("xl", [P, KD, T], F32R)
        SLOTS = 5
        parts = ph.sb("parts", [P, SLOTS, 3, CH], BF16)
        rem = ph.sb("rem", [P, SLOTS, CH])
        banks = ph.ps("banks", [P, 8, CH])
        ln = LayerNorm(ph, "ln")
        turn = Turn(ph, "turn", (banks[:, 0, :], banks[:, 1, :]), ident)
        ident_in, w_in, wh_done, w_split, qk_ready, p1_ready, r1_ready, p2_ready, p3_ready, v_ready, v_out, v_out_act = map(ph.sem, (
            "ident_in", "w_in", "wh_done", "w_split", "qk_ready", "p1_ready", "r1_ready", "p2_ready", "p3_ready", "v_ready", "v_out", "v_out_act"))
        x_in = [ph.sem(f"x_in{c}") for c in range(NC)]
        stored = [ph.sem(f"stored{n}") for n in range(SLOTS)]
        GF = HG * HD
        FT = 2 * KD
        NQ = FT * NC
        QB, VB = 2, 5
        block = ph.stack.enter_context(nc.Block())

        @block.sync
        def _(sp):
            for c in range(NC):
                sp.dma_start(x[:, c * BPC:(c + 1) * BPC, :],
                             io["x"][tokens(c), :].rearrange("(b p) d -> p b d", p=P)).then_inc(x_in[c], 16)
                if c == 0:
                    sp.dma_start(ident[:, :], io["ident"]).then_inc(ident_in, 16)
                    sp.dma_start(w[:, :, :], io["wqkvT"].rearrange("(k p) f -> p k f", p=P)).then_inc(w_in, 16)
            for n in range(NQ):
                ft, c = n % FT, n // FT
                sp.wait_ge(p3_ready, n + 1)
                for half in range(2):
                    g = 2 * (ft % KD) + half
                    sp.dma_start(io["qk_parts"][ft // KD, g, c].rearrange("a p t -> p a t"),
                                 parts[half * GF:(half + 1) * GF, n % SLOTS, :, :]).then_inc(stored[n % SLOTS], 16)
            for s in range(SLOTS):
                sp.wait_ge(stored[s], 32 * len(range(s, NQ, SLOTS)))

        @block.vector
        def _(dve):
            def normalise(c):
                dve.wait_ge(x_in[c], 16)
                ln.collect(dve, x, c)
                ln.apply(dve, x, x, c)

            def triple(n):
                dve.wait_ge(p1_ready, n + 1)
                dve.tensor_tensor(rem[:, n % SLOTS, :], banks[:, QB + n % 3, :], parts[:, n % SLOTS, 0, :], ALU.subtract)\
                    .then_inc(r1_ready, 1)

            def finish(n):
                dve.wait_ge(p2_ready, n + 1)
                dve.tensor_tensor(parts[:, n % SLOTS, 2, :], rem[:, n % SLOTS, :], parts[:, n % SLOTS, 1, :], ALU.subtract)\
                    .then_inc(p3_ready, 1)

            def low(c):
                for k in range(KD):
                    turn.low(dve, xh[:, k, tokens(c)], xl[:, k, tokens(c)], c, k)

            normalise(0)
            normalise(1)
            low(0)
            dve.wait_ge(wh_done, 1)
            dve.tensor_tensor(wl[:, :, :], w[:, :, :], wh[:, :, :], ALU.subtract).then_inc(w_split, 1)
            low(1)
            for c in range(2, NC):
                normalise(c)
            for c in range(NC):
                for n in range(c * FT, (c + 1) * FT):
                    triple(n)
                    if n >= 1:
                        finish(n - 1)
                if c + 2 < NC:
                    low(c + 2)
            finish(NQ - 1)
            for b in range(1, NB, 2):
                dve.wait_ge(v_ready, b + 1)
                dve.tensor_copy(keep["v"][:, b, :], banks[:, VB + b % 3, 0:D]).then_inc(v_out, 1)

        @block.scalar
        def _(act):
            def first(n):
                act.wait_ge(qk_ready, n + 1)
                if n >= SLOTS:
                    act.wait_ge(stored[n % SLOTS], 32 * (n // SLOTS))
                act.activation(parts[:, n % SLOTS, 0, :], banks[:, QB + n % 3, :], ACT.Copy).then_inc(p1_ready, 1)

            def second(n):
                act.wait_ge(r1_ready, n + 1)
                act.activation(parts[:, n % SLOTS, 1, :], rem[:, n % SLOTS, :], ACT.Copy).then_inc(p2_ready, 1)

            def high(c):
                for k in range(KD):
                    turn.high(act, xh[:, k, tokens(c)], c, k)

            for c in range(2):
                ln.root(act, c)
            high(0)
            act.wait_ge(w_in, 16)
            act.activation(wh[:, :, :], w[:, :, :], ACT.Copy).then_inc(wh_done, 1)
            high(1)
            for c in range(2, NC):
                ln.root(act, c)
            for c in range(NC):
                for n in range(c * FT, (c + 1) * FT):
                    first(n)
                    if n >= 1:
                        second(n - 1)
                if c + 2 < NC:
                    high(c + 2)
            second(NQ - 1)
            for b in range(0, NB, 2):
                act.wait_ge(v_ready, b + 1)
                act.activation(keep["v"][:, b, :], banks[:, VB + b % 3, 0:D], ACT.Copy).then_inc(v_out_act, 1)

        @block.tensor
        def _(pe):
            def turn_chunk(c):
                for k in range(KD):
                    turn.turn(pe, x, c, k, ready=ln.done)

            pe.wait_ge(ident_in, 16)
            turn_chunk(0)
            turn_chunk(1)
            pe.wait_ge(w_split, 1)
            for c in range(NC):
                pe.wait_ge(turn.low_done, (c + 1) * KD)
                for n in range(c * FT, (c + 1) * FT):
                    if n >= 3:
                        pe.wait_ge(r1_ready, n - 2)
                    feat = slice((n % FT) * P, (n % FT + 1) * P)
                    split_product(pe, banks[:, QB + n % 3, :],
                                  [(wh[:, k, feat], wl[:, k, feat], xh[:, k, tokens(c)], xl[:, k, tokens(c)])
                                   for k in range(KD)]).then_inc(qk_ready, 1)
                    if n == c * FT and c + 2 < NC:
                        turn_chunk(c + 2)
            for b in range(NB):
                if b >= 3:
                    pe.wait_ge(v_out if (b - 3) % 2 else v_out_act, (b - 3) // 2 + 1)
                tok, feat = slice(b * P, (b + 1) * P), slice(2 * D, 3 * D)
                split_product(pe, banks[:, VB + b % 3, 0:D],
                              [(xh[:, k, tok], xl[:, k, tok], wh[:, k, feat], wl[:, k, feat]) for k in range(KD)]).then_inc(v_ready, 1)


def causal_steps():
    return [(qc, kb, max(kb - BPC * qc, 0) * P) for qc in range(NC) for kb in range(BPC * (qc + 1))]


def max_tiles():
    return [(qb, c, min(CH, (qb + 1) * P - c * CH), h)
            for qb in range(NB) for c in range(qb // BPC + 1) for h in range(HG)]


def ring_items(steps, tiles, ahead, lag):
    ns, wait = len(steps), 7
    chunk_end = {max(u for u, tile in enumerate(tiles) if tile[0] // BPC == qc): qc for qc in range(NC)}

    def with_rows(run):
        items, pending = [], []
        for n, (a, u) in enumerate(run):
            items.append(("max", a, u))
            if u in chunk_end:
                pending.append((n + wait, ("rows", a, chunk_end[u])))
            if pending and pending[0][0] <= n:
                items.append(pending.pop(0)[1])
        assert not pending
        return items

    def spread(plan, items, first, last):
        cost = lambda item: 64 + tiles[item[2]][2] if item[0] == "max" else 300
        weights = [(CH - off + 320) * w for _, _, off in steps[first:last] for w in (1, 1, 1)]
        items, given, due, total = list(items), 0.0, 0.0, sum(map(cost, items))
        for slot, weight in enumerate(weights):
            due += total * weight / sum(weights)
            while items and (given + cost(items[0]) / 2 <= due or slot == len(weights) - 1):
                given += cost(items[0])
                plan[first + slot // 3][slot % 3].append(items.pop(0))

    first_step = [min(i for i, step in enumerate(steps) if step[0] == qc) for qc in range(NC)] + [ns]
    plans = [[[[], [], [], []] for _ in range(ns + lag)] for _ in range(2)]
    to_ahead = [(1, u) for u in range(ahead)]
    run = with_rows([(0, u) for u in range(len(tiles))] + to_ahead)
    cuts = [run.index(("rows", 0, qc)) + wait for qc in range(NC)] + [len(run)]
    for qc in range(NC):
        spread(plans[0], run[cuts[qc]:cuts[qc + 1]], first_step[qc], first_step[qc + 1])
    spread(plans[1], with_rows([(0, u) for u in range(ahead, len(tiles))] + to_ahead), 0, ns)
    for plan in plans:
        for qc in range(NC):
            plan[min(first_step[qc + 1] + 3, ns + lag - 1)][3].append(("out", 0, qc))
    return run[:cuts[0]], plans[0], plans[1]


def phase_attention(nc, io, keep):
    with Phase(nc, "att") as ph:
        qst, kst = ph.sb("qst", [P, NH * T], BF16), ph.sb("kst", [P, NH * T], BF16)
        vg = ph.sb("vg", [P, NB, HG, 32])
        prob = ph.sb("prob", [P, 3, HG, CH])
        osb = ph.sb("osb", [P, 2, CH])
        rden = ph.sb("rden", [P, BPC, HG])
        pmax = ph.sb("pmax", [P, HG * NB, NC])
        NU = HG * BPC
        NTURN = 96
        nmax, nrem = ph.sb("nmax", [P, HG, BPC]), ph.sb("nrem", [P, HG, BPC])
        nparts = ph.sb("nparts", [P, NTURN], BF16)
        npart = nparts[:, 0:3 * NU].rearrange("p (a h b) -> p a h b", a=3, h=HG)
        nrow = ph.sb("nrow", [NTURN, 2, P], BF16)
        ident, identb = keep["ident"], ph.sb("identb", [P, P], BF16)
        wout = ph.sb("wout", [P, KD, D])
        mask_qk, mask_kq = ph.sb("mask_qk", [P, P], BF16), ph.sb("mask_kq", [P, P], BF16)
        banks = ph.ps("banks", [P, 8, CH])
        S, O, RING = 0, 4, (5, 6, 7)

        wout_in, wout_split, stack_in, ones_ready, pmax_ready, vg_zero, ring_ready, ring_read, chain_s, nm_split, \
            vg_ready, s_ready, exp_done, pv_done, o_copied, rden_ready, constb_in = map(ph.sem, (
                "wout_in", "wout_split", "stack_in", "ones_ready", "pmax_ready", "vg_zero", "ring_ready",
                "ring_read", "dve_chain", "nm_split", "vg_ready", "s_ready",
                "exp_done", "pv_done", "o_copied", "rden_ready", "constb_in"))
        nm_in = [ph.sem(f"nm_in{p}") for p in range(2)]
        first_in = [ph.sem(f"first_in{n}") for n in range(2)]
        steps, tiles = causal_steps(), max_tiles()
        NS, NM = len(steps), len(tiles)
        last_step = [max(i for i, s in enumerate(steps) if s[0] == qc) for qc in range(NC)]
        LAG = 2
        AHEAD = next(u for u, tile in enumerate(tiles) if tile[0] == NB - 5)
        before, first_plan, plan = ring_items(steps, tiles, AHEAD, LAG)
        last_plan = [[[item for item in slot if not item[1]] for slot in step] for step in plan]
        flat = lambda p: [item for step in p for slot in step for item in slot]
        ITEMS = len(flat(plan))
        START = len(before) + len(flat(first_plan)) - ITEMS
        assert ITEMS % len(RING) == 0
        CHAIN = 4
        PARTS_IN = 9 * 16
        ROWS_IN = 3 * 16

        def query(g, h, t):
            return g * (HG * T) + (t // CH) * (HG * CH) + h * CH + t % CH


        def base(g, p):
            return len(before) if p is first_plan else START + g * ITEMS

        def bank_of(n, p):
            return RING[((len(before) if p is first_plan else START) + n) % len(RING)]

        def rows_at(g, qc):
            item, plan_of = ("rows", 0, qc), lambda g: (first_plan, plan, plan, last_plan)[g]
            if g == 0 and item in before:
                return before.index(item)
            if item not in flat(plan_of(g)):
                g, item = g - 1, ("rows", 1, qc)
            return base(g, plan_of(g)) + flat(plan_of(g)).index(item)

        def needs_next(p):
            return next((s for s, step in enumerate(p) for slot in step for item in slot if item[1]), None)

        block = ph.stack.enter_context(nc.Block())

        @block.sync
        def _(sp):

            def load(g, first, last, sem):
                cols = slice(query(g, 0, first * CH), query(g, 0, first * CH) + (last - first) * HG * CH)
                row = 0
                for part, n in enumerate((3, 2, 1)):
                    rows = slice(row * HD, (row + n) * HD)
                    src = io["qk_parts"][0, g, first:last, 0:n].rearrange("c a (d h) t -> (a d) c (h t)", h=HG)
                    sp.dma_start(qst[rows, cols].rearrange("p (c n) -> p c n", n=HG * CH), src).then_inc(sem, 16)
                    for i in range(n):
                        src = io["qk_parts"][1, g, first:last, part].rearrange("c (d h) t -> d c (h t)", h=HG)
                        sp.dma_start(kst[(row + i) * HD:(row + i + 1) * HD, cols].rearrange("p (c n) -> p c n", n=HG * CH),
                                     src).then_inc(sem, 16)
                    row += n

            load(0, 0, 1, first_in[0])
            load(0, 1, NC, first_in[1])
            sp.dma_start(wout[:, :, :], io["woutT"].rearrange("(k p) f -> p k f", p=P)).then_inc(wout_in, 16)
            for g in range(NG):
                for qc in range(NC):
                    sp.wait_ge(ring_read, rows_at(g, qc) + 1)
                    for part in range(3):
                        own = query(g, 0, qc * CH)
                        sp.dma_start(qst[KROWS + part:KROWS + part + 1, own:own + HG * CH].rearrange("a (n t) -> a n t", t=P),
                                     nrow[part * NU:(part + 1) * NU, qc % 2, :]).then_inc(nm_in[qc % 2], 16)
                    if g + 1 < NG and qc == 1:
                        if g >= 1:
                            sp.wait_ge(stack_in, g * PARTS_IN)
                        load(g + 1, 0, NC, stack_in)

        @block.gpsimd
        def _(pool):
            for dst, name in ((identb, "ident"), (mask_qk, "mask_qk"), (mask_kq, "mask_kq")):
                pool.dma_start(dst[:, :], io[name]).then_inc(constb_in, 16)
            for g in range(NG):
                pool.memset(kst[KROWS:MROWS, g * (HG * T):(g + 1) * (HG * T)], 1.0).then_inc(ones_ready, 1)
            pool.wait_ge(ones_ready, NG)
            pool.wait_ge(wout_in, 16)
            pool.tensor_copy(keep["wouth"][:, :, :], wout[:, :, :]).then_inc(wout_split, 1)
            pool.wait_ge(wout_split, 1)
            pool.tensor_tensor(keep["woutl"][:, :, :], wout[:, :, :], keep["wouth"][:, :, :], ALU.subtract).then_inc(wout_split, 1)
            pool.wait_ge(wout_split, 2)

        @block.tensor
        def _(pe):
            def max_tile(r, u, bank):
                qb, c, width, h = tiles[u]
                out = banks[:, bank, 0:width]
                diagonal = c == qb // BPC
                last = pe.matmul(out, qst[0:KROWS, at(query(r, h, qb * P), P)],
                                 kst[0:KROWS, at(query(r, h, c * CH), width)], start=True, stop=not diagonal)
                if diagonal:
                    last = pe.matmul(out[:, width - P:width], identb[:, :], mask_qk[:, :], start=False, stop=True)
                return last

            def turn_maxima(r, qc, bank):
                pe.wait_ge(nm_split, r * NC + qc + 1)
                rowbank = banks[0:NTURN, bank, :].bitcast(BF16)
                return pe.transpose(rowbank[:, 0:P], nparts[:, :], identb[:, :])

            def turn_output(g, qc, bank):
                pe.wait_ge(o_copied, FREE + g * NC + qc + 1)
                for j in range(BPC):
                    last = pe.transpose(banks[:, bank, j * P:(j + 1) * P], osb[:, qc % 2, j * P:(j + 1) * P], ident[:, :])
                return last

            def items(g, p, slot, n):
                for kind, ahead, what in slot:
                    pe.wait_ge(ring_read, base(g, p) + n - len(RING) + 1)
                    bank = bank_of(n, p)
                    if kind == "max" and p is first_plan and not ahead:
                        pe.wait_ge(first_in[1], PARTS_IN)
                    last = (max_tile(g + ahead, what, bank) if kind == "max" else
                            turn_maxima(g + ahead, what, bank) if kind == "rows" else turn_output(g, what, bank))
                    last.then_inc(ring_ready, 1)
                    n += 1
                return n

            def scores(g, s, pair):
                qc, kb, off = steps[s]
                if kb == 0 and pair == 0:
                    pe.wait_ge(nm_in[qc % 2], g * (NC // 2 * ROWS_IN) + (qc // 2 + 1) * ROWS_IN)
                if s >= 1:
                    pe.wait_ge(exp_done, g * (2 * NS) + 2 * (s - 1) + pair + 1)
                for h in (2 * pair, 2 * pair + 1):
                    out = banks[:, S + h, off:CH]
                    diagonal = kb >= BPC * qc
                    last = pe.matmul(out, kst[0:MROWS, at(query(g, h, kb * P), P)],
                                     qst[0:MROWS, at(query(g, h, qc * CH + off), CH - off)],
                                     start=True, stop=not diagonal)
                    if diagonal:
                        last = pe.matmul(out[:, 0:P], identb[:, :], mask_kq[:, :], start=False, stop=True)
                last.then_inc(s_ready, 1)

            def values(g, s):
                qc, kb, off = steps[s]
                if s == 0:
                    pe.wait_ge(vg_ready, g + 1)
                if kb == 0:
                    pe.wait_ge(o_copied, FREE + g * NC + qc)
                pe.wait_ge(exp_done, g * (2 * NS) + 2 * (s + 1))
                for h in range(HG):
                    last = pe.matmul(banks[32 * h:32 * h + 32, O, off:CH], vg[:, kb, h, :], prob[:, s % 3, h, off:CH],
                                     start=kb == 0, stop=kb == BPC * qc + BPC - 1)
                last.then_inc(pv_done, 1)

            def round_(g, plan):
                n, loop = 0, g
                for s, slots in enumerate(plan):
                    g = fresh(pe, loop, NG - 2, 1)
                    if s == needs_next(plan):
                        pe.wait_ge(stack_in, (g + 1) * PARTS_IN)
                    n = items(g, plan, slots[0], n)
                    if s < NS:
                        scores(g, s, 0)
                    n = items(g, plan, slots[1], n)
                    if s < NS:
                        scores(g, s, 1)
                    n = items(g, plan, slots[2], n)
                    if s >= LAG:
                        values(g, s - LAG)
                    n = items(g, plan, slots[3], n)

            pe.sem_inc(pv_done, FREE)
            pe.wait_ge(constb_in, 48)
            for n, (kind, _, what) in enumerate(before):
                if n >= len(RING):
                    pe.wait_ge(ring_read, n - len(RING) + 1)
                bank = RING[n % len(RING)]
                if kind == "max":
                    pe.wait_ge(first_in[min(tiles[what][0] // BPC, 1)], PARTS_IN)
                (max_tile(0, what, bank) if kind == "max" else turn_maxima(0, what, bank)).then_inc(ring_ready, 1)
            pe.wait_ge(ones_ready, 1)
            round_(0, first_plan)
            pe.wait_ge(ones_ready, NG)
            with pe.Fori(1, NG - 1) as g:
                round_(g, plan)
            round_(NG - 1, last_plan)

        @block.scalar
        def _(act):
            def round_(loop):
                for s in range(NS):
                    g = fresh(act, loop, NG - 1)
                    qc, kb, off = steps[s]
                    act.wait_ge(pv_done, FREE + g * NS + max(s - 2, 0))
                    for pair in range(2):
                        act.wait_ge(s_ready, g * (2 * NS) + 2 * s + pair + 1)
                        heads = slice(2 * pair, 2 * pair + 2)
                        act.activation(prob[:, s % 3, heads, off:CH], banks[:, 2 * pair:2 * pair + 2, off:CH], ACT.Exp,
                                       scale=SCALE).then_inc(exp_done, 1)
                        if pair == 0 and s - 3 in last_step:
                            copy_output(g, last_step.index(s - 3))
                copy_output(g, NC - 1)

            def copy_output(g, qc):
                act.wait_ge(pv_done, FREE + g * NS + last_step[qc] + 1)
                act.activation(osb[:, qc % 2, :], banks[:, O, :], ACT.Copy).then_inc(o_copied, 1)

            act.sem_inc(o_copied, FREE)
            with act.Fori(0, NG) as g:
                round_(g)

        @block.vector
        def _(dve):
            def max_tile(r, u, bank):
                qb, c, width, h = tiles[u]
                n = h * NB + qb
                return dve.tensor_reduce(pmax[:, n, c:c + 1], banks[:, bank, 0:width], AX.X, ALU.max)

            def ends_chunk(u):
                return u == NM - 1 or tiles[u + 1][0] // BPC > tiles[u][0] // BPC

            def split_maxima(r, qc, reduced):
                chain = Chain(dve, chain_s, (r * NC + qc) * CHAIN)
                dve.wait_ge(ring_read, reduced)
                own = pmax[:, :, :].rearrange("p (h n) c -> p h n c", h=HG)[:, :, qc * BPC:(qc + 1) * BPC, :]
                chain.link(dve.tensor_reduce(nmax[:, :, :], own, AX.X, ALU.max, negate=True))
                chain.link(dve.tensor_copy(npart[:, 0, :, :], nmax[:, :, :]))
                chain.link(dve.tensor_tensor(nrem[:, :, :], nmax[:, :, :], npart[:, 0, :, :], ALU.subtract))
                chain.link(dve.tensor_copy(npart[:, 1, :, :], nrem[:, :, :]))
                assert chain.n == CHAIN
                dve.tensor_tensor(npart[:, 2, :, :], nrem[:, :, :], npart[:, 1, :, :], ALU.subtract).then_inc(nm_split, 1)

            def copy_maxima(r, qc, bank):
                if not isinstance(r, int) or r * NC + qc >= 2:
                    dve.wait_ge(nm_in[qc % 2], r * (NC // 2 * ROWS_IN) + qc // 2 * ROWS_IN)
                rowbank = banks[0:NTURN, bank, :].bitcast(BF16)
                return dve.tensor_copy(nrow[:, qc % 2, :], rowbank[:, 0:P])

            def group_values(g):
                dve.wait_ge(pv_done, FREE + g * NS)
                dve.tensor_copy(vg[:, :, :, 0:HD], keep["v"][:, :, at(g * (HG * HD), HG * HD)]
                                .rearrange("p b (h d) -> p b h d", h=HG)).then_inc(vg_ready, 1)

            def scale_output(g, qc, bank, before_it):
                dve.wait_ge(ring_read, before_it)
                turned = banks[:, bank, :].rearrange("p (b h d) -> p b h d", b=BPC, h=HG)
                dve.reciprocal(rden[:, :, :], turned[:, :, :, HD]).then_inc(rden_ready, 1)
                dve.wait_ge(rden_ready, g * NC + qc + 1)
                return dve.tensor_tensor(keep["attn"][:, qc * BPC:(qc + 1) * BPC, at(g * (HG * HD), HG * HD)]
                                         .rearrange("p b (h d) -> p b h d", h=HG), turned[:, :, :, 0:HD],
                                         rden[:, :, :].unsqueeze(3).broadcast_to([P, BPC, HG, HD]), ALU.mult)

            def items(g, p, slot, n):
                for kind, ahead, what in slot:
                    dve.wait_ge(ring_ready, base(g, p) + n + 1)
                    bank = bank_of(n, p)
                    last = (max_tile(g + ahead, what, bank) if kind == "max" else
                            copy_maxima(g + ahead, what, bank) if kind == "rows" else
                            scale_output(g, what, bank, base(g, p) + n))
                    last.then_inc(ring_read, 1)
                    n += 1
                    if kind == "max" and ends_chunk(what):
                        split_maxima(g + ahead, tiles[what][0] // BPC, base(g, p) + n)
                return n

            def round_(g, plan):
                n, loop = 0, g
                for s, slots in enumerate(plan):
                    g = fresh(dve, loop, NG - 2, 1)
                    if s == 1:
                        group_values(g)
                    for slot in slots:
                        n = items(g, plan, slot, n)

            dve.memset(pmax[:, :, :], NEGBIG).then_inc(pmax_ready, 1)
            dve.memset(nparts[:, :], 0.0).then_inc(pmax_ready, 1)
            dve.memset(vg[:, :, :, :], 0.0).then_inc(vg_zero, 1)
            dve.wait_ge(vg_zero, 1)
            dve.memset(vg[:, :, :, HD:VW], 1.0).then_inc(vg_zero, 1)
            dve.wait_ge(vg_zero, 2)
            dve.wait_ge(pmax_ready, 2)
            for n, (kind, _, what) in enumerate(before):
                dve.wait_ge(ring_ready, n + 1)
                bank = RING[n % len(RING)]
                (max_tile(0, what, bank) if kind == "max" else copy_maxima(0, what, bank)).then_inc(ring_read, 1)
                if kind == "max" and ends_chunk(what):
                    split_maxima(0, tiles[what][0] // BPC, n + 1)
            round_(0, first_plan)
            with dve.Fori(1, NG - 1) as g:
                round_(g, plan)
            round_(NG - 1, last_plan)


def phase_projection(nc, io, keep):
    x1, cn, cT, ch, cl = (keep[n] for n in ("x1", "cn", "cT", "ch", "cl"))
    with Phase(nc, "proj") as ph:
        bias, ident, wh, wl = ph.sb("bias", [P, D]), keep["ident"], keep["wouth"], keep["woutl"]
        ah, al = ph.sb("ah", [P, 2, KD, CH], F32R), ph.sb("al", [P, 2, KD, CH], F32R)
        ctx = keep["wf"][:, :, :].rearrange("p b d -> p (b d)")
        qT = ctx[:, 0:KD * LPAD].rearrange("p (k l) -> p k l", k=KD)
        q = ctx[:, 0:LB * D].rearrange("p (b d) -> p b d", d=D)
        banks = ph.ps("banks", [P, 8, CH])
        ln = LayerNorm(ph, "ln")
        turn_a = Turn(ph, "a", (banks[:, 0, :], banks[:, 1, :]), ident)
        turn_c = Turn(ph, "c", (banks[:, 2, :], banks[:, 3, :]), ident)
        x_in = [ph.sem(f"x_in{c}") for c in range(NC)]
        bias_in, wcol_in, xb_done, o_ready, o_added, qT_in, q_in, ctx_high, ctx_low = map(ph.sem, (
            "bias_in", "wcol_in", "xb_done", "o_ready", "o_added", "qT_in", "q_in", "ctx_high", "ctx_low"))
        block = ph.stack.enter_context(nc.Block())

        @block.sync
        def _(sp):
            sp.dma_start(bias[:, :], io["b_out"].partition_broadcast(P)).then_inc(bias_in, 16)
            for c in range(NC):
                sp.dma_start(x1[:, c * BPC:(c + 1) * BPC, :],
                             io["x"][tokens(c), :].rearrange("(b p) d -> p b d", p=P)).then_inc(x_in[c], 16)
            sp.dma_start(keep["wcol"][:, 0, :], io["w_cq"]).then_inc(wcol_in, 16)
            sp.dma_start(keep["wcol"][:, 1, :], io["w_q"]).then_inc(wcol_in, 16)
            sp.dma_start(qT, io["ctxT"].rearrange("(k p) l -> p k l", p=P)).then_inc(qT_in, 16)
            sp.wait_ge(wcol_in, 32)
            sp.wait_ge(ctx_low, 1)
            sp.dma_start(q, io["ctx"].rearrange("(b p) d -> p b d", p=P)).then_inc(q_in, 16)

        @block.gpsimd
        def _(pool):
            pool.wait_ge(bias_in, 16)
            for b in range(NB):
                if b % BPC == 0:
                    pool.wait_ge(x_in[b // BPC], 16)
                pool.tensor_tensor(x1[:, b, :], x1[:, b, :], bias[:, :], ALU.add).then_inc(xb_done, 1)
            pool.wait_ge(ctx_high, 1)
            pool.tensor_tensor(keep["qTl"][:, :, :], qT, keep["qTh"][:, :, :], ALU.subtract).then_inc(ctx_low, 1)
            pool.wait_ge(ctx_high, 2)
            pool.tensor_tensor(keep["ql"][:, :, :], q, keep["qh"][:, :, :], ALU.subtract).then_inc(ctx_low, 1)

        @block.vector
        def _(dve):
            def low_a(c):
                for k in range(KD):
                    turn_a.low(dve, ah[:, c % 2, k, :], al[:, c % 2, k, :], c, k)

            def low_c(c):
                for k in range(KD):
                    turn_c.low(dve, ch[:, k, tokens(c)], cl[:, k, tokens(c)], c, k)

            low_a(0)
            low_a(1)
            for c in range(NC):
                for b in range(c * BPC, (c + 1) * BPC):
                    dve.wait_ge(o_ready, b + 1)
                    dve.wait_ge(xb_done, b + 1)
                    dve.tensor_tensor(x1[:, b, :], banks[:, 4 + b % 4, 0:D], x1[:, b, :], ALU.add).then_inc(o_added, 1)
                dve.wait_ge(o_added, (c + 1) * BPC)
                ln.collect(dve, x1, c)
                if c + 2 < NC:
                    low_a(c + 2)
                ln.apply(dve, x1, cn, c)
                if c >= 1:
                    low_c(c - 1)
            low_c(NC - 1)

        @block.scalar
        def _(act):
            def high_a(c):
                if c >= 2:
                    act.wait_ge(o_ready, (c - 1) * BPC)
                for k in range(KD):
                    turn_a.high(act, ah[:, c % 2, k, :], c, k)

            def high_c(c):
                for k in range(KD):
                    turn_c.high(act, ch[:, k, tokens(c)], c, k, plain=cT[:, k, tokens(c)])

            high_a(0)
            high_a(1)
            for c in range(NC):
                if c + 2 < NC:
                    high_a(c + 2)
                ln.root(act, c)
                if c >= 1:
                    high_c(c - 1)
                if c == 0:
                    act.wait_ge(qT_in, 16)
                    act.activation(keep["qTh"][:, :, :], qT, ACT.Copy).then_inc(ctx_high, 1)
                if c == 2:
                    act.wait_ge(q_in, 16)
                    act.activation(keep["qh"][:, :, :], q, ACT.Copy).then_inc(ctx_high, 1)
            high_c(NC - 1)

        @block.tensor
        def _(pe):
            def turn_attention(c):
                for k in range(KD):
                    turn_a.turn(pe, keep["attn"], c, k)

            def turn_norm(c):
                for k in range(KD):
                    turn_c.turn(pe, cn, c, k, ready=ln.done)

            def project(c):
                pe.wait_ge(turn_a.low_done, (c + 1) * KD)
                for b in range(c * BPC, (c + 1) * BPC):
                    if b >= 4:
                        pe.wait_ge(o_added, b - 3)
                    tok = slice((b % BPC) * P, (b % BPC + 1) * P)
                    split_product(pe, banks[:, 4 + b % 4, 0:D], [(ah[:, c % 2, k, tok], al[:, c % 2, k, tok], wh[:, k, :], wl[:, k, :])
                                                                 for k in range(KD)]).then_inc(o_ready, 1)

            turn_attention(0)
            turn_attention(1)
            for c in range(NC):
                project(c)
                if c + 2 < NC:
                    turn_attention(c + 2)
                if c >= 1:
                    turn_norm(c - 1)
            turn_norm(NC - 1)


def phase_cross(nc, io, keep):
    cT = keep["cT"]
    with Phase(nc, "cross") as ph:
        qTh, qTl, qh, ql = (keep[n] for n in ("qTh", "qTl", "qh", "ql"))
        w, wh, wl = keep["wf"], keep["wfh"], keep["wfl"]
        wc, junk = ph.sb("wc", [P, D]), ph.sb("junk", [P, D])
        wcol, ident = keep["wcol"], keep["ident"]
        cw, cwh, cwl = ph.sb("cw", [P, KD, P]), ph.sb("cwh", [P, KD, P], F32R), ph.sb("cwl", [P, KD, P], F32R)
        prob, total, rtotal = ph.sb("prob", [P, L]), ph.sb("total", [P, NB]), ph.sb("rtotal", [P, NB])
        pTh, pTl = ph.sb("pTh", [P, LB, P], F32R), ph.sb("pTl", [P, LB, P], F32R)
        banks = ph.ps("banks", [P, 8, CH])
        S, R, O = 0, 4, 6
        GROUPS = [list(range(t, min(t + 4, LB))) for t in range(0, LB, 4)]
        NGR = len(GROUPS)
        rows = lambda t: P if t < LB - 1 else LLAST
        in_, w_in, b_in, dots, xb_done, split_s, split_done, cw_s, cw_ready, s_ready, nm_ready, exp_done, turned, high_done, low_done, \
            o_ready, r_ready, o_done = map(ph.sem, (
                "in", "w_in", "b_in", "dots", "xb_done", "split_s", "split_done", "cw_s", "cw_ready", "s_ready", "nm_ready", "exp_done", "turned",
                "high_done", "low_done", "o_ready", "r_ready", "o_done"))
        block = ph.stack.enter_context(nc.Block())

        @block.sync
        def _(sp):
            sp.dma_start(wc[:, :], io["w_c"].partition_broadcast(P)).then_inc(in_, 16)
            sp.dma_start(keep["bias_f"][:, :], io["b_l"].partition_broadcast(P)).then_inc(b_in, 16)
            sp.dma_start(w[:, 0:4 * KD, :], io["wlT"].rearrange("(k p) f -> p k f", p=P)).then_inc(w_in, 16)
            for n, name in enumerate(("b_c", "b_q", "b_cq")):
                sp.dma_start(keep["bs"][:, n:n + 1], io[name].partition_broadcast(P)).then_inc(w_in, 16)
            sp.dma_start(keep["ones"][:, :], io["ones"]).then_inc(w_in, 16)

        @block.gpsimd
        def _(pool):
            pool.wait_ge(b_in, 16)
            for b in range(NB):
                pool.tensor_tensor(keep["x1"][:, b, :], keep["x1"][:, b, :], keep["bias_f"][:, :], ALU.add).then_inc(xb_done, 1)
            pool.wait_ge(w_in, 80)
            pool.tensor_copy(wh[:, KD:3 * KD, :], w[:, KD:3 * KD, :]).then_inc(split_s, 1)
            pool.wait_ge(split_s, 1)
            pool.tensor_tensor(wl[:, KD:3 * KD, :], w[:, KD:3 * KD, :], wh[:, KD:3 * KD, :], ALU.subtract).then_inc(split_done, 1)
            pool.wait_ge(xb_done, NB)
            pool.wait_ge(split_done, 1)

        @block.vector
        def _(dve):
            def weigh(i, first=False):
                for k in range(KD):
                    dve.tensor_scalar(cw[:, k, :], cT[:, k, at(i * P, P)], wcol[:, 0, k:k + 1], wcol[:, 1, k:k + 1],
                                      ALU.mult, ALU.add).then_inc(cw_s, 1)
                dve.wait_ge(cw_s, i * 3 + 2)
                dve.tensor_copy(cwh[:, :, :], cw[:, :, :]).then_inc(cw_s, 1)
                dve.wait_ge(cw_s, i * 3 + 3)
                dve.tensor_tensor(cwl[:, :, :], cw[:, :, :], cwh[:, :, :], ALU.subtract).then_inc(cw_ready, 1)

            def context_term(i):
                if not isinstance(i, int):
                    dve.wait_ge(dots, 2 * i)
                dve.tensor_tensor(junk[:, :], keep["cn"][:, at(i), :].rearrange("p a d -> p (a d)"), wc[:, :],
                                  ALU.mult).then_inc(dots, 1)
                dve.wait_ge(dots, 2 * i + 1)
                dve.tensor_reduce(keep["rowc"][:, at(i)], junk[:, :], AX.X, ALU.add).then_inc(dots, 1)

            def maximum(i):
                dve.wait_ge(s_ready, i + 1)
                dve.tensor_reduce(keep["nmax"][:, at(i)], banks[:, S:S + 4, :].rearrange("p b c -> p (b c)")[:, 0:L],
                                  AX.X, ALU.max, negate=True).then_inc(nm_ready, 1)

            def low(i):
                for g, ts in enumerate(GROUPS):
                    dve.wait_ge(high_done, i * NGR + g + 1)
                    r = rows(ts[-1])
                    dve.tensor_tensor(pTl[0:r, ts[0]:ts[-1] + 1, :], banks[0:r, R + g % 2, 0:len(ts) * P]
                                      .rearrange("p (t c) -> p t c", c=P), pTh[0:r, ts[0]:ts[-1] + 1, :],
                                      ALU.subtract).then_inc(low_done, 1)

            def normalise(i):
                dve.reciprocal(rtotal[:, at(i)], total[:, at(i)]).then_inc(r_ready, 1)
                dve.wait_ge(r_ready, i + 1)
                dve.wait_ge(o_ready, i + 1)
                dve.tensor_scalar(keep["c2q"][:, at(i), :].rearrange("p a d -> p (a d)"), banks[:, O, 0:D],
                                  rtotal[:, at(i)], None, ALU.mult).then_inc(o_done, 1)

            dve.sem_inc(o_done, FREE)
            weigh(0)
            dve.wait_ge(in_, 16)
            context_term(0)
            maximum(0)
            weigh(1)
            with dve.Fori(1, NB - 1) as i:
                low(i - 1)
                maximum(i)
                weigh(i + 1)
                context_term(i)
                normalise(i - 1)
            low(NB - 2)
            maximum(NB - 1)
            normalise(NB - 2)
            dve.wait_ge(dots, 2 * (NB - 1))
            context_term(NB - 1)
            low(NB - 1)
            normalise(NB - 1)

        @block.scalar
        def _(act):
            def exponent(i):
                act.wait_ge(nm_ready, i + 1)
                act.activation(prob[:, :], banks[:, S:S + 4, :].rearrange("p b c -> p (b c)")[:, 0:L], ACT.Exp,
                               bias=keep["nmax"][:, at(i)], accum_out=total[:, at(i)]).then_inc(exp_done, 1)

            def high(i):
                for g, ts in enumerate(GROUPS):
                    act.wait_ge(turned, i * NGR + g + 1)
                    r = rows(ts[-1])
                    act.activation(pTh[0:r, ts[0]:ts[-1] + 1, :], banks[0:r, R + g % 2, 0:len(ts) * P]
                                   .rearrange("p (t c) -> p t c", c=P), ACT.Copy).then_inc(high_done, 1)

            exponent(0)
            with act.Fori(1, NB) as i:
                high(i - 1)
                exponent(i)
            high(NB - 1)

        @block.tensor
        def _(pe):
            CHUNKS = [(a, min(a + CH, LPAD)) for a in range(0, LPAD, CH)]

            def score(i, chunk, first=False):
                a, b = CHUNKS[chunk]
                if chunk == 0:
                    pe.wait_ge(cw_ready, i + 1)
                    if not first:
                        pe.wait_ge(exp_done, i)
                last = split_product(pe, banks[:, S + chunk, 0:b - a],
                                     [(cwh[:, k, :], cwl[:, k, :], qTh[:, k, a:b], qTl[:, k, a:b]) for k in range(KD)])
                if chunk == len(CHUNKS) - 1:
                    last.then_inc(s_ready, 1)

            def turn(i, g, first=False):
                if g == 0:
                    pe.wait_ge(exp_done, i + 1)
                if g >= 2:
                    pe.wait_ge(low_done, i * NGR + g - 1)
                for n, t in enumerate(GROUPS[g]):
                    last = pe.transpose(banks[0:rows(t), R + g % 2, n * P:(n + 1) * P], prob[:, t * P:t * P + rows(t)],
                                        ident[:, :])
                last.then_inc(turned, 1)

            def attend(i):
                pe.wait_ge(low_done, (i + 1) * NGR)
                pe.wait_ge(o_done, FREE + i)
                split_product(pe, banks[:, O, 0:D], [(pTh[0:rows(t), t, :], pTl[0:rows(t), t, :], qh[0:rows(t), t, :],
                                                      ql[0:rows(t), t, :]) for t in range(LB)]).then_inc(o_ready, 1)

            for chunk in range(4):
                score(0, chunk, first=True)
            with pe.Fori(1, NB) as i:
                turn(i - 1, 0)
                turn(i - 1, 1)
                score(i, 0)
                turn(i - 1, 2)
                score(i, 1)
                turn(i - 1, 3)
                score(i, 2)
                score(i, 3)
                attend(i - 1)
            for g in range(NGR):
                turn(NB - 1, g)
            attend(NB - 1)


def phase_fuse(nc, io, keep):
    x1, cn, cT, ch, cl, c2q = (keep[n] for n in ("x1", "cn", "cT", "ch", "cl", "c2q"))
    with Phase(nc, "fuse") as ph:
        ident, ones, w, wh, wl, bs, rowc = (keep[n] for n in ("ident", "ones", "wf", "wfh", "wfl", "bs", "rowc"))
        e = ph.sb("e", [P, NB, 32])
        smax = ph.sb("smax", [P, NB])
        wm, gate = ph.sb("wm", [P, KD, D]), ph.sb("gate", [P, FH * NE // 2])
        one = ph.sb("one", [P, 8])
        q2c, q2col = ph.sb("q2c", [P, D]), ph.sb("q2col", [P, KD])
        qTh, qTl = ph.sb("qTh", [P, 2, KD, CH], F32R), ph.sb("qTl", [P, 2, KD, CH], F32R)
        mul = ph.sb("mul", [P, 2, CH])
        mh, ml = ph.sb("mh", [P, 2, KD, CH], F32R), ph.sb("ml", [P, 2, KD, CH], F32R)
        banks = ph.ps("banks", [P, 8, CH])
        ln = LayerNorm(ph, "ln")
        turn_q = Turn(ph, "q", (banks[:, 0, :], banks[:, 1, :]), ident)
        turn_n = Turn(ph, "n", (banks[:, 2, :], banks[:, 3, :]), ident)
        e_zero, route_in, route_split, chain_s, mul_done, mh_done, ml_done, z_ready, z_added, sm, sm_e, sm_pe, w_fused = map(ph.sem, (
            "e_zero", "route_in", "route_split", "dve_chain", "mul_done", "mh_done", "ml_done", "z_ready", "z_added", "sm",
            "sm_e", "sm_pe", "w_fused"))
        SM = 6
        block = ph.stack.enter_context(nc.Block())

        @block.sync
        def _(sp):
            sp.dma_start(wm[:, :, :], io["wm"].rearrange("(k p) f -> p k f", p=P)).then_inc(route_in, 16)
            for dst, name in ((gate, "gate"), (keep["bcol"], "bm"), (keep["iota"], "iota")):
                sp.dma_start(dst[:, :], io[name]).then_inc(route_in, 16)

        @block.gpsimd
        def _(pool):
            pool.wait_ge(route_in, 64)
            pool.tensor_copy(keep["wmh"][:, :, :], wm[:, :, :]).then_inc(route_split, 1)
            pool.tensor_copy(keep["gh"][:, :], gate[:, :]).then_inc(route_split, 1)
            pool.wait_ge(route_split, 2)
            pool.tensor_tensor(keep["wml"][:, :, :], wm[:, :, :], keep["wmh"][:, :, :], ALU.subtract).then_inc(route_split, 1)
            pool.tensor_tensor(keep["gl"][:, :], gate[:, :], keep["gh"][:, :], ALU.subtract).then_inc(route_split, 1)
            for n in range(NC * KD):
                c, k = n // KD, n % KD
                pool.wait_ge(mh_done, n + 1)
                if c >= 2:
                    pool.wait_ge(z_ready, (c - 1) * BPC)
                pool.tensor_tensor(ml[:, c % 2, k, :], mul[:, k, :], mh[:, c % 2, k, :], ALU.subtract).then_inc(ml_done, 1)
            pool.wait_ge(route_split, 4)

        @block.vector
        def _(dve):
            chain = Chain(dve, chain_s)

            dve.memset(e[:, :, :], 0.0).then_inc(e_zero, 1)

            def softmax_over_tokens():
                chain.link(dve.tensor_tensor(smax[:, :], rowc[:, :], keep["nmax"][:, :], ALU.subtract))
                for n in range(3):
                    chain.link(dve.tensor_scalar(smax[:, :], smax[:, :], bs[:, n:n + 1], None, ALU.add))
                dve.tensor_reduce(one[:, 0:1], smax[:, :], AX.X, ALU.max).then_inc(sm, 1)
                dve.wait_ge(sm_pe, 1)
                dve.tensor_reduce(one[0:1, 1:2], banks[0:1, SM, 0:P], AX.X, ALU.max, negate=True).then_inc(sm, 1)
                dve.wait_ge(sm_pe, 2)
                dve.tensor_copy(one[:, 2:3], banks[:, SM, P:P + 1]).then_inc(sm, 1)

            def fuse_weights():
                dve.wait_ge(sm_pe, 3)
                chain.link(dve.reciprocal(one[:, 4:5], banks[:, SM, P + 2:P + 3]))
                dve.wait_ge(sm_pe, 4)
                dve.tensor_scalar(q2c[:, :], banks[:, SM + 1, 0:D], one[:, 4:5], None, ALU.mult).then_inc(sm, 1)
                dve.wait_ge(sm_pe, 5)
                chain.link(dve.tensor_copy(q2col[:, :], banks[:, SM, 256:256 + KD]))
                for k in range(KD):
                    chain.then(dve.scalar_tensor_tensor(out=w[:, k, :], in0=w[:, 3 * KD + k, :], scalar=q2col[:, k:k + 1],
                                                        in1=w[:, k, :], op0=ALU.mult, op1=ALU.add))
                chain.wait()
                chain.link(dve.tensor_copy(wh[:, 0:KD, :], w[:, 0:KD, :]))
                dve.tensor_tensor(wl[:, 0:KD, :], w[:, 0:KD, :], wh[:, 0:KD, :], ALU.subtract).then_inc(w_fused, 1)

            def low_q(c, k):
                n = c * KD + k
                dve.wait_ge(turn_q.high_done, n + 1)
                if n >= 2:
                    dve.wait_ge(ml_done, n - 1)
                dve.tensor_tensor(mul[:, k, :], turn_q.banks[n % 2], cT[:, k, tokens(c)], ALU.mult).then_inc(mul_done, 1)
                turn_q.low(dve, qTh[:, c % 2, k, :], qTl[:, c % 2, k, :], c, k)

            def low_n(c):
                for k in range(KD):
                    turn_n.low(dve, keep["nh"][:, k, tokens(c)], keep["nl"][:, k, tokens(c)], c, k)

            softmax_over_tokens()
            for k in range(KD):
                low_q(0, k)
            fuse_weights()
            for c in range(NC):
                for b in range(c * BPC, (c + 1) * BPC):
                    dve.wait_ge(z_ready, b + 1)
                    dve.tensor_tensor(x1[:, b, :], banks[:, 4 + b % 2, 0:D], x1[:, b, :], ALU.add).then_inc(z_added, 1)
                    if b % BPC < KD and c + 1 < NC:
                        low_q(c + 1, b % BPC)
                dve.wait_ge(z_added, (c + 1) * BPC)
                ln.collect(dve, x1, c)
                ln.apply(dve, x1, cn, c)
                if c >= 1:
                    low_n(c - 1)
            low_n(NC - 1)

        @block.scalar
        def _(act):
            def high_q(c):
                for k in range(KD):
                    if c >= 2:
                        act.wait_ge(z_ready, (c - 1) * BPC)
                    turn_q.high(act, qTh[:, c % 2, k, :], c, k)
                for k in range(KD):
                    act.wait_ge(mul_done, c * KD + k + 1)
                    act.activation(mh[:, c % 2, k, :], mul[:, k, :], ACT.Copy).then_inc(mh_done, 1)

            def high_n(c):
                for k in range(KD):
                    turn_n.high(act, keep["nh"][:, k, tokens(c)], c, k)

            act.wait_ge(sm, 3)
            act.wait_ge(e_zero, 1)
            act.activation(e[:, :, 0], smax[:, :], ACT.Exp, bias=one[:, 2:3], accum_out=one[:, 3:4]).then_inc(sm_e, 1)
            high_q(0)
            for c in range(NC):
                if c + 1 < NC:
                    high_q(c + 1)
                ln.root(act, c)
                if c >= 1:
                    high_n(c - 1)
            high_n(NC - 1)

        @block.tensor
        def _(pe):
            def softmax_over_tokens():
                pe.wait_ge(sm, 1)
                pe.transpose(banks[0:1, SM, 0:P], one[:, 0:1], ident[:, :]).then_inc(sm_pe, 1)
                pe.wait_ge(sm, 2)
                pe.matmul(banks[:, SM, P:P + 1], ones[0:1, :], one[0:1, 1:2], start=True, stop=True).then_inc(sm_pe, 1)
                pe.wait_ge(sm_e, 1)
                pe.matmul(banks[:, SM, P + 2:P + 3], ones[:, :], one[:, 3:4], start=True, stop=True).then_inc(sm_pe, 1)
                for b in range(NB):
                    j = b % 4
                    last = pe.matmul(banks[32 * j:32 * j + 32, SM + 1, 0:D], e[:, b, :], cn[:, b, :], start=b < 4, stop=b >= NB - 4)
                last.then_inc(sm_pe, 1)
                pe.wait_ge(sm, 4)
                for k in range(KD):
                    last = pe.matmul(banks[:, SM, 256 + k:257 + k], q2c[:, k * P:(k + 1) * P], ones[:, 0:1],
                                     start=True, stop=True)
                last.then_inc(sm_pe, 1)

            def turn_attended(c):
                for k in range(KD):
                    turn_q.turn(pe, c2q, c, k)

            def turn_norm(c):
                for k in range(KD):
                    turn_n.turn(pe, cn, c, k, ready=ln.done)

            def fuse(c):
                pe.wait_ge(ml_done, (c + 1) * KD)
                pe.wait_ge(turn_q.low_done, (c + 1) * KD)
                if c == 0:
                    pe.wait_ge(w_fused, 1)
                for b in range(c * BPC, (c + 1) * BPC):
                    if b >= 2:
                        pe.wait_ge(z_added, b - 1)
                    tok, own = slice(b * P, (b + 1) * P), slice((b % BPC) * P, (b % BPC + 1) * P)
                    terms = [(qTh[:, c % 2, k, own], qTl[:, c % 2, k, own], wh[:, KD + k, :], wl[:, KD + k, :])
                              for k in range(KD)]
                    terms += [(mh[:, c % 2, k, own], ml[:, c % 2, k, own], wh[:, 2 * KD + k, :], wl[:, 2 * KD + k, :])
                              for k in range(KD)]
                    terms += [(ch[:, k, tok], cl[:, k, tok], wh[:, k, :], wl[:, k, :]) for k in range(KD)]
                    split_product(pe, banks[:, 4 + b % 2, 0:D], terms).then_inc(z_ready, 1)

            turn_attended(0)
            softmax_over_tokens()
            for c in range(NC):
                if c + 1 < NC:
                    turn_attended(c + 1)
                fuse(c)
                if c >= 1:
                    turn_norm(c - 1)
            turn_norm(NC - 1)


def phase_route(nc, io, keep):
    nh, nl, stack, wT = (keep[n] for n in ("nh", "nl", "stack", "wT"))
    with Phase(nc, "route") as ph:
        identb, bias = ph.sb("identb", [P, P], BF16), ph.sb("bias", [P, D])
        wh, wl, gh, gl, bcol, iota = (keep[n] for n in ("wmh", "wml", "gh", "gl", "bcol", "iota"))
        HE = FH * NE
        th, tl = ph.sb("th", [P, 2, KD, CH], F32R), ph.sb("tl", [P, 2, KD, CH], F32R)
        G = BPC * FH
        rows = keep["attn"][:, :, :].rearrange("p b d -> p (b d)").rearrange("p (n g e) -> p n g e", g=G, e=NE)
        row = {n: rows[:, i, :, :] for i, n in enumerate(("shifted", "expd", "eq", "cand", "first", "rest", "second", "chosen"))}
        col = {n: ph.sb(n, [P, G]) for n in ("max", "sum", "rsum", "top", "pick")}
        free = keep["v"][:, :, :].rearrange("p b d -> p (b d)")
        w1f = free[0:96, 0:NE * EI]
        wof = free[:, NE * EI:NE * EI + KD * D].rearrange("p (k d) -> p k d", k=KD)
        for i, n in enumerate(("wgt", "rem")):
            first = NE * EI + KD * D + i * (G * NE)
            row[n] = free[:, first:first + G * NE].rearrange("p (g e) -> p g e", e=NE)
        parts = ph.sb("parts", [P, BPC, FH // 2, 3, 2 * NE], BF16)
        banks = ph.ps("banks", [P, 8, CH])
        X, GB, TB = 0, 2, 4
        x_added, chain0, chain1, h_ready, th_done, tl_done, stacked0, stacked1, g_ready, shifted, expd, weighed, \
            rem_done, p1_done, p2_done, p3_done, turned, copied, identb_in, ffn_in, ffn_split = map(ph.sem, (
                "x_added", "chain0", "chain1", "h_ready", "th_done", "tl_done", "stacked0", "stacked1",
                "g_ready", "shifted", "expd", "weighed", "rem_done", "p1_done", "p2_done", "p3_done", "turned", "copied",
                "identb_in", "ffn_in", "ffn_split"))
        stacked = (stacked0, stacked1)
        HB = BPC // 2

        def half(a, x):
            return a[:, x * (G // 2):(x + 1) * (G // 2)]

        def wide(name, x):
            return half(row[name], x).rearrange("p (b q h) e -> p b q (h e)", b=HB, q=FH // 2)

        def part(x, n):
            return parts[:, x * HB:(x + 1) * HB, :, n, :]

        block = ph.stack.enter_context(nc.Block())

        @block.sync
        def _(sp):
            for dst, name in ((w1f, "w1"), (keep["b1"][:, :], "b1"), (keep["b2"][:, :], "b2"), (keep["sum_w"][:, :], "sum_w"),
                              (keep["w2"][:, :, :], "w2")):
                sp.dma_start(dst, io[name]).then_inc(ffn_in, 16)
            sp.dma_start(bias[:, :], io["bo"].partition_broadcast(P)).then_inc(ffn_in, 16)
            sp.dma_start(wof, io["wo"].rearrange("(k p) f -> p k f", p=P)).then_inc(ffn_in, 16)
            for c in range(NC):
                sp.wait_ge(th_done, (c + 1) * KD)
                sp.wait_ge(tl_done, (c + 1) * KD)
                for rows, src in enumerate((th, tl, th)):
                    for h in range(4):
                        sp.dma_start(stack[rows * FD:(rows + 1) * FD, c * KD:(c + 1) * KD, h, :].bitcast(F32),
                                     src[h * FD:(h + 1) * FD, c % 2, :, :].bitcast(F32)).then_inc(stacked[c % 2], 16)
            for s in stacked:
                sp.wait_ge(s, 12 * 16 * NC // 2)
            sp.wait_ge(ffn_in, 112)

        @block.gpsimd
        def _(pool):
            pool.dma_start(identb[:, :], io["ident"]).then_inc(identb_in, 16)
            pool.dma_start(keep["spread_w"][:, :, :], io["spread_w"]).then_inc(identb_in, 16)

            def remainders(c):
                for x in range(2):
                    pool.wait_ge(p1_done, 2 * c + x + 1)
                    if c >= 1:
                        pool.wait_ge(p2_done, 2 * c + x - 1)
                        pool.wait_ge(p3_done, 2 * c + x - 1)
                    pool.tensor_tensor(wide("rem", x), wide("wgt", x), part(x, 0), ALU.subtract).then_inc(rem_done, 1)
                for x in range(2):
                    pool.wait_ge(p2_done, 2 * c + x + 1)
                    pool.tensor_tensor(part(x, 2), wide("rem", x), part(x, 1), ALU.subtract).then_inc(p3_done, 1)

            def split_ffn_weights():
                w1, flat = keep["w1"], "p e i -> p (e i)"
                pool.wait_ge(ffn_split, 2)
                pool.wait_ge(p3_done, 2)
                pool.tensor_tensor(w1[64:96, :, :].rearrange(flat), w1f[64:96, :], w1[64:96, :, :].rearrange(flat),
                                   ALU.subtract).then_inc(ffn_split, 1)
                pool.wait_ge(ffn_split, 3)
                pool.tensor_tensor(keep["wol"][:, :, :], wof, keep["woh"][:, :, :], ALU.subtract).then_inc(ffn_split, 1)

            for c in range(NC):
                remainders(c)
                if c == 0:
                    split_ffn_weights()
                for b in list(range(NB))[max(c - 1, 0) * NB // 2:c * NB // 2] if c < NC - 1 else ():
                    pool.tensor_tensor(keep["x1"][:, b, :], keep["x1"][:, b, :], bias[:, :], ALU.add).then_inc(x_added, 1)
            pool.wait_ge(identb_in, 32)
            pool.wait_ge(ffn_split, 4)
            pool.wait_ge(x_added, NB)

        @block.vector
        def _(dve):
            chains = (Chain(dve, chain0), Chain(dve, chain1))
            indices = iota[:, :].unsqueeze(1).broadcast_to([P, G // 2, NE])
            spread = lambda name, x: half(col[name], x).unsqueeze(2).broadcast_to([P, G // 2, NE])

            def link(do):
                for x, chain in enumerate(chains):
                    if chain.n:
                        chain.wait()
                    chain.then(do(x))

            def largest(out, of):
                link(lambda x: dve.tensor_reduce(half(col[out], x), half(row[of], x), AX.X, ALU.max))

            def pick_first(out):
                largest("pick", "cand")
                link(lambda x: dve.tensor_tensor(half(row[out], x), half(row["cand"], x), spread("pick", x), ALU.is_equal))

            def pair(n):
                dve.wait_ge(th_done, n + 1)
                c, k = n // KD, n % KD
                dve.scalar_tensor_tensor(out=tl[:, c % 2, k, :], in0=banks[:, X + n % 2, :], scalar=bcol[:, k:k + 1],
                                         in1=th[:, c % 2, k, :], op0=ALU.add, op1=ALU.subtract).then_inc(tl_done, 1)

            for k in range(KD):
                pair(k)
            for c in range(NC):
                gates = banks[:, GB + c % 2, :].rearrange("p (g e) -> p g e", e=NE)
                dve.wait_ge(g_ready, c + 1)
                link(lambda x: dve.tensor_reduce(half(col["max"], x), half(gates, x), AX.X, ALU.max))
                for x in range(2):
                    chains[x].wait()
                    dve.tensor_tensor(half(row["shifted"], x), half(gates, x), spread("max", x), ALU.subtract).then_inc(shifted, 1)
                dve.wait_ge(shifted, 2 * c + 2)
                link(lambda x: dve.scalar_tensor_tensor(out=half(row["cand"], x), in0=half(row["shifted"], x), scalar=0.0,
                                                        in1=indices, op0=ALU.is_equal, op1=ALU.mult))
                pick_first("first")
                link(lambda x: dve.scalar_tensor_tensor(out=half(row["rest"], x), in0=half(row["first"], x), scalar=NEGBIG,
                                                        in1=half(row["shifted"], x), op0=ALU.mult, op1=ALU.add))
                largest("top", "rest")
                if c + 1 < NC:
                    for k in range(KD):
                        pair((c + 1) * KD + k)
                link(lambda x: dve.tensor_tensor(half(row["eq"], x), half(row["rest"], x), spread("top", x), ALU.is_equal))
                link(lambda x: dve.tensor_tensor(half(row["cand"], x), half(row["eq"], x), indices, ALU.mult))
                pick_first("second")
                dve.wait_ge(expd, 2 * c + 2)
                link(lambda x: dve.tensor_reduce(half(col["sum"], x), half(row["expd"], x), AX.X, ALU.add))
                link(lambda x: dve.tensor_tensor(half(row["chosen"], x), half(row["first"], x), half(row["second"], x), ALU.add))
                link(lambda x: dve.reciprocal(half(col["rsum"], x), half(col["sum"], x)))
                link(lambda x: dve.tensor_tensor(half(row["chosen"], x), half(row["chosen"], x), half(row["expd"], x), ALU.mult))
                for x in range(2):
                    chains[x].wait()
                    if c >= 1:
                        dve.wait_ge(rem_done, 2 * c + x - 1)
                    dve.tensor_tensor(half(row["wgt"], x), half(row["chosen"], x), spread("rsum", x), ALU.mult).then_inc(weighed, 1)

        @block.scalar
        def _(act):
            def high(n):
                act.wait_ge(h_ready, n + 1)
                c, k = n // KD, n % KD
                if c >= 2:
                    act.wait_ge(stacked[c % 2], 12 * 16 * (c // 2))
                    act.wait_ge(g_ready, c - 1)
                act.activation(th[:, c % 2, k, :], banks[:, X + n % 2, :], ACT.Identity,
                               bias=bcol[:, k:k + 1]).then_inc(th_done, 1)

            for k in range(KD):
                high(k)
            for c in range(NC):
                for x in range(2):
                    act.wait_ge(shifted, 2 * c + x + 1)
                    act.activation(half(row["expd"], x), half(row["shifted"], x), ACT.Exp).then_inc(expd, 1)
                if c + 1 < NC:
                    for k in range(KD):
                        high((c + 1) * KD + k)
                if c == 0:
                    act.wait_ge(ffn_in, 112)
                    act.activation(keep["w1"][:, :, :].rearrange("p e i -> p (e i)"), w1f, ACT.Copy).then_inc(ffn_split, 1)
                    act.activation(keep["woh"][:, :, :], wof, ACT.Copy).then_inc(ffn_split, 1)
                for x in range(2):
                    act.wait_ge(weighed, 2 * c + x + 1)
                    if c >= 1:
                        act.wait_ge(turned, c)
                    act.activation(part(x, 0), wide("wgt", x), ACT.Copy).then_inc(p1_done, 1)
                for x in range(2):
                    act.wait_ge(rem_done, 2 * c + x + 1)
                    act.activation(part(x, 1), wide("rem", x), ACT.Copy).then_inc(p2_done, 1)
                act.wait_ge(turned, c + 1)
                for q in range(FH // 2):
                    src = banks[0:96, TB + q // 2, :].bitcast(BF16)[:, (q % 2) * CH:(q % 2 + 1) * CH]
                    act.activation(wT[:, c * 2 + q // 2, q % 2, :], src, ACT.Copy).then_inc(copied, 1)

        @block.tensor
        def _(pe):
            def product(c):
                for k in range(KD):
                    n = c * KD + k
                    if n >= 2:
                        pe.wait_ge(tl_done, n - 1)
                    feat = slice(k * P, (k + 1) * P)
                    split_product(pe, banks[:, X + n % 2, :], [(wh[:, j, feat], wl[:, j, feat], nh[:, j, tokens(c)],
                                                                nl[:, j, tokens(c)]) for j in range(KD)]).then_inc(h_ready, 1)

            def gate(c):
                pe.wait_ge(tl_done, (c + 1) * KD)
                for b in range(BPC):
                    for k in range(KD):
                        tok, at_ = slice(b * P, (b + 1) * P), b * P + k * (HE // 2)
                        last = split_product(pe, banks[:, GB + c % 2, at_:at_ + HE // 2],
                                             [(th[:, c % 2, k, tok], tl[:, c % 2, k, tok], gh[:, :], gl[:, :])])
                last.then_inc(g_ready, 1)

            def turn(c):
                pe.wait_ge(p3_done, 2 * c + 2)
                if c >= 1:
                    pe.wait_ge(copied, c * (FH // 2))
                else:
                    pe.wait_ge(identb_in, 32)
                for q in range(FH // 2):
                    dst = banks[0:96, TB + q // 2, :].bitcast(BF16)
                    for b in range(BPC):
                        last = pe.transpose(dst[:, (q % 2) * CH + b * P:(q % 2) * CH + (b + 1) * P],
                                            parts[:, b, q, :, :].rearrange("p a e -> p (a e)"), identb[:, :])
                last.then_inc(turned, 1)

            product(0)
            gate(0)
            product(1)
            for c in range(NC):
                if c + 1 < NC:
                    gate(c + 1)
                if c + 2 < NC:
                    product(c + 2)
                turn(c)


def phase_experts(nc, io, keep):
    nh, nl, stack, wT, x2 = (keep[n] for n in ("nh", "nl", "stack", "wT", "x1"))
    acc = keep["v"][:, 0:8, :].rearrange("p (q h c) d -> p q h (c d)", q=2, h=2)
    prod = keep["v"][:, 8:16, :].rearrange("p (q h c) d -> p q h (c d)", q=2, h=2)
    hid0 = keep["attn"][:, :, :].rearrange("p (e h c) d -> p e h (c d)", e=EG, h=2)
    high, low = (a[:, :, :].rearrange("p k t -> p (k t)") for a in (nh, nl))
    R = KD * NC
    NST = 2 * NEG
    NX = NST * EG
    with Phase(nc, "ffn") as ph:
        w1, w2, b1, b2, spread_w, sum_w, woh, wol = (keep[n] for n in (
            "w1", "w2", "b1", "b2", "spread_w", "sum_w", "woh", "wol"))
        hid1 = ph.sb("hid1", [P, EG, 2, CH])
        hid = (hid0, hid1)
        wide = ph.sb("wide", [P, 2, CH])
        banks = ph.ps("banks", [P, 8, CH])
        combined = ph.sb("combined", [P, CH])
        A, B, W = 0, 6, 7
        a_ready, gelu_done, b_ready, wide_ready, wide_copied, prod_ready, \
            added, sum_ready, comb_out, comb_high, comb_low, out_ready, out_added, stored = map(ph.sem, (
                "a_ready", "gelu_done", "b_ready", "wide_ready",
                "wide_copied", "prod_ready", "added", "sum_ready", "comb_out", "comb_high", "comb_low", "out_ready",
                "out_added", "stored"))
        block = ph.stack.enter_context(nc.Block())

        NHALF = 2 * NST
        COMBINE = (13, 5)

        def back(r, j, by):
            return (r, j - by) if j >= by else (r - 1, j - by + NHALF)

        def pair_of(x):
            return x % 3

        def earlier_tiles(x):
            last = x - 3 if x >= 3 else max(y for y in range(NX) if pair_of(y) == x) - NX
            return last + 1

        def wait_from(eng, sem, value, r):
            if not isinstance(r, int) or value > 0:
                eng.wait_ge(sem, value)

        @block.sync
        def _(sp):
            for c in range(NC):
                sp.wait_ge(out_added, (c + 1) * BPC)
                sp.dma_start(io["out"][c * CH:(c + 1) * CH, :].rearrange("(b p) d -> p b d", p=P),
                             x2[:, c * BPC:(c + 1) * BPC, :]).then_inc(stored, 16)
            sp.wait_ge(stored, 16 * NC)

        @block.gpsimd
        def _(pool):
            def add(r, n):
                q = n // NEG
                pool.wait_ge(prod_ready, r * NHALF + 2 * n + 2)
                if n % NEG >= 2:
                    pool.wait_ge(added, r * 6 + 3 * q + n % NEG - 1)
                pool.tensor_tensor(acc[:, q, :, :], acc[:, q, :, :], prod[:, n % 2, :, :], ALU.add).then_inc(added, 1)

            with pool.Fori(0, R) as r:
                for n in range(NST):
                    if n % NEG:
                        add(r, n)

        @block.tensor
        def _(pe):
            def first(r, n, e):
                x = n * EG + e
                wait_from(pe, gelu_done, r * NX + earlier_tiles(x), r)
                g = n % NEG
                for h in range(2):
                    last = pe.matmul(banks[:, A + 2 * pair_of(x) + h, :], w1[:, g * EG + e, :],
                                     stack[0:96, at(r), 2 * (n // NEG) + h, :].rearrange("p a t -> p (a t)"), start=True, stop=True)
                last.then_inc(a_ready, 1)

            def widen(r, i, combined_before=None):
                n, h = i // 2, i % 2
                wait_from(pe, wide_copied, r * NHALF + i, r)
                if combined_before is not None:
                    pe.wait_ge(comb_out, combined_before)
                pe.matmul(banks[:, W, :], spread_w[:, h * NEG + n % NEG, :],
                          wT[:, at(r), n // NEG, :].rearrange("p a t -> p (a t)"), start=True, stop=True).then_inc(wide_ready, 1)

            def second(r, i):
                n, h = i // 2, i % 2
                if h == 0:
                    pe.wait_ge(gelu_done, r * NX + (n + 1) * EG)
                wait_from(pe, prod_ready, r * NHALF + i, r)
                for e in range(EG):
                    last = pe.matmul(banks[32 * e:32 * e + 32, B, :], w2[:, (n % NEG) * EG + e, :],
                                     hid[n % 2][:, e, h, :], start=True, stop=True)
                last.then_inc(b_ready, 1)

            def combine(r, q, copied):
                pe.wait_ge(added, r * 6 + 3 * q + 3)
                pe.wait_ge(wide_copied, copied)
                for h in range(2):
                    hh = 2 * q + h
                    last = pe.matmul(banks[32 * hh:32 * hh + 32, W, :], sum_w[:, :], acc[:, q, h, :], start=True, stop=True)
                last.then_inc(sum_ready, 1)

            def round_(loop, lone=False):
                for j in range(NHALF):
                    r = fresh(pe, loop, R - 1, 1)
                    for e in range(2):
                        first(r, j // 2, 2 * (j % 2) + e)
                    combined_before = None
                    if j == COMBINE[0]:
                        combine(r, 0, r * NHALF + j - 1)
                        combined_before = 2 * r + 1
                    if j == COMBINE[1] and not lone:
                        combine(r - 1, 1, r * NHALF + j - 1)
                        combined_before = 2 * r
                    if j >= 2 or not lone:
                        second(*back(r, j, 2))
                    if j >= 1 or not lone:
                        widen(*back(r, j, 1), combined_before)

            round_(0, lone=True)
            with pe.Fori(1, R) as r:
                round_(r)
            second(R - 1, NHALF - 2)
            widen(R - 1, NHALF - 1)
            second(R - 1, NHALF - 1)
            combine(R - 1, 1, R * NHALF)
            pe.wait_ge(comb_low, 2 * R)
            for b in range(NB):
                if b >= 4:
                    pe.wait_ge(out_added, b - 3)
                terms = []
                for k in range(KD):
                    own = at(((b // BPC) * KD + k) * CH + (b % BPC) * P, P)
                    terms.append((high[:, own], low[:, own], woh[:, k, :], wol[:, k, :]))
                split_product(pe, banks[:, A + b % 4, 0:D], terms).then_inc(out_ready, 1)

        @block.scalar
        def _(act):
            def gelu(r, n, e):
                x = n * EG + e
                act.wait_ge(a_ready, r * NX + x + 1)
                if e == 0:
                    wait_from(act, b_ready, r * NHALF + 2 * n - 2, r)
                pair = A + 2 * pair_of(x)
                ex = (n % NEG) * EG + e
                act.activation(hid[n % 2][:, e, :, :], banks[:, pair:pair + 2, :], ACT.Gelu,
                               bias=b1[:, ex:ex + 1]).then_inc(gelu_done, 1)

            for n in range(NST):
                for e in range(EG):
                    gelu(0, n, e)
            with act.Fori(1, R) as r:
                for n in range(NST):
                    for e in range(EG):
                        gelu(r, n, e)

        @block.vector
        def _(dve):
            def copy_wide(r, i):
                dve.wait_ge(wide_ready, r * NHALF + i + 1)
                wait_from(dve, prod_ready, r * NHALF + i - 1, r)
                dve.tensor_copy(wide[:, i % 2, :], banks[:, W, :]).then_inc(wide_copied, 1)

            def weigh(r, i):
                n, h = i // 2, i % 2
                q, g = n // NEG, n % NEG
                dve.wait_ge(wide_copied, r * NHALF + i + 1)
                if h == 0:
                    if g == 0:
                        wait_from(dve, sum_ready, 2 * r + q - 1, r)
                    elif g < 3:
                        wait_from(dve, added, r * 6 + 3 * q, r)
                    else:
                        dve.wait_ge(added, r * 6 + 3 * q + 1)
                dst = acc[:, q] if g == 0 else prod[:, n % 2]
                dve.wait_ge(b_ready, r * NHALF + i + 1)
                dve.scalar_tensor_tensor(out=dst[:, h, :], in0=banks[:, B, :], scalar=b2[:, g:g + 1],
                                         in1=wide[:, h, :], op0=ALU.add, op1=ALU.mult).then_inc(prod_ready, 1)

            def copy_combined(r, q):
                dve.wait_ge(sum_ready, 2 * r + q + 1)
                wait_from(dve, comb_low, 2 * r + q, r)
                rows = slice(64 * q, 64 * q + 64)
                dve.tensor_copy(combined[rows, :], banks[rows, W, :]).then_inc(comb_out, 1)

            def split_combined(r, q):
                rows, own = slice(64 * q, 64 * q + 64), at(r * CH, CH)
                dve.wait_ge(comb_out, 2 * r + q + 1)
                dve.tensor_copy(high[rows, own], combined[rows, :]).then_inc(comb_high, 1)
                dve.wait_ge(comb_high, 2 * r + q + 1)
                dve.tensor_tensor(low[rows, own], combined[rows, :], high[rows, own], ALU.subtract).then_inc(comb_low, 1)

            def round_(loop, lone=False):
                for j in range(NHALF):
                    r = fresh(dve, loop, R - 1, 1)
                    now = None
                    if j == COMBINE[0]:
                        now = (r, 0)
                    if j == COMBINE[1] and not lone:
                        now = (r - 1, 1)
                    if now:
                        copy_combined(*now)
                    if j >= 2 or not lone:
                        weigh(*back(r, j, 2))
                    if j >= 1 or not lone:
                        copy_wide(*back(r, j, 1))
                    if now:
                        split_combined(*now)

            round_(0, lone=True)
            with dve.Fori(1, R) as r:
                round_(r)
            weigh(R - 1, NHALF - 2)
            copy_wide(R - 1, NHALF - 1)
            weigh(R - 1, NHALF - 1)
            copy_combined(R - 1, 1)
            split_combined(R - 1, 1)
            for b in range(NB):
                dve.wait_ge(out_ready, b + 1)
                dve.tensor_tensor(x2[:, b, :], banks[:, A + b % 4, 0:D], x2[:, b, :], ALU.add).then_inc(out_added, 1)


def split_product(pe, out, terms, start=True, stop=True):
    n = 0
    for ah, al, bh, bl in terms:
        for a, b in ((ah, bh), (ah, bl), (al, bh)):
            last = pe.matmul(out, a, b, start=start and n == 0, stop=stop and n == 3 * len(terms) - 1)
            n += 1
    return last


def program(nc, io, stop_after=99):
    keep = {}
    with ExitStack() as stack:
        def sb(name, shape, dt=F32):
            keep[name] = stack.enter_context(nc.sbuf_tensor("keep_" + name, shape, dt))

        sb("ident", [P, P])
        sb("wouth", [P, KD, D], F32R)
        sb("woutl", [P, KD, D], F32R)
        for name in ("v", "attn"):
            sb(name, [P, NB, D])
        phase_qkv(nc, io, keep)
        phase_attention(nc, io, keep)
        keep["cn"], keep["c2q"] = keep["v"], keep["attn"]
        sb("x1", [P, NB, D])
        sb("ch", [P, KD, T], F32R)
        sb("cl", [P, KD, T], F32R)
        keep["nh"], keep["nl"] = keep["ch"], keep["cl"]
        for name, shape, dt in (("wmh", [P, KD, D], F32R), ("wml", [P, KD, D], F32R), ("gh", [P, FH * NE // 2], F32R),
                                ("gl", [P, FH * NE // 2], F32R), ("bcol", [P, KD], F32), ("iota", [P, NE], F32)):
            sb(name, shape, dt)
        with ExitStack() as inner:
            keep["cT"] = inner.enter_context(nc.sbuf_tensor("keep_cT", [P, KD, T], F32))
            for name, shape, dt in (("nmax", [P, NB], F32), ("wcol", [P, 2, KD], F32), ("rowc", [P, NB], F32), ("wf", [P, LB, D], F32),
                                    ("wfh", [P, 3 * KD, D], F32R), ("wfl", [P, 3 * KD, D], F32R), ("bias_f", [P, D], F32),
                                    ("bs", [P, 3], F32), ("ones", [P, P], F32)):
                keep[name] = inner.enter_context(nc.sbuf_tensor("keep_" + name, shape, dt))
            with ExitStack() as context:
                for name, shape in (("qTh", [P, KD, LPAD]), ("qTl", [P, KD, LPAD]), ("qh", [P, LB, D]), ("ql", [P, LB, D])):
                    keep[name] = context.enter_context(nc.sbuf_tensor("keep_" + name, shape, F32R))
                phase_projection(nc, io, keep)
                phase_cross(nc, io, keep)
            phase_fuse(nc, io, keep)
        sb("stack", [96, KD * NC, 4, CH], F32R)
        sb("wT", [96, KD * NC, 2, CH], BF16)
        for name, shape, dt in (("w1", [96, NE, EI], F32R), ("w2", [P, NE, FD], F32), ("b1", [P, NE], F32), ("b2", [P, NEG], F32),
                                ("spread_w", [96, 2 * NEG, P], BF16), ("sum_w", [P, FD], F32), ("woh", [P, KD, D], F32R),
                                ("wol", [P, KD, D], F32R)):
            sb(name, shape, dt)
        phase_route(nc, io, keep)
        phase_experts(nc, io, keep)


def host_inputs(inputs):
    import numpy as np
    g = {k: np.asarray(v) for k, v in inputs.items()}
    c = np.ascontiguousarray
    a = {"x": g["x"][0], "ctx": g["ctx_1024"][0], "ctxT": g["ctx_1024"][0].T,
         "ident": np.eye(P, dtype=np.float32)}
    w = g["L0_attn_w_qkv"]
    qk = w[0:2 * D].reshape(2, NG, HG, HD, D).transpose(0, 1, 3, 2, 4).reshape(2 * D, D)
    a["wqkvT"] = np.concatenate([qk, w[2 * D:]]).T
    a["ones"] = np.ones((P, P), np.float32)
    a["ctx"] = np.pad(a["ctx"], ((0, LB * P - L), (0, 0)))
    a["ctxT"] = np.pad(a["ctxT"], ((0, 0), (0, LPAD - L)))
    a["woutT"], a["b_out"] = g["L0_attn_w_out"].T, g["L0_attn_b_out"]
    a["wlT"], a["b_l"] = g["L0_xattn_W_l"].T, g["L0_xattn_b_l"]
    a["w_c"] = g["L0_xattn_w_c"]
    for n in ("w_cq", "w_q"):
        a[n] = g["L0_xattn_" + n].reshape(KD, P).T
    for n in ("b_cq", "b_c", "b_q"):
        a[n] = g["L0_xattn_" + n].reshape(1)
    f = lambda n: g["L0_ffn_" + n]
    eye = np.eye(4, dtype=np.float32)
    a["wm"], a["bm"], a["wo"], a["bo"] = f("Wm"), f("bm").reshape(KD, P).T, f("Wo"), f("bo")
    gate = np.zeros((4, FD, 4, NE), np.float32)
    for h in range(4):
        gate[h, :, h, :] = f("expert_emb")
    a["gate"] = gate.reshape(P, 4 * NE)
    a["iota"] = np.tile(np.arange(NE, 0, -1, dtype=np.float32), (P, 1))
    a["w1"] = np.tile(f("W1").transpose(1, 0, 2).reshape(FD, NE * EI), (3, 1))
    a["b1"], a["w2"] = f("b1").T, f("W2").transpose(1, 0, 2)
    a["b2"] = f("b2").reshape(NEG, EG * FD).T
    a["sum_w"] = np.tile(np.eye(FD, dtype=np.float32), (EG, 1))
    spread = np.zeros((3, 2, NE, 2, NEG, EG, FD), np.float32)
    for h in range(2):
        for e in range(NE):
            spread[:, h, e, h, e // EG, e % EG, :] = 1.0
    a["spread_w"] = spread.reshape(96, 2 * NEG, P)
    future = np.triu(np.full((P, P), NEGBIG, np.float32), 1)
    a["mask_qk"], a["mask_kq"] = future, future.T
    return {k: c(v) for k, v in a.items()}


SCRATCH = {"qk_parts": ((2, NG, NC, 3, HD * HG, CH), BF16)}


def declare(nc, arrays):
    from concourse import mybir as _mybir
    io = {}
    for name, a in arrays.items():
        io[name] = nc.dram_tensor(f"in_{name}", a.shape, _mybir.dt.from_np(a.dtype), kind="ExternalInput").ap()
    for name, (shape, dt) in SCRATCH.items():
        io[name] = nc.dram_tensor(f"scratch_{name}", shape, dt, kind="Internal").ap()
    io["out"] = nc.dram_tensor("out", (T, D), F32, kind="ExternalOutput").ap()
    return io


def kernel(**inputs):
    import concourse.bacc as _bacc
    from concourse.bass_utils import run_bass_kernel_spmd as _run

    nc = _bacc.Bacc("TRN2", target_bir_lowering=False, num_devices=1)
    arrays = host_inputs(inputs)
    io = declare(nc, arrays)
    program(nc, io)
    r = _run(nc, [{f"in_{k}": v for k, v in arrays.items()}], core_ids=[0])
    return r.results[0]["out"].reshape(1, T, D)
```
